# Optimizing a Trainium2 kernel written in Bass

```python
import numpy as np
import jax
import jax.numpy as jnp

def _softmax(x, axis=-1):
    return jax.nn.softmax(x, axis=axis)

def _gelu(x):
    return jax.nn.gelu(x, approximate=True)

def _silu(x):
    return jax.nn.silu(x)

def _sigmoid(x):
    return jax.nn.sigmoid(x)

def _layernorm(x, axis=-1, eps=1e-05):
    m = jnp.mean(x, axis=axis, keepdims=True)
    v = jnp.var(x, axis=axis, keepdims=True)
    return (x - m) / jnp.sqrt(v + eps)

def _scatter_add(tgt, idx, src, axis=0):
    return tgt.at[idx].add(src)

def _segment_sum(src, seg, n):
    return jax.ops.segment_sum(src, seg, n)
kernel_name = 'mk_adj_ffn_d1_adj_r2_1627c0'

def setup_inputs(seed: int=0):
    np.random.seed(seed)
    _w = jnp.asarray

    def _rec_inputs():
        import jax
        import jax.numpy as jnp
        _gk = jax.random.key(seed)
        x = -0.0002928 + 1 * jax.random.normal(jax.random.fold_in(_gk, 1), (2048, 512), jnp.float32)
        _a = jax.random.bernoulli(jax.random.fold_in(_gk, 2), 0.000976562, (2048, 2048))
        _af = _a.astype(jnp.float32)
        adj = _af
        return (x, adj)
    x, adj = _rec_inputs()

    def _L0_gnn_setup():
        import jax, jax.numpy as jnp
        import numpy as np
        N = 2048
        D_IN = 512
        H = 16
        DH = D_IN // H
        ALPHA = 0.2
        MASK_VAL = -65500.0
        key = jax.random.key(seed)
        ks = jax.random.split(key, 7)
        x = jax.random.normal(ks[0], (N, D_IN), dtype=jnp.float32)
        adj = jax.random.randint(ks[1], (N, N), 0, 2).astype(jnp.float32)
        s = 1.0 / np.sqrt(D_IN)
        W_seq = jax.random.normal(ks[2], (D_IN, D_IN), dtype=jnp.float32) * s
        a1 = jax.random.normal(ks[3], (DH,), dtype=jnp.float32) / np.sqrt(DH)
        a2 = jax.random.normal(ks[4], (DH,), dtype=jnp.float32) / np.sqrt(DH)
        W_out = jax.random.normal(ks[5], (D_IN, D_IN), dtype=jnp.float32) * s
        b_out = jax.random.normal(ks[6], (D_IN,), dtype=jnp.float32) * 0.01
        return {'x': x, 'adj': adj, 'W_seq': W_seq, 'a1': a1, 'a2': a2, 'W_out': W_out, 'b_out': b_out}
    _L0_gnn_all = _L0_gnn_setup()
    _L0_gnn_in = {k: v for k, v in _L0_gnn_all.items() if k in ('W_seq', 'a1', 'a2', 'W_out', 'b_out')}
    del _L0_gnn_all

    def _L0_ffn_setup():
        import jax, jax.numpy as jnp
        import numpy as np
        HIDDEN = 512
        MOE_FF = 256
        SHARED_FF = 1408
        NUM_EXPERTS = 16
        TOP_K = 2
        NORM_TOPK = True
        key = jax.random.key(seed)
        ks = jax.random.split(key, 8)
        s = 0.02
        return {'layer_input': jax.random.normal(ks[0], (1, 1024, HIDDEN), dtype=jnp.float32), 'gate_w': jax.random.normal(ks[1], (NUM_EXPERTS, HIDDEN), dtype=jnp.float32) * s, 'w_gate_up': jax.random.normal(ks[2], (NUM_EXPERTS, HIDDEN, 2 * MOE_FF), dtype=jnp.float32) * s, 'w_down': jax.random.normal(ks[3], (NUM_EXPERTS, MOE_FF, HIDDEN), dtype=jnp.float32) * s, 'shared_w_gate': jax.random.normal(ks[4], (SHARED_FF, HIDDEN), dtype=jnp.float32) * s, 'shared_w_up': jax.random.normal(ks[5], (SHARED_FF, HIDDEN), dtype=jnp.float32) * s, 'shared_w_down': jax.random.normal(ks[6], (HIDDEN, SHARED_FF), dtype=jnp.float32) * s, 'shared_gate_w': jax.random.normal(ks[7], (1, HIDDEN), dtype=jnp.float32) * s}
    _L0_ffn_all = _L0_ffn_setup()
    _L0_ffn_in = {k: v for k, v in _L0_ffn_all.items() if k in ('gate_w', 'w_gate_up', 'w_down', 'shared_w_gate', 'shared_w_up', 'shared_w_down', 'shared_gate_w')}
    del _L0_ffn_all
    return {'x': x, 'adj': adj, 'L0_gnn_W_seq': _L0_gnn_in['W_seq'], 'L0_gnn_a1': _L0_gnn_in['a1'], 'L0_gnn_a2': _L0_gnn_in['a2'], 'L0_gnn_W_out': _L0_gnn_in['W_out'], 'L0_gnn_b_out': _L0_gnn_in['b_out'], 'L0_ffn_gate_w': _L0_ffn_in['gate_w'], 'L0_ffn_w_gate_up': _L0_ffn_in['w_gate_up'], 'L0_ffn_w_down': _L0_ffn_in['w_down'], 'L0_ffn_shared_w_gate': _L0_ffn_in['shared_w_gate'], 'L0_ffn_shared_w_up': _L0_ffn_in['shared_w_up'], 'L0_ffn_shared_w_down': _L0_ffn_in['shared_w_down'], 'L0_ffn_shared_gate_w': _L0_ffn_in['shared_gate_w']}

def reference(x, adj, L0_gnn_W_seq, L0_gnn_a1, L0_gnn_a2, L0_gnn_W_out, L0_gnn_b_out, L0_ffn_gate_w, L0_ffn_w_gate_up, L0_ffn_w_down, L0_ffn_shared_w_gate, L0_ffn_shared_w_up, L0_ffn_shared_w_down, L0_ffn_shared_gate_w):
    import jax
    import jax.numpy as jnp

    def _L0_gnn_ref(x, adj, W_seq, a1, a2, W_out, b_out):
        import jax, jax.numpy as jnp
        import numpy as np
        N = 2048
        D_IN = 512
        H = 16
        DH = D_IN // H
        ALPHA = 0.2
        MASK_VAL = -65500.0
        seq = (x @ W_seq).reshape(N, H, DH)
        score1 = jnp.einsum('nhd,d->hn', seq, a1)
        score2 = jnp.einsum('nhd,d->hn', seq, a2)
        scores = score1[:, :, None] + score2[:, None, :]
        scores = jax.nn.leaky_relu(scores, negative_slope=ALPHA)
        scores = scores + (1.0 - adj)[None, :, :] * MASK_VAL
        attn = jax.nn.softmax(scores, axis=-1)
        hidden = jnp.einsum('hij,jhd->ihd', attn, seq).reshape(N, D_IN)
        hidden = hidden @ W_out + b_out
        return jax.nn.elu(hidden)

    def _L0_ffn_ref(layer_input, gate_w, w_gate_up, w_down, shared_w_gate, shared_w_up, shared_w_down, shared_gate_w):
        import jax, jax.numpy as jnp
        import numpy as np
        HIDDEN = 512
        MOE_FF = 256
        SHARED_FF = 1408
        NUM_EXPERTS = 16
        TOP_K = 2
        NORM_TOPK = True
        B, S, D = layer_input.shape
        x = layer_input.reshape(-1, D)
        N = x.shape[0]
        shared = jax.nn.silu(x @ shared_w_gate.T) * (x @ shared_w_up.T) @ shared_w_down.T
        shared = shared * jax.nn.sigmoid(x @ shared_gate_w.T)
        logits = x @ gate_w.T
        probs = jax.nn.softmax(logits.astype(jnp.float32), axis=-1)
        rw, sel = jax.lax.top_k(probs, TOP_K)
        if NORM_TOPK:
            rw = rw / rw.sum(axis=-1, keepdims=True)
        rw = rw.astype(x.dtype)
        combine = jnp.zeros((N, NUM_EXPERTS), x.dtype).at[jnp.arange(N)[:, None], sel].set(rw)
        gu = jnp.einsum('nd,edf->nef', x, w_gate_up)
        g, h = jnp.split(gu, 2, axis=-1)
        h = jax.nn.silu(g) * h
        expert_out = jnp.einsum('nef,efd,ne->nd', h, w_down, combine)
        out = expert_out + shared
        return out.reshape(B, S, D)
    x = x + _L0_gnn_ref(_layernorm(x, axis=-1), adj, L0_gnn_W_seq, L0_gnn_a1, L0_gnn_a2, L0_gnn_W_out, L0_gnn_b_out)
    x = x + _L0_ffn_ref(_layernorm(x, axis=-1)[None], L0_ffn_gate_w, L0_ffn_w_gate_up, L0_ffn_w_down, L0_ffn_shared_w_gate, L0_ffn_shared_w_up, L0_ffn_shared_w_down, L0_ffn_shared_gate_w)[0]
    return x

_drawn_inputs = setup_inputs


def setup_inputs(seed=0):
    import zlib

    import numpy as np

    out = dict(_drawn_inputs(seed))
    spreads = {}
    factors = {'L0_gnn_b_out': 7.314, 'L0_ffn_gate_w': 7.599, 'L0_ffn_shared_gate_w': 7.351}
    for name, (base, spread) in spreads.items():
        noise = np.random.default_rng([zlib.crc32(name.encode()), seed]).standard_normal(out[name].shape)
        drawn = base * np.exp(spread * noise) if base else spread * noise
        out[name] = jnp.asarray(drawn.astype(out[name].dtype))
    for name, factor in factors.items():
        out[name] = (out[name] * factor).astype(out[name].dtype)
    return out
```

```python
from contextlib import ExitStack

import concourse.bass as bass
from concourse import mybir

P = 128
N, D = 2048, 512
H, DH = 16, 32
T = N // P
KC = D // P
GW = 2 * (DH + 1)
G_COLS = 3 * GW
PER_BANK = 3
BANKS = -(-T // PER_BANK)
RING = 4
ALPHA = 0.2
STEP = 1.0e30
GSCALE = 256.0
EPS = 1.0e-5
E = 16
FE = 256
FS = 1408
FC = FS // P
SLOTS = 2 * N // P + E

F32 = mybir.dt.float32
F16 = mybir.dt.float16
BF16 = mybir.dt.bfloat16
I32 = mybir.dt.int32
U32 = mybir.dt.uint32
ALU = mybir.AluOpType
ACT = mybir.ActivationFunctionType
AX = mybir.AxisListType
RMAX = bass.bass_isa.ReduceOp.max
STOP_AFTER = 9


class Steps:

    def __init__(self, sem):
        self.sem, self.at = sem, 0

    def did(self, ins):
        ins.then_inc(self.sem, 1)
        self.at = self.at + 1
        return self.at

    def settle(self, eng, ins):
        self.did(ins)
        eng.wait_ge(self.sem, self.at)


def peeled(eng, count, body):
    body(0, True)
    with eng.Fori(1, count) as i:
        body(i, False)


def peeled_both(eng, count, body):
    body(0, True, False)
    with eng.Fori(1, count - 1) as i:
        body(i, False, False)
    body(count - 1, False, True)


def wait_from(eng, sem, value):
    if not (isinstance(value, int) and value <= 0):
        eng.wait_ge(sem, value)


def make_tools(nc, ctx):
    def sb(name, shape, dt):
        return ctx.enter_context(nc.sbuf_tensor(name, shape, dt))

    def ps(name, shape, dt):
        return ctx.enter_context(nc.psum_tensor(name, shape, dt))

    def sem(name):
        return ctx.enter_context(nc.semaphore(name))

    return sb, ps, sem


def attention_operands(nc, io, dram, keep, ident):
    with ExitStack() as ctx:
        sb, ps, sem = make_tools(nc, ctx)
        x_all = keep["hidden"][:].rearrange("p t c -> p (t c)")[:, 0:T * D].rearrange("p (t d) -> p t d", t=T)
        w_seq = sb("w_seq", [P, KC, D], F32)
        w_seq_t = sb("w_seq_t", [P, KC, D], F32)
        a_rep = sb("a_rep", [P, 2], F32)
        a_diag = sb("a_diag", [P, KC, 2 * H], F32)
        v_sb = sb("v_sb", [P, KC, 2 * H], F32)
        stats = sb("stats", [P, T, 6], F32)
        mv = sb("mv", [P, T, 2], F32)
        rstd = sb("rstd", [P, T], F32)
        std = sb("std", [P, T], F32)
        xn_stage = [sb(f"xn_stage{q}", [P, D], F32) for q in range(2)]
        xn_t = [sb(f"xn_t{q}", [P, KC, P], F32) for q in range(2)]
        s_t = sb("s_t", [H, N], F32)
        ones = sb("ones", [P, P], F16)
        empty = sb("empty", [P, N], F16)
        b_max = sb("b_max", [P, H], F32)
        b_top = sb("b_top", [P, H], F32)
        z = sb("z", [P, H, T], F32)
        m = sb("m", [P, H, T], F32)
        ea = sb("ea", [P, H, T], F32)
        eb = sb("eb", [P, H, T], F32)
        a_all = sb("a_all", [P, H, T], F32)
        b_all = sb("b_all", [P, H, T], F32)

        p_xt = [ps(f"p_xt{q}", [P, 512], F32) for q in range(2)]
        p_seq = [ps(f"p_seq{q}", [P, 512], F32) for q in range(2)]
        p_s = [ps(f"p_s{q}", [P, 512], F32) for q in range(2)]
        p_w = [ps(f"p_w{q}", [P, 512], F32) for q in range(2)]

        x_in = sem("x_in")
        w_in = sem("w_in")
        wt_in = sem("wt_in")
        a_in = sem("a_in")
        adj_in = [sem(f"adj_in{j}") for j in range(T)]
        diag_ready = sem("diag_ready")
        ones_ready = sem("ones_ready")
        v_made = sem("v_made")
        v_ready = sem("v_ready")
        var_ready = sem("var_ready")
        std_ready = sem("std_ready")
        normed = sem("normed")
        turned = sem("turned")
        xn_t_ready = sem("xn_t_ready")
        projected = sem("projected")
        seq_saved = sem("seq_saved")
        scores_saved = sem("scores_saved")
        rows_saved = sem("rows_saved")
        max_local = sem("max_local")
        max_all = sem("max_all")
        counted = sem("counted")
        dve_step = Steps(sem("dve_step"))
        pool_step = Steps(sem("pool_step"))
        act_step = Steps(sem("act_step"))
        factors_in = sem("factors_in")
        rows_out = sem("rows_out")
        degree_read = sem("degree_read")
        block = ctx.enter_context(nc.Block())

        @block.sync
        def _(sp):
            sp.dma_start(w_seq_t[:], io["w_seq_t"].rearrange("(c p) k -> p c k", p=P)).then_inc(wt_in, 16)
            sp.dma_start(a_rep[:], io["a_rep"]).then_inc(a_in, 16)
            xv = io["x"].rearrange("(t p) d -> p t d", p=P)
            sp.dma_start(x_all[:, 0:T // 2, :], xv[:, 0:T // 2, :]).then_inc(x_in, 16)
            sp.wait_ge(x_in, 16)
            sp.dma_start(x_all[:, T // 2:T, :], xv[:, T // 2:T, :]).then_inc(x_in, 16)
            sp.dma_start(w_seq[:], io["w_seq"].rearrange("(c p) k -> p c k", p=P)).then_inc(w_in, 16)
            sp.wait_ge(rows_saved, T)
            sp.dma_start(dram["a_rows"], s_t[:]).then_inc(rows_out, 16)
            sp.wait_ge(rows_out, 16)

        @block.gpsimd
        def _(pool):
            for j in range(T):
                pool.dma_start(keep["mask"][:, j, :], io["adj_t"][j * P:(j + 1) * P, :]).then_inc(adj_in[j], 16)
            pool_step.settle(pool, pool.memset(ident[:], 0.0))
            pool_step.settle(pool, pool.affine_select(out=ident[:], in_=ident[:], compare_op=ALU.not_equal,
                                                      fill=1.0, base=0, pattern=[[-1, P]], channel_multiplier=1))
            pool.memset(ones[:], 1.0).then_inc(ones_ready, 1)
            pool_step.settle(pool, pool.memset(a_diag[:], 1.0))
            pool.wait_ge(a_in, 16)
            for w in range(2):
                half = a_diag[:, :, w * H:(w + 1) * H]
                pool_step.settle(pool, pool.tensor_scalar(half, half, a_rep[:, w:w + 1], None, ALU.mult))
                pool_step.settle(pool, pool.affine_select(
                    out=half, in_=half, compare_op=ALU.is_ge, fill=0.0, base=0,
                    pattern=[[P, KC], [-DH, H]], channel_multiplier=1))
                last = pool.affine_select(
                    out=half, in_=half, compare_op=ALU.is_ge, fill=0.0, base=DH - 1,
                    pattern=[[-P, KC], [DH, H]], channel_multiplier=-1)
                last.then_inc(diag_ready, 1)
            pool.wait_ge(max_local, 1)
            pool.partition_all_reduce(b_top[:], b_max[:], P, RMAX).then_inc(max_all, 1)

        @block.tensor
        def _(pe):
            pe.wait_ge(wt_in, 16)
            pe.wait_ge(diag_ready, 2)
            for k in range(KC):
                if k >= 2:
                    pe.wait_ge(v_ready, k - 1)
                for c in range(KC):
                    mm = pe.matmul(p_s[k % 2][:, 0:2 * H], w_seq_t[:, c, k * P:(k + 1) * P], a_diag[:, c, :],
                                   start=(c == 0), stop=(c == KC - 1))
                mm.then_inc(v_made, 1)
            pe.wait_ge(v_ready, KC)
            pe.wait_ge(w_in, 16)

            def tile_pair(i, first):
                for q in range(2):
                    t = i * 2 + q
                    pe.wait_ge(normed, t + 1)
                    if not first:
                        pe.wait_ge(xn_t_ready, t - 1)
                    for c in range(KC):
                        tr = pe.transpose(p_xt[q][:, c * P:(c + 1) * P],
                                          xn_stage[q][:, c * P:(c + 1) * P], ident[:])
                    tr.then_inc(turned, 1)
                for q in range(2):
                    t = i * 2 + q
                    pe.wait_ge(xn_t_ready, t + 1)
                    if not first:
                        pe.wait_ge(seq_saved, t - 1)
                        pe.wait_ge(scores_saved, t - 1)
                        pe.wait_ge(rows_saved, t - 1)
                    for c in range(KC):
                        pe.matmul(p_seq[q][:], xn_t[q][:, c, :], w_seq[:, c, :], start=(c == 0), stop=(c == KC - 1))
                    for c in range(KC):
                        pe.matmul(p_s[q][:, 0:2 * H], xn_t[q][:, c, :], v_sb[:, c, :],
                                  start=(c == 0), stop=(c == KC - 1))
                    for c in range(KC):
                        mm = pe.matmul(p_s[q][0:H, 128:256], v_sb[:, c, 0:H], xn_t[q][:, c, :],
                                       start=(c == 0), stop=(c == KC - 1))
                    mm.then_inc(projected, 1)

            peeled(pe, T // 2, tile_pair)

            pe.wait_ge(ones_ready, 1)
            for b in range(4):
                if b >= 2:
                    pe.wait_ge(degree_read, b - 1)
                for j in range(T):
                    if b == 0:
                        pe.wait_ge(adj_in[j], 16)
                    mm = pe.matmul(p_w[b % 2][:], ones[:], keep["mask"][:, j, b * 512:(b + 1) * 512],
                                   start=(j == 0), stop=(j == T - 1))
                mm.then_inc(counted, 1)

        @block.scalar
        def _(act):
            for k in range(KC):
                act.wait_ge(v_made, k + 1)
                act.activation(v_sb[:, k, :], p_s[k % 2][:, 0:2 * H], ACT.Copy).then_inc(v_ready, 1)
            act.wait_ge(var_ready, 1)
            act.activation(std[:], rstd[:], ACT.Sqrt).then_inc(std_ready, 1)

            def tile_pair(i, first):
                for q in range(2):
                    t = i * 2 + q
                    act.wait_ge(turned, t + 1)
                    if not first:
                        act.wait_ge(projected, t - 1)
                    act.activation(xn_t[q][:].rearrange("p c m -> p (c m)"), p_xt[q][:],
                                   ACT.Copy).then_inc(xn_t_ready, 1)
                for q in range(2):
                    t = i * 2 + q
                    act.wait_ge(projected, t + 1)
                    act.activation(s_t[:, bass.ds(t * P, P)], p_s[q][0:H, 128:256], ACT.Copy).then_inc(rows_saved, 1)
                    act.activation(keep["seq"][:, bass.ds(t * D, D)], p_seq[q][:], ACT.Copy).then_inc(seq_saved, 1)

            peeled(act, T // 2, tile_pair)
            act.wait_ge(factors_in, 1)
            act_step.did(act.activation(keep["e_pos"][:], ea[:], ACT.Exp))
            act_step.did(act.activation(keep["e_neg"][:], eb[:], ACT.Exp))
            act_step.did(act.activation(keep["f_pos"][:], z[:], ACT.Exp))
            act_step.did(act.activation(keep["f_neg"][:], m[:], ACT.Exp))
            act.wait_ge(act_step.sem, act_step.at)

        @block.vector
        def _(dve):
            dve.wait_ge(x_in, 32)
            for t in range(T):
                last = dve.bn_stats(stats[:, t, :], x_all[:, t, :])
            dve_step.settle(dve, last)
            for t in range(T):
                last = dve.bn_aggr(mv[:, t, :], stats[:, t, :])
            dve_step.settle(dve, last)
            dve.tensor_scalar(rstd[:], mv[:, :, 1], EPS, None, ALU.add).then_inc(var_ready, 1)
            dve.wait_ge(std_ready, 1)
            dve_step.settle(dve, dve.reciprocal(rstd[:], std[:]))
            base = dve_step.at

            def tile_pair(i, first):
                for q in range(2):
                    t = i * 2 + q
                    if not first:
                        dve.wait_ge(turned, t - 1)
                    dve.tensor_scalar(xn_stage[q][:], x_all[:, bass.ds(t, 1), :].rearrange("p a d -> p (a d)"),
                                      mv[:, bass.ds(t, 1), 0], rstd[:, bass.ds(t, 1)],
                                      ALU.subtract, ALU.mult).then_inc(normed, 1)
                for q in range(2):
                    t = i * 2 + q
                    dve.wait_ge(projected, t + 1)
                    dve.wait_ge(rows_saved, t + 1)
                    dve.tensor_copy(a_all[:, :, bass.ds(t, 1)].rearrange("p h a -> p (h a)"), p_s[q][:, 0:H])
                    dve.tensor_copy(b_all[:, :, bass.ds(t, 1)].rearrange("p h a -> p (h a)"),
                                    p_s[q][:, H:2 * H]).then_inc(scores_saved, 1)

            peeled(dve, T // 2, tile_pair)
            dve.wait_ge(scores_saved, T)
            dve.tensor_reduce(b_max[:], b_all[:], AX.X, ALU.max).then_inc(max_local, 1)
            dve.tensor_scalar(keep["neg_b"][:], b_all[:], -1.0, None, ALU.mult)
            dve_step.did(dve.tensor_scalar(keep["step_b"][:], b_all[:], STEP, None, ALU.mult))
            dve.wait_ge(max_all, 1)
            top = b_top[:].unsqueeze(2).broadcast_to([P, H, T])
            dve_step.settle(dve, dve.tensor_tensor(z[:], a_all[:], top, ALU.add))
            dve_step.settle(dve, dve.tensor_tensor(ea[:], b_all[:], top, ALU.subtract))
            dve_step.settle(dve, dve.tensor_scalar(eb[:], ea[:], ALPHA, None, ALU.mult))
            dve_step.settle(dve, dve.scalar_tensor_tensor(m[:], z[:], ALPHA, z[:], ALU.mult, ALU.max))
            dve_step.settle(dve, dve.scalar_tensor_tensor(b_all[:], z[:], ALPHA, m[:], ALU.mult, ALU.subtract))
            dve_step.settle(dve, dve.tensor_tensor(z[:], z[:], m[:], ALU.subtract))
            dve.tensor_copy(m[:], b_all[:]).then_inc(factors_in, 1)
            for b in range(4):
                dve.wait_ge(counted, b + 1)
                last = dve.tensor_scalar(empty[:, b * 512:(b + 1) * 512], p_w[b % 2][:], 0.0, None, ALU.is_equal)
                last.then_inc(degree_read, 1)
            dve.wait_ge(degree_read, 4)
            for j in range(T):
                last = dve.tensor_tensor(keep["mask"][:, j, :], keep["mask"][:, j, :], empty[:], ALU.max)
            dve_step.settle(dve, last)


def attention_heads(nc, io, dram, keep):
    with ExitStack() as ctx:
        sb, ps, sem = make_tools(nc, ctx)
        SOFT = [j for j in range(T) if j % 4 != 1]
        a_row = [sb(f"a_row{q}", [P, N], F32) for q in range(2)]
        pick = [sb(f"pick{r}", [P, N], F16) for r in range(RING)]
        over = [sb(f"over{r}", [P, N], BF16) for r in range(2)]
        g32 = sb("g32", [P, T, GW], F32)
        g = [sb(f"g{q}", [P, T, G_COLS], F16) for q in range(2)]
        sums = sb("sums", [P, T, 2 * GW], F32)
        acc = ps("acc", [P, BANKS, 512], F32)

        rows_in = [sem(f"rows_in{q}") for q in range(2)]
        weighted = sem("weighted")
        high_ready = sem("high_ready")
        low_ready = sem("low_ready")
        g_ready = sem("g_ready")
        over_ready = sem("over_ready")
        over_used = sem("over_used")
        pick_used = sem("pick_used")
        head_summed = sem("head_summed")
        bank_read = sem("bank_read")
        combined = sem("combined")
        hard_used = sem("hard_used")
        folded = sem("folded")
        block = ctx.enter_context(nc.Block())
        S = len(SOFT)
        HARD = [j for j in range(T) if j not in SOFT]
        mask, seq = keep["mask"], keep["seq"]

        @block.gpsimd
        def _(pool):
            def heads(i, first):
                for q in range(2):
                    h = i * 2 + q
                    if not first:
                        pool.wait_ge(over_ready, (h - 1) * S)
                        pool.wait_ge(hard_used, (h - 1) * (T - S))
                    pool.dma_start(a_row[q][:], dram["a_rows"][bass.ds(h, 1), :].broadcast_to([P, N]))\
                        .then_inc(rows_in[q], 16)
            peeled(pool, H // 2, heads)

        @block.scalar
        def _(act):
            def high_part(h, q):
                act.wait_ge(weighted, (h + 1) * 4)
                act.activation(g[q][:, :, 0:GW], g32[:], ACT.Copy).then_inc(high_ready, 1)

            def turned_part(h, q):
                act.wait_ge(low_ready, h + 1)
                act.activation(g[q][:, :, 2 * GW:3 * GW].rearrange("p t (s c) -> p t s c", s=2),
                               g[q][:, :, 0:2 * GW].rearrange("p t (s c) -> p t s c", s=2)[:, :, :, DH + 1:GW],
                               ACT.Copy, scale=-1.0).then_inc(g_ready, 1)

            def drain_banks(h):
                act.wait_ge(head_summed, h + 1)
                for b in range(BANKS):
                    n = min(PER_BANK, T - b * PER_BANK)
                    act.activation(sums[:, b * PER_BANK:b * PER_BANK + n, :].rearrange("p t c -> p (t c)"),
                                   acc[:, b, 0:n * 2 * GW], ACT.Copy).then_inc(bank_read, 1)

            high_part(0, 0)
            turned_part(0, 0)

            def heads(i, first, last):
                for q in range(2):
                    h = i * 2 + q
                    act.wait_ge(rows_in[q], (i + 1) * 16)
                    for n, j in enumerate(SOFT):
                        if not (first and q == 0 and n < 2):
                            act.wait_ge(over_used, h * S + n - 1)
                        act.activation(over[n % 2][:], a_row[q][:], ACT.Relu, scale=STEP,
                                       bias=keep["step_b"][:, bass.ds(h * T + j, 1)]).then_inc(over_ready, 1)
                        if n == 2 and not (first and q == 0):
                            if not (first and q == 1):
                                act.wait_ge(combined, h - 1)
                            drain_banks(h - 1)
                        if n == 4 and not (last and q == 1):
                            high_part(h + 1, 1 - q)
                        if n == 6 and not (last and q == 1):
                            turned_part(h + 1, 1 - q)

            peeled_both(act, H // 2, heads)
            act.wait_ge(combined, H - 1)
            drain_banks(H - 1)

        @block.vector
        def _(dve):
            def operand(h, first):
                if not first:
                    dve.wait_ge(low_ready, h)
                for s, e in enumerate(("e_pos", "e_neg")):
                    w = keep[e][:, bass.ds(h * T, T)]
                    lo = s * (DH + 1)
                    dve.scalar_tensor_tensor(
                        g32[:, :, lo:lo + DH], seq[:].rearrange("p (t d) -> p t d", t=T)[:, :, bass.ds(h * DH, DH)],
                        GSCALE, w.unsqueeze(2).broadcast_to([P, T, DH]), ALU.mult, ALU.mult).then_inc(weighted, 1)
                    dve.tensor_scalar(g32[:, :, lo + DH], w, GSCALE, None, ALU.mult).then_inc(weighted, 1)

            def low_part(h, q):
                dve.wait_ge(high_ready, h + 1)
                dve.tensor_tensor(g[q][:, :, GW:2 * GW], g32[:], g[q][:, :, 0:GW], ALU.subtract).then_inc(low_ready, 1)

            def combine(h):
                dve.wait_ge(bank_read, (h + 1) * BANKS)
                halves = sums[:, :, 0:GW]
                dve.tensor_tensor(halves, halves, sums[:, :, GW:2 * GW], ALU.add).then_inc(folded, 1)
                dve.wait_ge(folded, h * 3 + 1)
                for s, f in enumerate(("f_pos", "f_neg")):
                    part = sums[:, :, s * (DH + 1):(s + 1) * (DH + 1)]
                    w = keep[f][:, bass.ds(h * T, T)]
                    dve.tensor_tensor(part, part, w.unsqueeze(2).broadcast_to([P, T, DH + 1]),
                                      ALU.mult).then_inc(folded, 1)
                dve.wait_ge(folded, h * 3 + 3)
                dve.tensor_tensor(keep["hidden"][:, :, bass.ds(h * (DH + 1), DH + 1)],
                                  sums[:, :, 0:DH + 1], sums[:, :, DH + 1:GW], ALU.subtract).then_inc(combined, 1)

            operand(0, True)
            low_part(0, 0)

            def heads(i, first, last):
                for q in range(2):
                    h = i * 2 + q
                    dve.wait_ge(rows_in[q], (i + 1) * 16)
                    n = 0
                    for j in range(T):
                        slot = (q * T + j) % RING
                        if not (first and q * T + j < RING):
                            dve.wait_ge(pick_used, h * T + j - RING + 1)
                        if j in SOFT:
                            dve.wait_ge(over_ready, h * S + n + 1)
                            op = dve.tensor_tensor(pick[slot][:], over[n % 2][:], mask[:, j, :], ALU.min)
                            op.then_inc(over_used, 1)
                            n += 1
                        else:
                            op = dve.scalar_tensor_tensor(pick[slot][:], a_row[q][:],
                                                          keep["neg_b"][:, bass.ds(h * T + j, 1)], mask[:, j, :],
                                                          ALU.is_gt, ALU.mult)
                            op.then_inc(hard_used, 1)
                        if j == 3 and not (last and q == 1):
                            operand(h + 1, False)
                        if j == 7 and not (last and q == 1):
                            low_part(h + 1, 1 - q)
                        if j == 12 and not (first and q == 0):
                            combine(h - 1)
            peeled_both(dve, H // 2, heads)
            combine(H - 1)

        @block.tensor
        def _(pe):
            def heads(i, first):
                for q in range(2):
                    h = i * 2 + q
                    pe.wait_ge(g_ready, h + 1)
                    for j in range(T):
                        slot = (q * T + j) % RING
                        if j in SOFT:
                            pe.wait_ge(over_used, h * S + SOFT.index(j) + 1)
                        else:
                            pe.wait_ge(hard_used, h * (T - S) + HARD.index(j) + 1)
                        for t in range(T):
                            b, r = divmod(t, PER_BANK)
                            if j == 0 and r == 0 and not (first and q == 0):
                                pe.wait_ge(bank_read, (h - 1) * BANKS + b + 1)
                            out = acc[:, b, r * 2 * GW:(r + 1) * 2 * GW]
                            mm = pe.matmul(out, pick[slot][:, t * P:(t + 1) * P], g[q][:, j, 0:2 * GW],
                                           start=(j == 0 and r == 0), stop=False, skip_group_check=True)
                            if t == T - 1:
                                mm.then_inc(pick_used, 1)
                            mm = pe.matmul(out.rearrange("p (s c) -> p s c", s=2)[:, :, DH + 1:GW],
                                           mask[:, j, t * P:(t + 1) * P],
                                           g[q][:, j, 2 * GW:3 * GW].rearrange("p (s c) -> p s c", s=2),
                                           start=False, stop=(j == T - 1), skip_group_check=True)
                    mm.then_inc(head_summed, 1)
            peeled(pe, H // 2, heads)


def output_projection(nc, io, dram, keep, ident):
    with ExitStack() as ctx:
        sb, ps, sem = make_tools(nc, ctx)
        hidden, x1 = keep["hidden"], keep["x1"]
        rden = sb("rden", [P, T, H], F32)
        w_out = sb("w_out", [P, KC, D], F32)
        b_out = sb("b_out", [P, D], F32)
        w_route = sb("w_route", [P, KC, E + 1], F32)
        heads = [sb(f"heads{q}", [P, D], F32) for q in range(2)]
        heads_t = [sb(f"heads_t{q}", [P, KC, P], F32) for q in range(2)]
        x_in_tile = [sb(f"x_in_tile{q}", [P, D], F32) for q in range(2)]
        y = [sb(f"y{q}", [P, D], F32) for q in range(2)]
        below = [sb(f"below{q}", [P, D], F32) for q in range(2)]
        stats = sb("stats2", [P, T, 6], F32)
        mv = sb("mv2", [P, T, 2], F32)
        var = sb("var2", [P, T], F32)
        std = sb("std2", [P, T], F32)
        rstd = sb("rstd2", [P, T], F32)
        xn = [sb(f"xn{q}", [P, D], F32) for q in range(2)]
        xn_t = [sb(f"xn2_t{q}", [P, KC, P], F32) for q in range(2)]
        p_t = [ps(f"p_t{q}", [P, 512], F32) for q in range(2)]
        p_y = [ps(f"p_y{q}", [P, 512], F32) for q in range(2)]
        p_x = [ps(f"p_x{q}", [P, 512], F32) for q in range(2)]
        p_l = [ps(f"p_l{q}", [P, 512], F32) for q in range(2)]

        w_in, b_in, r_in = sem("w_out_in"), sem("b_out_in"), sem("w_route_in")
        x_in = [sem(f"x_in_tile{q}") for q in range(2)]
        paced = sem("paced3")
        rden_ready = sem("rden_ready")
        head_scaled = sem("head_scaled")
        head_turned = sem("head_turned")
        heads_t_ready = sem("heads_t_ready")
        projected = sem("out_projected")
        biased = sem("biased")
        capped = sem("capped")
        below_ready = sem("below_ready")
        above_added = sem("above_added")
        x1_ready = sem("x1_ready")
        stats_ready = sem("stats_ready")
        var_ready, std_ready, rstd_ready = sem("var2_ready"), sem("std2_ready"), sem("rstd2_ready")
        normed = sem("normed2")
        xn_saved = [sem(f"xn_saved{q}") for q in range(2)]
        turned = sem("turned2")
        xn_t_ready = sem("xn2_t_ready")
        high_ready = sem("x_high_ready")
        low_ready = sem("x_low_ready")
        routed = sem("routed")
        logits_saved = sem("logits_saved")
        block = ctx.enter_context(nc.Block())

        @block.sync
        def _(sp):
            sp.dma_start(w_out[:], io["w_out"].rearrange("(c p) k -> p c k", p=P)).then_inc(w_in, 16)
            sp.dma_start(b_out[:], io["b_out"].broadcast_to([P, D])).then_inc(b_in, 16)
            for q in range(2):
                sp.dma_start(x_in_tile[q][:], io["x"][q * P:(q + 1) * P, :]).then_inc(x_in[q], 16)
            sp.dma_start(w_route[:], io["w_route"].rearrange("(c p) e -> p c e", p=P)).then_inc(r_in, 16)
            with sp.Fori(1, T // 2) as i:
                for q in range(2):
                    t = i * 2 + q
                    sp.wait_ge(above_added, t - 1)
                    sp.sem_inc(paced, 1)
                    sp.dma_start(x_in_tile[q][:], io["x"][bass.ds(t * P, P), :]).then_inc(x_in[q], 16)

        @block.gpsimd
        def _(pool):
            def tile_pair(i, first):
                for q in range(2):
                    t = i * 2 + q
                    pool.wait_ge(normed, t + 1)
                    pool.dma_start(dram["xn_rows"][bass.ds(t * P, P), :], xn[q][:]).then_inc(xn_saved[q], 16)
            peeled(pool, T // 2, tile_pair)
            for q in range(2):
                pool.wait_ge(xn_saved[q], 16 * (T // 2))

        @block.tensor
        def _(pe):
            pe.wait_ge(w_in, 16)

            def project(i, first):
                for q in range(2):
                    t = i * 2 + q
                    pe.wait_ge(head_scaled, t + 1)
                    if not first:
                        pe.wait_ge(heads_t_ready, t - 1)
                    for c in range(KC):
                        tr = pe.transpose(p_t[q][:, c * P:(c + 1) * P], heads[q][:, c * P:(c + 1) * P], ident[:])
                    tr.then_inc(head_turned, 1)
                for q in range(2):
                    t = i * 2 + q
                    pe.wait_ge(heads_t_ready, t + 1)
                    if not first:
                        pe.wait_ge(biased, t - 1)
                    for c in range(KC):
                        mm = pe.matmul(p_y[q][:], heads_t[q][:, c, :], w_out[:, c, :],
                                       start=(c == 0), stop=(c == KC - 1))
                    mm.then_inc(projected, 1)
            peeled(pe, T // 2, project)

            pe.wait_ge(r_in, 16)

            def route(i, first):
                for q in range(2):
                    t = i * 2 + q
                    pe.wait_ge(normed, t + 1)
                    if not first:
                        pe.wait_ge(xn_t_ready, t - 1)
                        pe.wait_ge(low_ready, t - 1)
                    for c in range(KC):
                        tr = pe.transpose(p_x[q][:, c * P:(c + 1) * P], xn[q][:, c * P:(c + 1) * P], ident[:])
                    tr.then_inc(turned, 1)
                for q in range(2):
                    t = i * 2 + q
                    pe.wait_ge(xn_t_ready, t + 1)
                    if not first:
                        pe.wait_ge(logits_saved, t - 1)
                    for c in range(KC):
                        mm = pe.matmul(p_l[q][:, 0:E + 1], xn_t[q][:, c, :], w_route[:, c, :],
                                       start=(c == 0), stop=(c == KC - 1))
                    mm.then_inc(routed, 1)
            peeled(pe, T // 2, route)

        @block.scalar
        def _(act):
            def project(i, first):
                for q in range(2):
                    t = i * 2 + q
                    act.wait_ge(head_turned, t + 1)
                    if not first:
                        act.wait_ge(projected, t - 1)
                    act.activation(heads_t[q][:].rearrange("p c m -> p (c m)"), p_t[q][:], ACT.Copy)\
                       .then_inc(heads_t_ready, 1)
                for q in range(2):
                    t = i * 2 + q
                    act.wait_ge(capped, t + 1)
                    act.activation(below[q][:], below[q][:], ACT.Exp).then_inc(below_ready, 1)
            peeled(act, T // 2, project)
            act.wait_ge(var_ready, 1)
            act.activation(std[:], var[:], ACT.Sqrt).then_inc(std_ready, 1)

            def route(i, first):
                for q in range(2):
                    t = i * 2 + q
                    act.wait_ge(turned, t + 1)
                    if not first:
                        act.wait_ge(routed, t - 1)
                        act.wait_ge(low_ready, t - 1)
                    act.activation(xn_t[q][:].rearrange("p c m -> p (c m)"), p_x[q][:], ACT.Copy)\
                       .then_inc(xn_t_ready, 1)
                    act.activation(keep["x_high"][:, :, bass.ds(t * P, P)],
                                   p_x[q][:].rearrange("p (c m) -> p c m", c=KC), ACT.Copy).then_inc(high_ready, 1)
            peeled(act, T // 2, route)

        @block.vector
        def _(dve):
            dens = hidden[:].rearrange("p t (h c) -> p t h c", h=H)[:, :, :, DH]
            dve.reciprocal(rden[:], dens).then_inc(rden_ready, 1)
            dve.wait_ge(rden_ready, 1)
            dve.wait_ge(b_in, 16)

            def project(i, first):
                for q in range(2):
                    t = i * 2 + q
                    if not first:
                        dve.wait_ge(head_turned, t - 1)
                    dve.tensor_tensor(
                        heads[q][:].rearrange("p (h d) -> p h d", h=H),
                        hidden[:, bass.ds(t, 1), :].rearrange("p a (h c) -> p (a h) c", h=H)[:, :, 0:DH],
                        rden[:, bass.ds(t, 1), :].rearrange("p a h -> p (a h)").unsqueeze(2).broadcast_to([P, H, DH]),
                        ALU.mult).then_inc(head_scaled, 1)
                for q in range(2):
                    t = i * 2 + q
                    row = x1[:, bass.ds(t, 1), :].rearrange("p a d -> p (a d)")
                    dve.wait_ge(projected, t + 1)
                    dve.tensor_tensor(y[q][:], p_y[q][:], b_out[:], ALU.add).then_inc(biased, 1)
                    dve.wait_ge(biased, t + 1)
                    dve.tensor_scalar(below[q][:], y[q][:], 0.0, None, ALU.min).then_inc(capped, 1)
                    dve.wait_ge(x_in[q], i * 16 + 16)
                    dve.scalar_tensor_tensor(row, y[q][:], 0.0, x_in_tile[q][:], ALU.max, ALU.add)\
                       .then_inc(above_added, 1)
                for q in range(2):
                    t = i * 2 + q
                    row = x1[:, bass.ds(t, 1), :].rearrange("p a d -> p (a d)")
                    dve.wait_ge(below_ready, t + 1)
                    dve.wait_ge(above_added, t + 1)
                    dve.scalar_tensor_tensor(row, below[q][:], -1.0, row, ALU.add, ALU.add).then_inc(x1_ready, 1)
                    dve.wait_ge(x1_ready, t + 1)
                    dve.bn_stats(stats[:, bass.ds(t, 1), :].rearrange("p a s -> p (a s)"), row)\
                       .then_inc(stats_ready, 1)
            peeled(dve, T // 2, project)
            dve.wait_ge(stats_ready, T)
            for t in range(T):
                last = dve.bn_aggr(mv[:, t, :], stats[:, t, :])
            last.then_inc(stats_ready, 1)
            dve.wait_ge(stats_ready, T + 1)
            dve.tensor_scalar(var[:], mv[:, :, 1], EPS, None, ALU.add).then_inc(var_ready, 1)
            dve.wait_ge(std_ready, 1)
            dve.reciprocal(rstd[:], std[:]).then_inc(rstd_ready, 1)
            dve.wait_ge(rstd_ready, 1)

            def route(i, first):
                for q in range(2):
                    t = i * 2 + q
                    if not first:
                        dve.wait_ge(xn_saved[q], i * 16)
                        dve.wait_ge(turned, t - 1)
                    dve.tensor_scalar(xn[q][:], x1[:, bass.ds(t, 1), :].rearrange("p a d -> p (a d)"),
                                      mv[:, bass.ds(t, 1), 0], rstd[:, bass.ds(t, 1)],
                                      ALU.subtract, ALU.mult).then_inc(normed, 1)
                for q in range(2):
                    t = i * 2 + q
                    dve.wait_ge(high_ready, t + 1)
                    dve.tensor_tensor(keep["x_low"][:, :, bass.ds(t * P, P)], xn_t[q][:],
                                      keep["x_high"][:, :, bass.ds(t * P, P)], ALU.subtract).then_inc(low_ready, 1)
                for q in range(2):
                    t = i * 2 + q
                    dve.wait_ge(routed, t + 1)
                    dve.tensor_copy(keep["logits"][:, bass.ds(t, 1), :].rearrange("p a e -> p (a e)"),
                                    p_l[q][:, 0:E + 1]).then_inc(logits_saved, 1)
            peeled(dve, T // 2, route)


def feed_forward(nc, io, dram, keep, ident, out):
    with ExitStack() as ctx:
        sb, ps, sem = make_tools(nc, ctx)
        x1, x_high, x_low, logits = keep["x1"], keep["x_high"], keep["x_low"], keep["logits"]
        WS = 256.0
        BLK = 512
        BLOCKS = N // BLK
        TB = BLK // P

        count_e = sb("count_e", [P, P], F32)
        node_id = sb("node_id", [P, T], F32)
        before = sb("before", [P, P], F16)
        ones = sb("ones2", [P, P], F16)
        upto = sb("upto", [P, E, E], F32)
        raw = sb("raw", [P, T, E], F32)
        key = sb("key", [P, T, E], F32)
        hit = [sb(f"hit{k}", [P, T, E], F32) for k in range(2)]
        top = [sb(f"top{k}", [P, T], F32) for k in range(2)]
        low_key = sb("low_key", [P, T], F32)
        both_led = sb("both_led", [P, T + 1, E], F16)
        both = both_led[:, 1:T + 1, :]
        ratio = sb("ratio", [P, T], F32)
        share = [sb(f"share{k}", [P, T], F32) for k in range(2)]
        sgate = sb("sgate", [P, T], F32)
        held = sb("held", [P, E], F32)
        cube = sb("cube", [P, E, E], F32)
        tiles = sb("tiles", [P, E], F32)
        ends = sb("ends", [P, E], F32)
        base = sb("base", [P, E], F32)
        place = sb("place", [P, T, E], F32)
        past = sb("past", [P, SLOTS, E], F32)
        owner_f = sb("owner_f", [P, SLOTS], F32)
        owner = sb("owner", [P, SLOTS], I32)
        row_f = [sb(f"row_f{k}", [P, T], F32) for k in range(2)]
        row_i = [sb(f"row_i{k}", [P, T], I32) for k in range(2)]
        in_tile = [sb(f"in_tile{k}", [P, T], I32) for k in range(2)]
        in_tile_f = [sb(f"in_tile_f{k}", [P, T], F32) for k in range(2)]
        slot_f = [sb(f"slot_f{k}", [P, T], F32) for k in range(2)]
        at_row = [sb(f"at_row{k}", [P, P], F16) for k in range(2)]
        at_slot = [sb(f"at_slot{k}", [P, SLOTS], F16) for k in range(2)]
        tokens = sb("tokens", [P, SLOTS], I32)

        w_high = sb("w_high", [P, FC, 3, D], F16)
        w_low = sb("w_low", [P, FC, 3, D], F16)
        silu = [sb(f"silu{q}", [P, BLK], F32) for q in range(2)]
        act32 = [sb(f"act32{q}", [P, BLK], F32) for q in range(2)]
        a_high = [sb(f"a_high{q}", [P, BLK], F16) for q in range(2)]
        a_low = [sb(f"a_low{q}", [P, BLK], F16) for q in range(2)]

        w_gu = [sb(f"w_gu{q}", [P, KC, 2 * FE], F32) for q in range(2)]
        w_raw = [w_gu[q][:, 0:3, :] for q in range(2)]
        w_dn = [sb(f"w_dn{q}", [P, FE // P, D], F32) for q in range(2)]
        pick_now = [sb(f"pick_now{q}", [P, 1], I32) for q in range(2)]
        xg = [sb(f"xg{q}", [P, D], F32) for q in range(2)]
        xg_t = [sb(f"xg_t{q}", [P, D], F32) for q in range(2)]
        e_silu = [sb(f"e_silu{q}", [P, FE], F32) for q in range(2)]
        e_act = [sb(f"e_act{q}", [P, FE], F32) for q in range(2)]
        e_act_t = [sb(f"e_act_t{q}", [P, FE], F32) for q in range(2)]
        y_out = [sb(f"y_out{q}", [P, D], F32) for q in range(2)]

        y_buf = [[xg[0][:], xg[1][:]], [xg_t[0][:], xg_t[1][:]]]

        bank = [ps(f"bank{b}", [P, 512], F32) for b in range(8)]

        consts_ready = sem("consts_ready")
        dve_step = Steps(sem("route_step"))
        pool_step = Steps(sem("pool_const_step"))
        exps_in, exps_out = sem("exps_in"), sem("exps_out")
        both_ready, ranked = sem("both_ready"), sem("ranked")
        marked, mark_used = sem("marked"), sem("mark_used")
        listed, tokens_ready = sem("listed"), sem("tokens_ready")
        w_in = [sem(f"w_in{q}") for q in range(2)]
        w_high_ready, w_low_ready = sem("w_high_ready"), sem("w_low_ready")
        gated, silu_ready, act_ready = sem("gated"), sem("silu_ready"), sem("act_ready")
        a_high_ready, a_low_ready = sem("a_high_ready"), sem("a_low_ready")
        downed, block_done, added = sem("downed"), sem("block_done"), sem("added")
        e_w_in = [sem(f"e_w_in{q}") for q in range(2)]
        pick_set, gathered = sem("pick_set"), [sem(f"gathered{q}") for q in range(2)]
        e_turned, xg_t_ready = sem("e_turned"), sem("xg_t_ready")
        e_gated, e_silu_ready, e_act_ready = sem("e_gated"), sem("e_silu_ready"), sem("e_act_ready")
        e_act_turned, e_act_t_ready = sem("e_act_turned"), sem("e_act_t_ready")
        e_downed, y_ready, y_saved = sem("e_downed"), sem("y_ready"), [sem(f"y_saved{q}") for q in range(2)]
        paced, pool_paced = sem("paced"), sem("pool_paced")
        y_pick_set = sem("y_pick_set")
        y_in = [[sem(f"y_in{q}{k}") for k in range(2)] for q in range(2)]
        y_added = sem("y_added")
        out_saved = sem("out_saved")
        block = ctx.enter_context(nc.Block())
        PAIRS = SLOTS // 2

        @block.sync
        def _(sp):
            for f in range(FC):
                if f >= 2:
                    sp.wait_ge(w_low_ready, f - 1)
                sp.dma_start(w_raw[f % 2], io["w_shared"][f]).then_inc(w_in[f % 2], 16)
            sp.wait_ge(tokens_ready, 1)
            sp.wait_ge(w_low_ready, FC)

            def load(q, s):
                e = sp.value_load(owner[0:1, bass.ds(s, 1)], min_val=0, max_val=E - 1)
                sp.dma_start(w_gu[q][:], io["w_gate_up"][bass.ds(e, 1)].rearrange("a (c p) f -> p (a c) f", p=P))\
                  .then_inc(e_w_in[q], 16)
                sp.dma_start(w_dn[q][:], io["w_down"][bass.ds(e, 1)].rearrange("a (c p) f -> p (a c) f", p=P))\
                  .then_inc(e_w_in[q], 16)

            def slots(i, last):
                for q in range(2):
                    s = i * 2 + q
                    sp.wait_ge(y_ready, s + 1)
                    sp.sem_inc(paced, 1)
                    sp.dma_start(dram["y_rows"][bass.ds(s * P, P), :], y_out[q][:]).then_inc(y_saved[q], 16)
                    if not last:
                        load(q, s + 2)
            load(0, 0)
            load(1, 1)
            with sp.Fori(0, PAIRS - 1) as i:
                slots(i, False)
            slots(PAIRS - 1, True)

            def results(i, first):
                for q in range(2):
                    t = i * 2 + q
                    sp.wait_ge(y_added, 2 * t + 2)
                    sp.sem_inc(paced, 1)
                    sp.dma_start(out[bass.ds(t * P, P), :], x1[:, bass.ds(t, 1), :].rearrange("p a d -> p (a d)"))\
                      .then_inc(out_saved, 16)
            peeled(sp, T // 2, results)
            sp.wait_ge(out_saved, 16 * T)

        @block.gpsimd
        def _(pool):
            pool_step.did(pool.iota(past[:, 0:P // E, :].rearrange("p a e -> p (a e)").bitcast(I32),
                                    pattern=[[1, P]], base=0, channel_multiplier=0))
            pool_step.settle(pool, pool.iota(row_i[0][:], pattern=[[P, T]], base=0, channel_multiplier=1))
            pool.tensor_copy(count_e[:], past[:, 0:P // E, :].rearrange("p a e -> p (a e)").bitcast(I32))\
                .then_inc(consts_ready, 1)
            pool.tensor_copy(node_id[:], row_i[0][:]).then_inc(consts_ready, 1)
            pool.memset(ones[:], 1.0).then_inc(consts_ready, 1)
            pool.memset(both_led[:, 0, :], 0.0).then_inc(consts_ready, 1)
            pool_step.did(pool.memset(before[:], 1.0))
            pool_step.settle(pool, pool.memset(upto[:], 1.0))
            pool.affine_select(out=before[:], in_=before[:], compare_op=ALU.is_gt, fill=0.0, base=0,
                               pattern=[[1, P]], channel_multiplier=-1).then_inc(consts_ready, 1)
            pool.affine_select(out=upto[:], in_=upto[:], compare_op=ALU.is_ge, fill=0.0, base=0,
                               pattern=[[1, E], [-1, E]], channel_multiplier=0).then_inc(consts_ready, 1)
            pool.wait_ge(tokens_ready, 1)

            def gather(s, q):
                pool.tensor_copy(pick_now[q][:], tokens[:, bass.ds(s, 1)]).then_inc(pick_set, 1)
                pool.wait_ge(pick_set, s + 1)
                pool.sem_inc(pool_paced, 1)
                pool.indirect_dma_start(out=xg[q][:], out_offset=None, in_=dram["xn_rows"],
                                        in_offset=bass.IndirectOffsetOnAxis(ap=pick_now[q][:], axis=0))\
                    .then_inc(gathered[q], 16)

            def slots(i, first):
                for q in range(2):
                    s = i * 2 + q
                    if not first:
                        pool.wait_ge(e_turned, s - 1)
                    gather(s, q)
            peeled(pool, PAIRS, slots)

            for q in range(2):
                pool.wait_ge(y_saved[q], 16 * PAIRS)

            def results(i, first):
                for q in range(2):
                    for k in range(2):
                        n = i * 4 + q * 2 + k
                        if not first:
                            pool.wait_ge(y_added, n - 3)
                        pool.tensor_copy(pick_now[k][:], row_i[k][:, bass.ds(i * 2 + q, 1)]).then_inc(y_pick_set, 1)
                        pool.wait_ge(y_pick_set, n + 1)
                        pool.sem_inc(pool_paced, 1)
                        pool.indirect_dma_start(out=y_buf[q][k], out_offset=None, in_=dram["y_rows"],
                                                in_offset=bass.IndirectOffsetOnAxis(ap=pick_now[k][:], axis=0))\
                            .then_inc(y_in[q][k], 16)
                    for k in range(2):
                        pool.wait_ge(y_in[q][k], i * 16 + 16)
            peeled(pool, T // 2, results)

        @block.tensor
        def _(pe):
            pe.wait_ge(consts_ready, 6)
            pe.wait_ge(both_ready, 1)
            rank = bank[0][:, 0:T * E].rearrange("p (t e) -> p t e", t=T)
            total = bank[1][:, 0:E]
            pe.matmul(rank, before[:], both, start=True, stop=False)
            for d in range(2, T):
                pe.matmul(rank[:, d:T, :], ones[:], both[:, 0:T - d, :], start=False, stop=False,
                          skip_group_check=True)
            pe.matmul(rank, ones[:], both_led[:, 0:T, :], start=False, stop=True).then_inc(ranked, 1)
            for t in range(T):
                mm = pe.matmul(total, ones[:], both[:, t, :], start=(t == 0), stop=(t == T - 1))
            mm.then_inc(ranked, 1)
            for n in range(2 * T):
                pe.wait_ge(marked, 2 * n + 2)
                mm = pe.matmul(bank[2][:, 0:SLOTS], at_row[n % 2][:], at_slot[n % 2][:],
                               start=(n == 0), stop=(n == 2 * T - 1))
                mm.then_inc(mark_used, 1)

            pe.wait_ge(tokens_ready, 1)

            def back(f):
                return 2 if f >= 2 else (1 if f == 0 else 3)

            def down(i, f):
                u = i * FC + f
                q = f % 2
                pe.wait_ge(a_high_ready, u + 1)
                pe.wait_ge(a_low_ready, u + 1)
                for m in range(TB):
                    cols = slice(m * P, (m + 1) * P)
                    pe.matmul(bank[4 + m][:], a_high[q][:, cols], w_high[:, f, 2, :], start=(f == 0), stop=False)
                    pe.matmul(bank[4 + m][:], a_high[q][:, cols], w_low[:, f, 2, :], start=False, stop=False)
                    mm = pe.matmul(bank[4 + m][:], a_low[q][:, cols], w_high[:, f, 2, :],
                                   start=False, stop=(f == FC - 1))
                mm.then_inc(downed, 1)

            def shared(i, first):
                for f in range(FC):
                    u = i * FC + f
                    q = f % 2
                    if first:
                        pe.wait_ge(w_low_ready, f + 1)
                    if not (first and f < 2):
                        pe.wait_ge(act_ready, u - back(f) + 1)
                    for part in range(2):
                        lhs = lambda w, c: w[:, f, part, c * P:(c + 1) * P]
                        for c in range(KC):
                            xh = x_high[:, c, bass.ds(i * BLK, BLK)]
                            xl = x_low[:, c, bass.ds(i * BLK, BLK)]
                            pe.matmul(bank[2 * q + part][:], lhs(w_high, c), xh, start=(c == 0), stop=False)
                            pe.matmul(bank[2 * q + part][:], lhs(w_high, c), xl, start=False, stop=False)
                            mm = pe.matmul(bank[2 * q + part][:], lhs(w_low, c), xh, start=False, stop=(c == KC - 1))
                    mm.then_inc(gated, 1)
                    if f == 1 and not first:
                        pe.wait_ge(added, TB * i)
                    if f >= 1:
                        down(i, f - 1)
                down(i, FC - 1)
            peeled(pe, BLOCKS, shared)

            def turn(s, q, i):
                pe.wait_ge(gathered[q], i * 16 + 16)
                for c in range(KC):
                    tr = pe.transpose(bank[q][:, c * P:(c + 1) * P], xg[q][:, c * P:(c + 1) * P], ident[:])
                tr.then_inc(e_turned, 1)

            def gate_up(s, q, i):
                pe.wait_ge(xg_t_ready, s + 1)
                pe.wait_ge(e_w_in[q], i * 32 + 32)
                wait_from(pe, e_act_ready, s - 1)
                for c in range(KC):
                    mm = pe.matmul(bank[2 + q][:], xg_t[q][:, c * P:(c + 1) * P], w_gu[q][:, c, :],
                                   start=(c == 0), stop=(c == KC - 1))
                mm.then_inc(e_gated, 1)

            def turn_act(s, q):
                pe.wait_ge(e_act_ready, s + 1)
                wait_from(pe, e_act_t_ready, s - 1)
                for c in range(FE // P):
                    tr = pe.transpose(bank[4 + q][:, c * P:(c + 1) * P], e_act[q][:, c * P:(c + 1) * P], ident[:])
                tr.then_inc(e_act_turned, 1)

            def expert_down(s, q):
                pe.wait_ge(e_act_t_ready, s + 1)
                wait_from(pe, y_ready, s - 1)
                for c in range(FE // P):
                    mm = pe.matmul(bank[6 + q][:], e_act_t[q][:, c * P:(c + 1) * P], w_dn[q][:, c, :],
                                   start=(c == 0), stop=(c == FE // P - 1))
                mm.then_inc(e_downed, 1)

            pe.wait_ge(act_ready, BLOCKS * FC)
            pe.wait_ge(added, BLOCKS * TB)
            turn(0, 0, 0)

            def slots(i, first, last):
                for q in range(2):
                    s = i * 2 + q
                    gate_up(s, q, i)
                    if not (first and q == 0):
                        turn_act(s - 1, 1 - q)
                    if not (last and q == 1):
                        wait_from(pe, xg_t_ready, s)
                        turn(s + 1, 1 - q, i + q)
                    if not (first and q == 0):
                        expert_down(s - 1, 1 - q)
            slots(0, True, False)
            slots(1, False, False)
            with pe.Fori(2, PAIRS - 1) as i:
                slots(i, False, False)
            slots(PAIRS - 1, False, True)
            turn_act(SLOTS - 1, 1)
            expert_down(SLOTS - 1, 1)

        @block.scalar
        def _(act):
            act.wait_ge(exps_in, 2)
            act.activation(ratio[:], ratio[:], ACT.Exp).then_inc(exps_out, 1)
            act.activation(sgate[:], logits[:, :, E], ACT.Exp, scale=-1.0).then_inc(exps_out, 1)
            for f in range(FC):
                act.wait_ge(w_in[f % 2], 16 * (f // 2 + 1))
                act.activation(w_high[:, f, :, :], w_raw[f % 2], ACT.Copy, scale=WS).then_inc(w_high_ready, 1)

            def shared(i, first):
                for f in range(FC):
                    u = i * FC + f
                    q = f % 2
                    act.wait_ge(gated, u + 1)
                    act.activation(silu[q][:], bank[2 * q][:], ACT.Silu, scale=1.0 / WS).then_inc(silu_ready, 1)
                    act.wait_ge(act_ready, u + 1)
                    if not (first and f < 2):
                        act.wait_ge(downed, u - (2 if f >= 2 else (1 if f == 0 else 3)) + 1)
                    act.activation(a_high[q][:], act32[q][:], ACT.Copy).then_inc(a_high_ready, 1)
            peeled(act, BLOCKS, shared)

            def slots(i, first):
                for q in range(2):
                    s = i * 2 + q
                    act.wait_ge(e_turned, s + 1)
                    if not first:
                        act.wait_ge(e_gated, s - 1)
                    act.activation(xg_t[q][:], bank[q][:], ACT.Copy).then_inc(xg_t_ready, 1)
                    act.wait_ge(e_gated, s + 1)
                    if not first:
                        act.wait_ge(e_act_ready, s - 1)
                    act.activation(e_silu[q][:], bank[2 + q][:, 0:FE], ACT.Silu).then_inc(e_silu_ready, 1)
            peeled(act, PAIRS, slots)

        @block.vector
        def _(dve):
            def settle(ins):
                dve_step.settle(dve, ins)

            def wide(a, shape, axis):
                return a.unsqueeze(axis).broadcast_to(shape)

            dve.wait_ge(consts_ready, 6)
            grid = [P, T, E]
            e_row = wide(count_e[:, 0:E], grid, 1)
            settle(dve.tensor_copy(raw[:], logits[:, :, 0:E]))
            for k in range(2):
                settle(dve.tensor_reduce(top[k][:], raw[:], AX.X, ALU.max))
                settle(dve.tensor_tensor(key[:], raw[:], wide(top[k][:], grid, 2), ALU.is_equal))
                settle(dve.scalar_tensor_tensor(hit[k][:], e_row, -float(P), key[:], ALU.add, ALU.mult))
                settle(dve.tensor_reduce(low_key[:], hit[k][:], AX.X, ALU.min))
                settle(dve.tensor_tensor(hit[k][:], hit[k][:], wide(low_key[:], grid, 2), ALU.is_equal))
                if k == 0:
                    settle(dve.scalar_tensor_tensor(raw[:], hit[0][:], -1.0e30, raw[:], ALU.mult, ALU.add))
            dve.tensor_tensor(both, hit[0][:], hit[1][:], ALU.add).then_inc(both_ready, 1)
            dve.tensor_tensor(ratio[:], top[1][:], top[0][:], ALU.subtract).then_inc(exps_in, 2)
            dve.wait_ge(exps_out, 2)
            settle(dve.tensor_scalar(share[1][:], ratio[:], 1.0, None, ALU.add))
            settle(dve.reciprocal(share[0][:], share[1][:]))
            settle(dve.tensor_tensor(share[1][:], ratio[:], share[0][:], ALU.mult))
            settle(dve.tensor_scalar(sgate[:], sgate[:], 1.0, None, ALU.add))
            settle(dve.reciprocal(sgate[:], sgate[:]))
            settle(dve.tensor_scalar(sgate[:], sgate[:], 1.0 / (WS * WS), None, ALU.mult))
            dve.wait_ge(ranked, 2)
            settle(dve.tensor_copy(held[:], bank[1][:, 0:E]))
            square = [P, E, E]
            settle(dve.tensor_scalar(base[:], count_e[:, 0:E], float(P), None, ALU.mult))
            settle(dve.tensor_tensor(cube[:], wide(held[:], square, 2), wide(base[:], square, 1), ALU.is_gt))
            settle(dve.tensor_reduce(tiles[:], cube[:], AX.X, ALU.add))
            settle(dve.tensor_tensor(cube[:], upto[:], wide(tiles[:], square, 1), ALU.mult))
            settle(dve.tensor_reduce(ends[:], cube[:], AX.X, ALU.add))
            settle(dve.tensor_tensor(base[:], ends[:], tiles[:], ALU.subtract))
            settle(dve.tensor_scalar(base[:], base[:], float(P), None, ALU.mult))
            settle(dve.tensor_tensor(place[:], bank[0][:, 0:T * E].rearrange("p (t e) -> p t e", t=T),
                                     wide(base[:], grid, 1), ALU.add))
            slot_grid = [P, SLOTS, E]
            settle(dve.tensor_tensor(past[:], wide(count_e[:, 0:SLOTS], slot_grid, 2), wide(ends[:], slot_grid, 1),
                                     ALU.is_ge))
            settle(dve.tensor_reduce(owner_f[:], past[:], AX.X, ALU.add))
            settle(dve.tensor_scalar(owner[:], owner_f[:], float(E - 1), None, ALU.min))
            for k in range(2):
                settle(dve.tensor_tensor(key[:], hit[k][:], place[:], ALU.mult))
                settle(dve.tensor_reduce(row_f[k][:], key[:], AX.X, ALU.add))
                settle(dve.tensor_copy(row_i[k][:], row_f[k][:]))
                settle(dve.tensor_scalar(in_tile[k][:], row_i[k][:], P - 1, None, ALU.bitwise_and))
                settle(dve.tensor_copy(in_tile_f[k][:], in_tile[k][:]))
                settle(dve.tensor_tensor(slot_f[k][:], row_f[k][:], in_tile_f[k][:], ALU.subtract))
                settle(dve.tensor_scalar(slot_f[k][:], slot_f[k][:], 1.0 / P, None, ALU.mult))
            for n in range(2 * T):
                t, k = divmod(n, 2)
                if n >= 2:
                    dve.wait_ge(mark_used, n - 1)
                dve.tensor_scalar(at_row[k][:], count_e[:], in_tile_f[k][:, t:t + 1], None,
                                  ALU.is_equal).then_inc(marked, 1)
                dve.tensor_scalar(at_slot[k][:], count_e[:, 0:SLOTS], slot_f[k][:, t:t + 1],
                                  node_id[:, t:t + 1], ALU.is_equal, ALU.mult).then_inc(marked, 1)
            dve.wait_ge(mark_used, 2 * T)
            dve.tensor_copy(tokens[:], bank[2][:, 0:SLOTS]).then_inc(tokens_ready, 1)

            for f in range(FC):
                dve.wait_ge(w_high_ready, f + 1)
                dve.scalar_tensor_tensor(w_low[:, f, :, :].rearrange("p a d -> p (a d)"),
                                         w_raw[f % 2].rearrange("p a d -> p (a d)"), WS,
                                         w_high[:, f, :, :].rearrange("p a d -> p (a d)"),
                                         ALU.mult, ALU.subtract).then_inc(w_low_ready, 1)

            def shared(i, first):
                for f in range(FC):
                    u = i * FC + f
                    q = f % 2
                    back = 2 if f >= 2 else (1 if f == 0 else 3)
                    dve.wait_ge(silu_ready, u + 1)
                    if not (first and f < 2):
                        dve.wait_ge(a_high_ready, u - back + 1)
                        dve.wait_ge(a_low_ready, u - back + 1)
                    dve.tensor_tensor(act32[q][:], silu[q][:], bank[2 * q + 1][:], ALU.mult).then_inc(act_ready, 1)
                    dve.wait_ge(a_high_ready, u + 1)
                    dve.tensor_tensor(a_low[q][:], act32[q][:], a_high[q][:], ALU.subtract).then_inc(a_low_ready, 1)
                dve.wait_ge(downed, (i + 1) * FC)
                for m in range(TB):
                    row = x1[:, bass.ds(i * TB + m, 1), :].rearrange("p a d -> p (a d)")
                    dve.scalar_tensor_tensor(row, bank[4 + m][:], sgate[:, bass.ds(i * TB + m, 1)], row,
                                             ALU.mult, ALU.add).then_inc(added, 1)
            peeled(dve, BLOCKS, shared)

            def finish(s, q, i):
                dve.wait_ge(e_act_turned, s + 1)
                wait_from(dve, e_downed, s - 1)
                dve.tensor_copy(e_act_t[q][:], bank[4 + q][:, 0:FE]).then_inc(e_act_t_ready, 1)
                dve.wait_ge(e_downed, s + 1)
                wait_from(dve, y_saved[q], i * 16)
                dve.tensor_copy(y_out[q][:], bank[6 + q][:]).then_inc(y_ready, 1)

            def slots(i, first):
                for q in range(2):
                    s = i * 2 + q
                    dve.wait_ge(e_silu_ready, s + 1)
                    wait_from(dve, e_act_turned, s - 1)
                    dve.tensor_tensor(e_act[q][:], e_silu[q][:], bank[2 + q][:, FE:2 * FE],
                                      ALU.mult).then_inc(e_act_ready, 1)
                    if q == 1:
                        finish(s - 1, 0, i)
                    elif not first:
                        finish(s - 1, 1, i - 1)
            slots(0, True)
            slots(1, False)
            with dve.Fori(2, PAIRS) as i:
                slots(i, False)
            finish(SLOTS - 1, 1, PAIRS - 1)
            dve.wait_ge(added, BLOCKS * TB)

            def results(i, first):
                for q in range(2):
                    t = i * 2 + q
                    row = x1[:, bass.ds(t, 1), :].rearrange("p a d -> p (a d)")
                    for k in range(2):
                        dve.wait_ge(y_in[q][k], i * 16 + 16)
                        if k == 1:
                            dve.wait_ge(y_added, 2 * t + 1)
                        dve.scalar_tensor_tensor(row, y_buf[q][k], share[k][:, bass.ds(t, 1)], row,
                                                 ALU.mult, ALU.add).then_inc(y_added, 1)
            peeled(dve, T // 2, results)


def program(nc, io, out):
    dram = {
        "a_rows": nc.dram_tensor("a_rows", [H, N], F32, kind="Internal").ap(),
        "xn_rows": nc.dram_tensor("xn_rows", [N, D], F32, kind="Internal").ap(),
        "y_rows": nc.dram_tensor("y_rows", [SLOTS * P, D], F32, kind="Internal").ap(),
    }
    with ExitStack() as ctx:
        sb, ps, sem = make_tools(nc, ctx)
        ident = sb("ident", [P, P], F32)
        with ExitStack() as upper:
            usb, _, _ = make_tools(nc, upper)
            keep = {"hidden": usb("hidden", [P, T, H * (DH + 1)], F32)}
            with ExitStack() as inner:
                isb, _, _ = make_tools(nc, inner)
                keep["mask"] = isb("mask", [P, T, N], F16)
                keep["seq"] = isb("seq", [P, T * D], F32)
                for n in ("e_pos", "e_neg", "f_pos", "f_neg", "neg_b", "step_b"):
                    keep[n] = isb(n, [P, H * T], F32)
                attention_operands(nc, io, dram, keep, ident)
                attention_heads(nc, io, dram, keep)
            keep["x1"] = keep["hidden"][:].rearrange("p t c -> p (t c)")[:, 0:T * D].rearrange("p (t d) -> p t d", t=T)
            keep["x_high"] = usb("x_high", [P, KC, N], F16)
            keep["x_low"] = usb("x_low", [P, KC, N], F16)
            keep["logits"] = usb("logits", [P, T, E + 1], F32)
            output_projection(nc, io, dram, keep, ident)
            if STOP_AFTER == 3:
                dump(nc, {"x1": keep["x1"], "x_high": keep["x_high"], "x_low": keep["x_low"], "logits": keep["logits"]})
                return
            feed_forward(nc, io, dram, keep, ident, out)


def dump(nc, tensors):
    with ExitStack() as ctx:
        dsem = ctx.enter_context(nc.semaphore("dsem"))
        block = ctx.enter_context(nc.Block())

        @block.sync
        def _(sp):
            for n, (k, t) in enumerate(tensors.items()):
                shape = list(t[:].shape)
                d = nc.dram_tensor("dbg_" + k, shape, t[:].dtype, kind="ExternalOutput").ap()
                sp.dma_start(d, t[:]).then_inc(dsem, 16)
                sp.wait_ge(dsem, 16 * (n + 1))


def kernel(**inputs):
    import numpy as np
    import concourse.bacc as bacc
    from concourse import mybir as mb
    from concourse.bass_utils import run_bass_kernel_spmd

    def plain(name):
        return np.asarray(inputs[name])

    a1, a2 = plain("L0_gnn_a1"), plain("L0_gnn_a2")
    sides = [plain(f"L0_ffn_shared_w_{n}").reshape(FC, P, KC, P).transpose(0, 3, 2, 1).reshape(FC, P, D)
             for n in ("gate", "up")]
    w_shared = np.stack(sides + [plain("L0_ffn_shared_w_down").T.reshape(FC, P, D)], axis=2)
    laid_out = {
        "x": plain("x"),
        "adj_t": plain("adj").T,
        "w_seq": plain("L0_gnn_W_seq"),
        "w_seq_t": plain("L0_gnn_W_seq").T,
        "w_out": plain("L0_gnn_W_out"),
        "b_out": plain("L0_gnn_b_out")[None, :],
        "w_route": np.concatenate([plain("L0_ffn_gate_w"), plain("L0_ffn_shared_gate_w")], axis=0).T,
        "w_shared": w_shared,
        "w_gate_up": plain("L0_ffn_w_gate_up"),
        "w_down": plain("L0_ffn_w_down"),
        "a_rep": np.stack([np.tile(a1, P // DH), np.tile(a2, P // DH)], axis=1),
    }
    nc = bacc.Bacc("TRN2", target_bir_lowering=False, num_devices=1)
    arrays, io = {}, {}
    for name, a in laid_out.items():
        a = np.ascontiguousarray(a)
        arrays[f"in_{name}"] = a
        io[name] = nc.dram_tensor(f"in_{name}", a.shape, mb.dt.from_np(a.dtype), kind="ExternalInput").ap()
    out = nc.dram_tensor("out_0", (N, D), mb.dt.float32, kind="ExternalOutput").ap()
    program(nc, io, out)
    r = run_bass_kernel_spmd(nc, [arrays], core_ids=[0])
    return r.results[0]["out_0"]
```

```python
from contextlib import ExitStack

import concourse.bass as bass
from concourse import mybir

P = 128
N, D = 2048, 512
H, DH = 16, 32
T = N // P
KC = D // P
GW = 2 * (DH + 1)
G_COLS = 3 * GW
PER_BANK = 3
BANKS = -(-T // PER_BANK)
RING = 4
ALPHA = 0.2
STEP = 1.0e30
GSCALE = 256.0
EPS = 1.0e-5
WS = 256.0
E = 16
FE = 256
FS = 1408
FC = FS // P
SLOTS = 2 * N // P + E
BLK = 256
BLOCKS = N // BLK
TB = BLK // P
PER_BLOCK = 8
SLOT_BLOCKS = SLOTS // PER_BLOCK
MARKS = 6
MARK_FROM = 3
MARK_TO = MARK_FROM - (-2 * T // MARKS)
SUM_FROM = 3
Y_BUFS = 12

F32 = mybir.dt.float32
F16 = mybir.dt.float16
BF16 = mybir.dt.bfloat16
I32 = mybir.dt.int32
U32 = mybir.dt.uint32
ALU = mybir.AluOpType
ACT = mybir.ActivationFunctionType
AX = mybir.AxisListType
RMAX = bass.bass_isa.ReduceOp.max


class Steps:

    def __init__(self, sem):
        self.sem, self.at = sem, 0

    def did(self, ins):
        ins.then_inc(self.sem, 1)
        self.at = self.at + 1
        return self.at

    def settle(self, eng, ins):
        self.did(ins)
        eng.wait_ge(self.sem, self.at)


def peeled(eng, count, body):
    body(0, True)
    with eng.Fori(1, count) as i:
        body(i, False)


def peeled_both(eng, count, body):
    body(0, True, False)
    with eng.Fori(1, count - 1) as i:
        body(i, False, False)
    body(count - 1, False, True)


def wait_from(eng, sem, value):
    if not (isinstance(value, int) and value <= 0):
        eng.wait_ge(sem, value)


def make_tools(nc, ctx):
    def sb(name, shape, dt):
        return ctx.enter_context(nc.sbuf_tensor(name, shape, dt))

    def ps(name, shape, dt):
        return ctx.enter_context(nc.psum_tensor(name, shape, dt))

    def sem(name):
        return ctx.enter_context(nc.semaphore(name))

    return sb, ps, sem


def attention_operands(nc, io, dram, keep, ident):
    with ExitStack() as ctx:
        sb, ps, sem = make_tools(nc, ctx)
        x_all = keep["hidden"][:].rearrange("p t c -> p (t c)")[:, 0:T * D].rearrange("p (t d) -> p t d", t=T)
        w_seq = sb("w_seq", [P, KC, D], F32)
        w_seq_t = sb("w_seq_t", [P, KC, D], F32)
        a_rep = sb("a_rep", [P, 2], F32)
        a_diag = sb("a_diag", [P, KC, 2 * H], F32)
        v_sb = sb("v_sb", [P, KC, 2 * H], F32)
        stats = sb("stats", [P, T, 6], F32)
        mv = sb("mv", [P, T, 2], F32)
        rstd = sb("rstd", [P, T], F32)
        std = sb("std", [P, T], F32)
        xn_stage = [sb(f"xn_stage{q}", [P, D], F32) for q in range(2)]
        xn_t = [sb(f"xn_t{q}", [P, KC, P], F32) for q in range(2)]
        s_t = sb("s_t", [H, N], F32)
        ones = sb("ones", [P, P], F16)
        empty = sb("empty", [P, N], F16)
        b_max = sb("b_max", [P, H], F32)
        b_top = sb("b_top", [P, H], F32)
        z = sb("z", [P, H, T], F32)
        m = sb("m", [P, H, T], F32)
        ea = sb("ea", [P, H, T], F32)
        eb = sb("eb", [P, H, T], F32)
        a_all = sb("a_all", [P, H, T], F32)
        b_all = sb("b_all", [P, H, T], F32)

        p_xt = [ps(f"p_xt{q}", [P, 512], F32) for q in range(2)]
        p_seq = [ps(f"p_seq{q}", [P, 512], F32) for q in range(2)]
        p_s = [ps(f"p_s{q}", [P, 512], F32) for q in range(2)]
        p_w = [ps(f"p_w{q}", [P, 512], F32) for q in range(2)]

        x_in = sem("x_in")
        w_in = sem("w_in")
        wt_in = sem("wt_in")
        a_in = sem("a_in")
        adj_in = [sem(f"adj_in{j}") for j in range(T)]
        diag_ready = sem("diag_ready")
        ones_ready = sem("ones_ready")
        v_made = sem("v_made")
        v_ready = sem("v_ready")
        var_ready = sem("var_ready")
        std_ready = sem("std_ready")
        normed = sem("normed")
        turned = sem("turned")
        xn_t_ready = sem("xn_t_ready")
        projected = sem("projected")
        seq_saved = sem("seq_saved")
        scores_saved = sem("scores_saved")
        rows_saved = sem("rows_saved")
        max_local = sem("max_local")
        max_all = sem("max_all")
        counted = sem("counted")
        dve_step = Steps(sem("dve_step"))
        pool_step = Steps(sem("pool_step"))
        act_step = Steps(sem("act_step"))
        factors_in = sem("factors_in")
        rows_out = sem("rows_out")
        degree_read = sem("degree_read")
        block = ctx.enter_context(nc.Block())

        @block.sync
        def _(sp):
            sp.dma_start(w_seq_t[:], io["w_seq_t"].rearrange("(c p) k -> p c k", p=P)).then_inc(wt_in, 16)
            sp.dma_start(a_rep[:], io["a_rep"]).then_inc(a_in, 16)
            xv = io["x"].rearrange("(t p) d -> p t d", p=P)
            sp.dma_start(x_all[:, 0:T // 2, :], xv[:, 0:T // 2, :]).then_inc(x_in, 16)
            sp.wait_ge(x_in, 16)
            sp.dma_start(x_all[:, T // 2:T, :], xv[:, T // 2:T, :]).then_inc(x_in, 16)
            sp.dma_start(w_seq[:], io["w_seq"].rearrange("(c p) k -> p c k", p=P)).then_inc(w_in, 16)
            sp.wait_ge(rows_saved, T)
            sp.dma_start(dram["a_rows"], s_t[:]).then_inc(rows_out, 16)
            sp.wait_ge(rows_out, 16)

        @block.gpsimd
        def _(pool):
            for j in range(T):
                pool.dma_start(keep["mask"][:, j, :], io["adj_t"][j * P:(j + 1) * P, :]).then_inc(adj_in[j], 16)
            pool_step.settle(pool, pool.memset(ident[:], 0.0))
            pool_step.settle(pool, pool.affine_select(out=ident[:], in_=ident[:], compare_op=ALU.not_equal,
                                                      fill=1.0, base=0, pattern=[[-1, P]], channel_multiplier=1))
            pool_step.did(pool.tensor_copy(keep["ident16"][:], ident[:]))
            pool.memset(ones[:], 1.0).then_inc(ones_ready, 1)
            pool_step.settle(pool, pool.memset(a_diag[:], 1.0))
            pool.wait_ge(a_in, 16)
            for w in range(2):
                half = a_diag[:, :, w * H:(w + 1) * H]
                pool_step.settle(pool, pool.tensor_scalar(half, half, a_rep[:, w:w + 1], None, ALU.mult))
                pool_step.settle(pool, pool.affine_select(
                    out=half, in_=half, compare_op=ALU.is_ge, fill=0.0, base=0,
                    pattern=[[P, KC], [-DH, H]], channel_multiplier=1))
                last = pool.affine_select(
                    out=half, in_=half, compare_op=ALU.is_ge, fill=0.0, base=DH - 1,
                    pattern=[[-P, KC], [DH, H]], channel_multiplier=-1)
                last.then_inc(diag_ready, 1)
            pool.wait_ge(max_local, 1)
            pool.partition_all_reduce(b_top[:], b_max[:], P, RMAX).then_inc(max_all, 1)

        @block.tensor
        def _(pe):
            pe.wait_ge(wt_in, 16)
            pe.wait_ge(diag_ready, 2)
            for k in range(KC):
                if k >= 2:
                    pe.wait_ge(v_ready, k - 1)
                for c in range(KC):
                    mm = pe.matmul(p_s[k % 2][:, 0:2 * H], w_seq_t[:, c, k * P:(k + 1) * P], a_diag[:, c, :],
                                   start=(c == 0), stop=(c == KC - 1))
                mm.then_inc(v_made, 1)
            pe.wait_ge(v_ready, KC)
            pe.wait_ge(w_in, 16)

            def tile_pair(i, first):
                for q in range(2):
                    t = i * 2 + q
                    pe.wait_ge(normed, t + 1)
                    if not first:
                        pe.wait_ge(xn_t_ready, t - 1)
                    for c in range(KC):
                        tr = pe.transpose(p_xt[q][:, c * P:(c + 1) * P],
                                          xn_stage[q][:, c * P:(c + 1) * P], ident[:])
                    tr.then_inc(turned, 1)
                for q in range(2):
                    t = i * 2 + q
                    pe.wait_ge(xn_t_ready, t + 1)
                    if not first:
                        pe.wait_ge(seq_saved, t - 1)
                        pe.wait_ge(scores_saved, t - 1)
                        pe.wait_ge(rows_saved, t - 1)
                    for c in range(KC):
                        pe.matmul(p_seq[q][:], xn_t[q][:, c, :], w_seq[:, c, :], start=(c == 0), stop=(c == KC - 1))
                    for c in range(KC):
                        pe.matmul(p_s[q][:, 0:2 * H], xn_t[q][:, c, :], v_sb[:, c, :],
                                  start=(c == 0), stop=(c == KC - 1))
                    for c in range(KC):
                        mm = pe.matmul(p_s[q][0:H, 128:256], v_sb[:, c, 0:H], xn_t[q][:, c, :],
                                       start=(c == 0), stop=(c == KC - 1))
                    mm.then_inc(projected, 1)

            peeled(pe, T // 2, tile_pair)

            pe.wait_ge(ones_ready, 1)
            for b in range(4):
                if b >= 2:
                    pe.wait_ge(degree_read, b - 1)
                for j in range(T):
                    if b == 0:
                        pe.wait_ge(adj_in[j], 16)
                    mm = pe.matmul(p_w[b % 2][:], ones[:], keep["mask"][:, j, b * 512:(b + 1) * 512],
                                   start=(j == 0), stop=(j == T - 1))
                mm.then_inc(counted, 1)

        @block.scalar
        def _(act):
            for k in range(KC):
                act.wait_ge(v_made, k + 1)
                act.activation(v_sb[:, k, :], p_s[k % 2][:, 0:2 * H], ACT.Copy).then_inc(v_ready, 1)
            act.wait_ge(var_ready, 1)
            act.activation(std[:], rstd[:], ACT.Sqrt).then_inc(std_ready, 1)

            def tile_pair(i, first):
                for q in range(2):
                    t = i * 2 + q
                    act.wait_ge(turned, t + 1)
                    if not first:
                        act.wait_ge(projected, t - 1)
                    act.activation(xn_t[q][:].rearrange("p c m -> p (c m)"), p_xt[q][:],
                                   ACT.Copy).then_inc(xn_t_ready, 1)
                for q in range(2):
                    t = i * 2 + q
                    act.wait_ge(projected, t + 1)
                    act.activation(s_t[:, bass.ds(t * P, P)], p_s[q][0:H, 128:256], ACT.Copy).then_inc(rows_saved, 1)
                    act.activation(keep["seq"][:, bass.ds(t * D, D)], p_seq[q][:], ACT.Copy).then_inc(seq_saved, 1)

            peeled(act, T // 2, tile_pair)
            act.wait_ge(factors_in, 1)
            act_step.did(act.activation(keep["e_pos"][:], ea[:], ACT.Exp))
            act_step.did(act.activation(keep["e_neg"][:], eb[:], ACT.Exp))
            act_step.did(act.activation(keep["f_pos"][:], z[:], ACT.Exp))
            act_step.did(act.activation(keep["f_neg"][:], m[:], ACT.Exp))
            act.wait_ge(act_step.sem, act_step.at)

        @block.vector
        def _(dve):
            dve.wait_ge(x_in, 32)
            for t in range(T):
                last = dve.bn_stats(stats[:, t, :], x_all[:, t, :])
            dve_step.settle(dve, last)
            for t in range(T):
                last = dve.bn_aggr(mv[:, t, :], stats[:, t, :])
            dve_step.settle(dve, last)
            dve.tensor_scalar(rstd[:], mv[:, :, 1], EPS, None, ALU.add).then_inc(var_ready, 1)
            dve.wait_ge(std_ready, 1)
            dve_step.settle(dve, dve.reciprocal(rstd[:], std[:]))
            base = dve_step.at

            def tile_pair(i, first):
                for q in range(2):
                    t = i * 2 + q
                    if not first:
                        dve.wait_ge(turned, t - 1)
                    dve.tensor_scalar(xn_stage[q][:], x_all[:, bass.ds(t, 1), :].rearrange("p a d -> p (a d)"),
                                      mv[:, bass.ds(t, 1), 0], rstd[:, bass.ds(t, 1)],
                                      ALU.subtract, ALU.mult).then_inc(normed, 1)
                for q in range(2):
                    t = i * 2 + q
                    dve.wait_ge(projected, t + 1)
                    dve.wait_ge(rows_saved, t + 1)
                    dve.tensor_copy(a_all[:, :, bass.ds(t, 1)].rearrange("p h a -> p (h a)"), p_s[q][:, 0:H])
                    dve.tensor_copy(b_all[:, :, bass.ds(t, 1)].rearrange("p h a -> p (h a)"),
                                    p_s[q][:, H:2 * H]).then_inc(scores_saved, 1)

            peeled(dve, T // 2, tile_pair)
            dve.wait_ge(scores_saved, T)
            dve.tensor_reduce(b_max[:], b_all[:], AX.X, ALU.max).then_inc(max_local, 1)
            dve.tensor_scalar(keep["neg_b"][:], b_all[:], -1.0, None, ALU.mult)
            dve_step.did(dve.tensor_scalar(keep["step_b"][:], b_all[:], STEP, None, ALU.mult))
            dve.wait_ge(max_all, 1)
            top = b_top[:].unsqueeze(2).broadcast_to([P, H, T])
            dve_step.settle(dve, dve.tensor_tensor(z[:], a_all[:], top, ALU.add))
            dve_step.settle(dve, dve.tensor_tensor(ea[:], b_all[:], top, ALU.subtract))
            dve_step.settle(dve, dve.tensor_scalar(eb[:], ea[:], ALPHA, None, ALU.mult))
            dve_step.settle(dve, dve.scalar_tensor_tensor(m[:], z[:], ALPHA, z[:], ALU.mult, ALU.max))
            dve_step.settle(dve, dve.scalar_tensor_tensor(b_all[:], z[:], ALPHA, m[:], ALU.mult, ALU.subtract))
            dve_step.settle(dve, dve.tensor_tensor(z[:], z[:], m[:], ALU.subtract))
            dve.tensor_copy(m[:], b_all[:]).then_inc(factors_in, 1)
            for b in range(4):
                dve.wait_ge(counted, b + 1)
                last = dve.tensor_scalar(empty[:, b * 512:(b + 1) * 512], p_w[b % 2][:], 0.0, None, ALU.is_equal)
                last.then_inc(degree_read, 1)
            dve.wait_ge(degree_read, 4)
            for j in range(T):
                last = dve.tensor_tensor(keep["mask"][:, j, :], keep["mask"][:, j, :], empty[:], ALU.max)
            dve_step.settle(dve, last)


def attention_heads(nc, io, dram, keep):
    with ExitStack() as ctx:
        sb, ps, sem = make_tools(nc, ctx)
        SOFT = [j for j in range(T) if j % 4 != 1]
        a_row = [sb(f"a_row{q}", [P, N], F32) for q in range(2)]
        pick = [sb(f"pick{r}", [P, N], F16) for r in range(RING)]
        over = [sb(f"over{r}", [P, N], BF16) for r in range(2)]
        g32 = sb("g32", [P, T, GW], F32)
        g = [sb(f"g{q}", [P, T, G_COLS], F16) for q in range(2)]
        sums = sb("sums", [P, T, 2 * GW], F32)
        acc = ps("acc", [P, BANKS, 512], F32)

        rows_in = [sem(f"rows_in{q}") for q in range(2)]
        weighted = sem("weighted")
        high_ready = sem("high_ready")
        low_ready = sem("low_ready")
        g_ready = sem("g_ready")
        over_ready = sem("over_ready")
        over_used = sem("over_used")
        pick_used = sem("pick_used")
        head_summed = sem("head_summed")
        bank_read = sem("bank_read")
        combined = sem("combined")
        hard_used = sem("hard_used")
        folded = sem("folded")
        block = ctx.enter_context(nc.Block())
        S = len(SOFT)
        HARD = [j for j in range(T) if j not in SOFT]
        mask, seq = keep["mask"], keep["seq"]

        @block.gpsimd
        def _(pool):
            def heads(i, first):
                for q in range(2):
                    h = i * 2 + q
                    if not first:
                        pool.wait_ge(over_ready, (h - 1) * S)
                        pool.wait_ge(hard_used, (h - 1) * (T - S))
                    pool.dma_start(a_row[q][:], dram["a_rows"][bass.ds(h, 1), :].broadcast_to([P, N]))\
                        .then_inc(rows_in[q], 16)
            peeled(pool, H // 2, heads)

        @block.scalar
        def _(act):
            def high_part(h, q):
                act.wait_ge(weighted, (h + 1) * 4)
                act.activation(g[q][:, :, 0:GW], g32[:], ACT.Copy).then_inc(high_ready, 1)

            def turned_part(h, q):
                act.wait_ge(low_ready, h + 1)
                act.activation(g[q][:, :, 2 * GW:3 * GW].rearrange("p t (s c) -> p t s c", s=2),
                               g[q][:, :, 0:2 * GW].rearrange("p t (s c) -> p t s c", s=2)[:, :, :, DH + 1:GW],
                               ACT.Copy, scale=-1.0).then_inc(g_ready, 1)

            def drain_banks(h):
                act.wait_ge(head_summed, h + 1)
                for b in range(BANKS):
                    n = min(PER_BANK, T - b * PER_BANK)
                    act.activation(sums[:, b * PER_BANK:b * PER_BANK + n, :].rearrange("p t c -> p (t c)"),
                                   acc[:, b, 0:n * 2 * GW], ACT.Copy).then_inc(bank_read, 1)

            high_part(0, 0)
            turned_part(0, 0)

            def heads(i, first, last):
                for q in range(2):
                    h = i * 2 + q
                    act.wait_ge(rows_in[q], (i + 1) * 16)
                    for n, j in enumerate(SOFT):
                        if not (first and q == 0 and n < 2):
                            act.wait_ge(over_used, h * S + n - 1)
                        act.activation(over[n % 2][:], a_row[q][:], ACT.Relu, scale=STEP,
                                       bias=keep["step_b"][:, bass.ds(h * T + j, 1)]).then_inc(over_ready, 1)
                        if n == 2 and not (first and q == 0):
                            if not (first and q == 1):
                                act.wait_ge(combined, h - 1)
                            drain_banks(h - 1)
                        if n == 4 and not (last and q == 1):
                            high_part(h + 1, 1 - q)
                        if n == 6 and not (last and q == 1):
                            turned_part(h + 1, 1 - q)

            peeled_both(act, H // 2, heads)
            act.wait_ge(combined, H - 1)
            drain_banks(H - 1)

        @block.vector
        def _(dve):
            def operand(h, first):
                if not first:
                    dve.wait_ge(low_ready, h)
                for s, e in enumerate(("e_pos", "e_neg")):
                    w = keep[e][:, bass.ds(h * T, T)]
                    lo = s * (DH + 1)
                    dve.scalar_tensor_tensor(
                        g32[:, :, lo:lo + DH], seq[:].rearrange("p (t d) -> p t d", t=T)[:, :, bass.ds(h * DH, DH)],
                        GSCALE, w.unsqueeze(2).broadcast_to([P, T, DH]), ALU.mult, ALU.mult).then_inc(weighted, 1)
                    dve.tensor_scalar(g32[:, :, lo + DH], w, GSCALE, None, ALU.mult).then_inc(weighted, 1)

            def low_part(h, q):
                dve.wait_ge(high_ready, h + 1)
                dve.tensor_tensor(g[q][:, :, GW:2 * GW], g32[:], g[q][:, :, 0:GW], ALU.subtract).then_inc(low_ready, 1)

            def combine(h):
                dve.wait_ge(bank_read, (h + 1) * BANKS)
                halves = sums[:, :, 0:GW]
                dve.tensor_tensor(halves, halves, sums[:, :, GW:2 * GW], ALU.add).then_inc(folded, 1)
                dve.wait_ge(folded, h * 3 + 1)
                for s, f in enumerate(("f_pos", "f_neg")):
                    part = sums[:, :, s * (DH + 1):(s + 1) * (DH + 1)]
                    w = keep[f][:, bass.ds(h * T, T)]
                    dve.tensor_tensor(part, part, w.unsqueeze(2).broadcast_to([P, T, DH + 1]),
                                      ALU.mult).then_inc(folded, 1)
                dve.wait_ge(folded, h * 3 + 3)
                dve.tensor_tensor(keep["hidden"][:, :, bass.ds(h * (DH + 1), DH + 1)],
                                  sums[:, :, 0:DH + 1], sums[:, :, DH + 1:GW], ALU.subtract).then_inc(combined, 1)

            operand(0, True)
            low_part(0, 0)

            def heads(i, first, last):
                for q in range(2):
                    h = i * 2 + q
                    dve.wait_ge(rows_in[q], (i + 1) * 16)
                    n = 0
                    for j in range(T):
                        slot = (q * T + j) % RING
                        if not (first and q * T + j < RING):
                            dve.wait_ge(pick_used, h * T + j - RING + 1)
                        if j in SOFT:
                            dve.wait_ge(over_ready, h * S + n + 1)
                            op = dve.tensor_tensor(pick[slot][:], over[n % 2][:], mask[:, j, :], ALU.min)
                            op.then_inc(over_used, 1)
                            n += 1
                        else:
                            op = dve.scalar_tensor_tensor(pick[slot][:], a_row[q][:],
                                                          keep["neg_b"][:, bass.ds(h * T + j, 1)], mask[:, j, :],
                                                          ALU.is_gt, ALU.mult)
                            op.then_inc(hard_used, 1)
                        if j == 3 and not (last and q == 1):
                            operand(h + 1, False)
                        if j == 7 and not (last and q == 1):
                            low_part(h + 1, 1 - q)
                        if j == 12 and not (first and q == 0):
                            combine(h - 1)
            peeled_both(dve, H // 2, heads)
            combine(H - 1)

        @block.tensor
        def _(pe):
            def heads(i, first):
                for q in range(2):
                    h = i * 2 + q
                    pe.wait_ge(g_ready, h + 1)
                    for j in range(T):
                        slot = (q * T + j) % RING
                        if j in SOFT:
                            pe.wait_ge(over_used, h * S + SOFT.index(j) + 1)
                        else:
                            pe.wait_ge(hard_used, h * (T - S) + HARD.index(j) + 1)
                        for t in range(T):
                            b, r = divmod(t, PER_BANK)
                            if j == 0 and r == 0 and not (first and q == 0):
                                pe.wait_ge(bank_read, (h - 1) * BANKS + b + 1)
                            out = acc[:, b, r * 2 * GW:(r + 1) * 2 * GW]
                            mm = pe.matmul(out, pick[slot][:, t * P:(t + 1) * P], g[q][:, j, 0:2 * GW],
                                           start=(j == 0 and r == 0), stop=False, skip_group_check=True)
                            if t == T - 1:
                                mm.then_inc(pick_used, 1)
                            mm = pe.matmul(out.rearrange("p (s c) -> p s c", s=2)[:, :, DH + 1:GW],
                                           mask[:, j, t * P:(t + 1) * P],
                                           g[q][:, j, 2 * GW:3 * GW].rearrange("p (s c) -> p s c", s=2),
                                           start=False, stop=(j == T - 1), skip_group_check=True)
                    mm.then_inc(head_summed, 1)
            peeled(pe, H // 2, heads)


def output_projection(nc, io, dram, keep, ident):
    with ExitStack() as ctx:
        sb, ps, sem = make_tools(nc, ctx)
        hidden, x1, x_parts = keep["hidden"], keep["x1"], keep["x_parts"]
        rden = sb("rden", [P, T, H], F32)
        w_out = sb("w_out", [P, KC * D], F32)
        w_route = sb("w_route", [P, KC, E + 1], F32)
        wo = [sb(f"wo{r}", [P, KC, D], F16) for r in range(2)]
        wr = [sb(f"wr{r}", [P, KC, E + 1], F16) for r in range(2)]
        b_out = sb("b_out", [P, D], F32)
        heads = [sb(f"heads{q}", [P, D], F32) for q in range(2)]
        parts = [sb(f"parts{q}", [P, 2, D], F16) for q in range(2)]
        parts_t = [sb(f"parts_t{q}", [P, 2, KC, P], F16) for q in range(2)]
        x_in_tile = [sb(f"x_in_tile{q}", [P, D], F32) for q in range(2)]
        y = [sb(f"y{q}", [P, D], F32) for q in range(2)]
        below = [sb(f"below{q}", [P, D], F32) for q in range(2)]
        stats = sb("stats2", [P, T, 6], F32)
        mv = sb("mv2", [P, T, 2], F32)
        var = sb("var2", [P, T], F32)
        std = sb("std2", [P, T], F32)
        rstd = sb("rstd2", [P, T], F32)
        p_t = [ps(f"p_t{q}", [P, 2 * D], F16) for q in range(2)]
        p_y = [ps(f"p_y{q}", [P, 512], F32) for q in range(2)]
        p_l = [ps(f"p_l{q}", [P, 512], F32) for q in range(2)]

        w_in, b_in, r_in = sem("w_out_in"), sem("b_out_in"), sem("w_route_in")
        x_in = [sem(f"x_in_tile{q}") for q in range(2)]
        paced = sem("paced3")
        wo_high, wo_low = sem("wo_high"), sem("wo_low")
        rden_ready = sem("rden_ready")
        scaled, high_ready, low_ready = sem("head_scaled"), sem("head_high"), sem("head_low")
        head_turned, parts_t_ready = sem("head_turned"), sem("parts_t_ready")
        projected, biased = sem("out_projected"), sem("biased")
        negated, below_ready, above_added = sem("negated"), sem("below_ready"), sem("above_added")
        x1_ready, stats_ready = sem("x1_ready"), sem("stats_ready")
        var_ready, std_ready, rstd_ready = sem("var2_ready"), sem("std2_ready"), sem("rstd2_ready")
        normed, x_high, x_low = sem("normed2"), sem("x_high_made"), sem("x_low_made")
        rows_saved = [sem(f"xn_saved{q}") for q in range(2)]
        turned, x_parts_ready = sem("turned2"), sem("x_parts_ready")
        routed, logits_saved = sem("routed"), sem("logits_saved")
        block = ctx.enter_context(nc.Block())

        def flat(a):
            return a.rearrange("p a d -> p (a d)")

        def tile(a, t):
            return flat(a[:, bass.ds(t, 1), :])

        @block.sync
        def _(sp):
            sp.dma_start(w_out[:].rearrange("p (c k) -> p c k", c=KC),
                         io["w_out"].rearrange("(c p) k -> p c k", p=P)).then_inc(w_in, 16)
            sp.dma_start(b_out[:], io["b_out"].broadcast_to([P, D])).then_inc(b_in, 16)
            for q in range(2):
                sp.dma_start(x_in_tile[q][:], io["x"][q * P:(q + 1) * P, :]).then_inc(x_in[q], 16)
            sp.dma_start(w_route[:], io["w_route"].rearrange("(c p) e -> p c e", p=P)).then_inc(r_in, 16)
            with sp.Fori(1, T // 2) as i:
                for q in range(2):
                    t = i * 2 + q
                    sp.wait_ge(above_added, t - 1)
                    sp.sem_inc(paced, 1)
                    sp.dma_start(x_in_tile[q][:], io["x"][bass.ds(t * P, P), :]).then_inc(x_in[q], 16)

        @block.gpsimd
        def _(pool):
            def rows(i, first):
                for q in range(2):
                    t = i * 2 + q
                    pool.wait_ge(x_high, t + 1)
                    pool.wait_ge(x_low, t + 1)
                    pool.dma_start(dram["xn_rows"][bass.ds(t * P, P), :], flat(parts[q][:])).then_inc(rows_saved[q], 16)
            peeled(pool, T // 2, rows)
            for q in range(2):
                pool.wait_ge(rows_saved[q], 16 * (T // 2))

        @block.tensor
        def _(pe):
            def turn(t, q, high, low, copied, done):
                pe.wait_ge(high, t + 1)
                pe.wait_ge(low, t + 1)
                wait_from(pe, copied, t - 1)
                for r in range(2):
                    for c in range(KC):
                        tr = pe.transpose(p_t[q][:, (r * KC + c) * P:(r * KC + c + 1) * P],
                                          parts[q][:, r, c * P:(c + 1) * P], keep["ident16"][:])
                tr.then_inc(done, 1)

            turn(0, 0, high_ready, low_ready, parts_t_ready, head_turned)
            pe.wait_ge(wo_low, 1)

            def project(i, first, last):
                for q in range(2):
                    t = i * 2 + q
                    if not (last and q == 1):
                        turn(t + 1, 1 - q, high_ready, low_ready, parts_t_ready, head_turned)
                    pe.wait_ge(parts_t_ready, t + 1)
                    wait_from(pe, biased, t - 1)
                    n = 0
                    for c in range(KC):
                        for a, b in ((0, 0), (0, 1), (1, 0)):
                            mm = pe.matmul(p_y[q][:], parts_t[q][:, a, c, :], wo[b][:, c, :],
                                           start=(n == 0), stop=(n == 3 * KC - 1))
                            n += 1
                    mm.then_inc(projected, 1)
            peeled_both(pe, T // 2, project)

            turn(0, 0, x_high, x_low, x_parts_ready, turned)

            def route(i, first, last):
                for q in range(2):
                    t = i * 2 + q
                    if not (last and q == 1):
                        turn(t + 1, 1 - q, x_high, x_low, x_parts_ready, turned)
                    pe.wait_ge(x_parts_ready, t + 1)
                    wait_from(pe, logits_saved, t - 1)
                    n = 0
                    for c in range(KC):
                        for a, b in ((0, 0), (0, 1), (1, 0)):
                            mm = pe.matmul(p_l[q][:, 0:E + 1], x_parts[:, a, c, bass.ds(t * P, P)], wr[b][:, c, :],
                                           start=(n == 0), stop=(n == 3 * KC - 1))
                            n += 1
                    mm.then_inc(routed, 1)
            peeled_both(pe, T // 2, route)

        @block.scalar
        def _(act):
            def high(t, q, ready, made):
                act.wait_ge(ready, t + 1)
                act.activation(parts[q][:, 0, :], heads[q][:], ACT.Copy).then_inc(made, 1)

            act.wait_ge(w_in, 16)
            act.activation(flat(wo[0][:]), w_out[:], ACT.Copy, scale=WS).then_inc(wo_high, 1)
            act.wait_ge(r_in, 16)
            act.activation(wr[0][:], w_route[:], ACT.Copy, scale=WS).then_inc(wo_high, 1)

            def copy_turned(t, q):
                act.wait_ge(head_turned, t + 1)
                wait_from(act, projected, t - 1)
                act.activation(parts_t[q][:].rearrange("p r c m -> p (r c m)"), p_t[q][:], ACT.Copy)\
                   .then_inc(parts_t_ready, 1)

            high(0, 0, scaled, high_ready)
            copy_turned(0, 0)

            def project(i, first, last):
                for q in range(2):
                    t = i * 2 + q
                    if not (last and q == 1):
                        wait_from(act, head_turned, t)
                        high(t + 1, 1 - q, scaled, high_ready)
                        copy_turned(t + 1, 1 - q)
                    act.wait_ge(biased, t + 1)
                    wait_from(act, x1_ready, t - 1)
                    act.activation(below[q][:], y[q][:], ACT.Relu, scale=-1.0).then_inc(negated, 1)
                    act.wait_ge(negated, t + 1)
                    act.activation(below[q][:], below[q][:], ACT.Exp, scale=-1.0).then_inc(below_ready, 1)
            peeled_both(act, T // 2, project)
            act.wait_ge(var_ready, 1)
            act.activation(std[:], var[:], ACT.Sqrt).then_inc(std_ready, 1)

            def spread(t, q):
                act.wait_ge(turned, t + 1)
                act.activation(x_parts[:, :, :, bass.ds(t * P, P)].rearrange("p r c m -> p (r c) m"),
                               p_t[q][:].rearrange("p (g m) -> p g m", m=P), ACT.Copy).then_inc(x_parts_ready, 1)

            def route(i, first, last):
                for q in range(2):
                    t = i * 2 + q
                    if not first:
                        act.wait_ge(rows_saved[q], i * 16)
                    high(t, q, normed, x_high)
                    spread(t, q)
            peeled_both(act, T // 2, route)

        @block.vector
        def _(dve):
            dens = hidden[:].rearrange("p t (h c) -> p t h c", h=H)[:, :, :, DH]
            dve.reciprocal(rden[:], dens).then_inc(rden_ready, 1)
            dve.wait_ge(rden_ready, 1)

            def low(t, q, made_high, made):
                dve.wait_ge(made_high, t + 1)
                dve.tensor_tensor(parts[q][:, 1, :], heads[q][:], parts[q][:, 0, :], ALU.subtract).then_inc(made, 1)

            def scale(t, q):
                wait_from(dve, low_ready, t - 1)
                dve.tensor_tensor(
                    heads[q][:].rearrange("p (h d) -> p h d", h=H),
                    hidden[:, bass.ds(t, 1), :].rearrange("p a (h c) -> p (a h) c", h=H)[:, :, 0:DH],
                    tile(rden, t).unsqueeze(2).broadcast_to([P, H, DH]), ALU.mult).then_inc(scaled, 1)

            scale(0, 0)
            low(0, 0, high_ready, low_ready)
            for n, (hi, lo, raw) in enumerate(((wo[0], wo[1], w_out[:].rearrange("p (c k) -> p c k", c=KC)),
                                               (wr[0], wr[1], w_route[:]))):
                dve.wait_ge(wo_high, n + 1)
                dve.scalar_tensor_tensor(lo[:], raw, WS, hi[:], ALU.mult, ALU.subtract).then_inc(wo_low, 1)
            dve.wait_ge(b_in, 16)

            def finish(t, q):
                row = tile(x1, t)
                dve.wait_ge(below_ready, t + 1)
                dve.wait_ge(above_added, t + 1)
                dve.scalar_tensor_tensor(row, below[q][:], -1.0, row, ALU.add, ALU.add).then_inc(x1_ready, 1)
                dve.wait_ge(x1_ready, t + 1)
                dve.bn_stats(tile(stats, t), row).then_inc(stats_ready, 1)

            def project(i, first, last):
                for q in range(2):
                    t = i * 2 + q
                    if not (last and q == 1):
                        scale(t + 1, 1 - q)
                        low(t + 1, 1 - q, high_ready, low_ready)
                    dve.wait_ge(projected, t + 1)
                    wait_from(dve, above_added, t - 1)
                    wait_from(dve, negated, t - 1)
                    dve.scalar_tensor_tensor(y[q][:], p_y[q][:], 1.0 / WS, b_out[:], ALU.mult, ALU.add)\
                       .then_inc(biased, 1)
                    dve.wait_ge(biased, t + 1)
                    dve.wait_ge(x_in[q], i * 16 + 16)
                    dve.scalar_tensor_tensor(tile(x1, t), y[q][:], 0.0, x_in_tile[q][:], ALU.max, ALU.add)\
                       .then_inc(above_added, 1)
                    if not (first and q == 0):
                        finish(t - 1, 1 - q)
            peeled_both(dve, T // 2, project)
            finish(T - 1, 1)
            dve.wait_ge(stats_ready, T)
            for t in range(T):
                last = dve.bn_aggr(mv[:, t, :], stats[:, t, :])
            last.then_inc(stats_ready, 1)
            dve.wait_ge(stats_ready, T + 1)
            dve.tensor_scalar(var[:], mv[:, :, 1], EPS, None, ALU.add).then_inc(var_ready, 1)
            dve.wait_ge(std_ready, 1)
            dve.reciprocal(rstd[:], std[:]).then_inc(rstd_ready, 1)
            dve.wait_ge(rstd_ready, 1)

            def norm(t, q):
                wait_from(dve, x_low, t - 1)
                dve.tensor_scalar(heads[q][:], tile(x1, t), mv[:, bass.ds(t, 1), 0], rstd[:, bass.ds(t, 1)],
                                  ALU.subtract, ALU.mult).then_inc(normed, 1)

            def save_logits(t, q):
                dve.wait_ge(routed, t + 1)
                dve.tensor_scalar(tile(keep["logits"], t), p_l[q][:, 0:E + 1], 1.0 / WS, None, ALU.mult)\
                   .then_inc(logits_saved, 1)

            norm(0, 0)

            def route(i, first, last):
                for q in range(2):
                    t = i * 2 + q
                    if not (last and q == 1):
                        norm(t + 1, 1 - q)
                    low(t, q, x_high, x_low)
                    if not (first and q == 0):
                        save_logits(t - 1, 1 - q)
            peeled_both(dve, T // 2, route)
            save_logits(T - 1, 1)


def feed_forward(nc, io, dram, keep, ident, out):
    with ExitStack() as ctx:
        sb, ps, sem = make_tools(nc, ctx)
        x1, x_parts, logits = keep["x1"], keep["x_parts"], keep["logits"]
        ident16 = keep["ident16"]

        count_e = sb("count_e", [P, P], F32)
        node_id = sb("node_id", [P, T], F32)
        before = sb("before", [P, P], F16)
        ones = sb("ones2", [P, P], F16)
        upto = sb("upto", [P, E, E], F32)
        raw = sb("raw", [P, T, E], F32)
        key = sb("key", [P, T, E], F32)
        hit = [sb(f"hit{k}", [P, T, E], F32) for k in range(2)]
        top = [sb(f"top{k}", [P, T], F32) for k in range(2)]
        low_key = sb("low_key", [P, T], F32)
        both_led = sb("both_led", [P, T + 1, E], F16)
        both = both_led[:, 1:T + 1, :]
        ratio = sb("ratio", [P, T], F32)
        share = [sb(f"share{k}", [P, T], F32) for k in range(2)]
        sgate = sb("sgate", [P, T], F32)
        held = sb("held", [P, E], F32)
        cube, place = raw, key
        tiles = sb("tiles", [P, E], F32)
        ends = sb("ends", [P, E], F32)
        base = sb("base", [P, E], F32)
        owner_f = sb("owner_f", [P, SLOTS], F32)
        owner = sb("owner", [P, SLOTS], I32)
        row_f = [sb(f"row_f{k}", [P, T], F32) for k in range(2)]
        row_i = [sb(f"row_i{k}", [P, T], I32) for k in range(2)]
        in_tile = [sb(f"in_tile{k}", [P, T], I32) for k in range(2)]
        in_tile_f = [sb(f"in_tile_f{k}", [P, T], F32) for k in range(2)]
        slot_f = [sb(f"slot_f{k}", [P, T], F32) for k in range(2)]
        at_row = [sb(f"at_row{m}", [P, P], F16) for m in range(MARKS)]
        at_slot = [sb(f"at_slot{m}", [P, SLOTS], F16) for m in range(MARKS)]
        tokens = sb("tokens", [P, SLOTS], I32)

        w_raw = [sb(f"w_raw{q}", [P, 6 * D], F32) for q in range(2)]
        gu_raw = [w[:, 0:KC * D].rearrange("p (c f) -> p c f", c=KC) for w in w_raw]
        dn_raw = [w[:, KC * D:6 * D].rearrange("p (c f) -> p c f", c=FE // P) for w in w_raw]
        s_raw = [w_raw[r // 2][:, (r % 2) * 3 * D:(r % 2 + 1) * 3 * D] for r in range(4)]
        y_buf = [w_raw[b // 6][:, (b % 6) * D:(b % 6 + 1) * D] for b in range(Y_BUFS)]

        w_sh = [sb(f"w_shared_part{r}", [P, FC, 3, D], F16) for r in range(2)]
        silu = [sb(f"silu{q}", [P, BLK], F32) for q in range(2)]
        act32 = sb("act32", [P, BLK], F32)
        a_parts = [sb(f"a_parts{q}", [P, 2, BLK], F16) for q in range(2)]

        gu16 = sb("gu16", [P, 2, KC, 2 * FE], F16)
        dn16 = sb("dn16", [P, 2, FE // P, D], F16)
        pick_now = [sb(f"pick_now{q}", [P, 1], I32) for q in range(2)]
        xg = [sb(f"xg{q}", [P, 2, D], F16) for q in range(2)]
        xg_t = sb("xg_t", [P, 2, KC, P], F16)
        e_silu = sb("e_silu", [P, FE], F32)
        e_act = sb("e_act", [P, FE], F32)
        e_parts = [sb(f"e_parts{q}", [P, 2, FE], F16) for q in range(2)]
        e_parts_t = sb("e_parts_t", [P, 2, FE // P, P], F16)
        y_out = [sb(f"y_out{q}", [P, D], F32) for q in range(2)]
        past = sb("past", [P, SLOTS, E], F32)

        p_gu = [ps(f"p_gate_up{q}", [P, 512], F32) for q in range(2)]
        p_dn = [ps(f"p_down{m}", [P, 512], F32) for m in range(TB)]
        p_xt = ps("p_x_turned", [P, 1024], F16)
        p_egu = ps("p_expert_gate_up", [P, 512], F32)
        p_at = ps("p_act_turned", [P, 1024], F16)
        p_y = ps("p_expert_down", [P, 512], F32)
        rank = p_egu[:, 0:T * E].rearrange("p (t e) -> p t e", t=T)
        total = p_egu[:, T * E:T * E + E]
        token_table = p_y[:, 0:SLOTS]

        consts_ready = sem("consts_ready")
        dve_step = Steps(sem("route_step"))
        pool_step = Steps(sem("pool_const_step"))
        exps_in, exps_out = sem("exps_in"), sem("exps_out")
        both_ready, ranked = sem("both_ready"), sem("ranked")
        marked, mark_used = sem("marked"), sem("mark_used")
        owner_ready, tokens_ready = sem("owner_ready"), sem("tokens_ready")
        w_in = [sem(f"w_in{r}") for r in range(4)]
        w_high_ready, w_low_ready = sem("w_high_ready"), sem("w_low_ready")
        gated, silu_ready, act_ready = sem("gated"), sem("silu_ready"), sem("act_ready")
        a_high_ready, a_low_ready = sem("a_high_ready"), sem("a_low_ready")
        downed, added = sem("downed"), sem("added")
        gu_in = [sem(f"gu_in{q}") for q in range(2)]
        dn_in = [sem(f"dn_in{q}") for q in range(2)]
        gu_high, gu_low, dn_high, dn_low = sem("gu_high"), sem("gu_low"), sem("dn_high"), sem("dn_low")
        pick_set, gathered = sem("pick_set"), [sem(f"gathered{q}") for q in range(2)]
        e_turned, xg_t_ready = sem("e_turned"), sem("xg_t_ready")
        e_gated, e_silu_ready, e_act_ready = sem("e_gated"), sem("e_silu_ready"), sem("e_act_ready")
        e_high_ready, e_low_ready = sem("e_high_ready"), sem("e_low_ready")
        e_act_turned, e_act_t_ready = sem("e_act_turned"), sem("e_act_t_ready")
        e_downed, y_ready, y_saved = sem("e_downed"), sem("y_ready"), [sem(f"y_saved{q}") for q in range(2)]
        paced, pool_paced = sem("paced"), sem("pool_paced")
        y_in = [sem(f"y_in{b}") for b in range(Y_BUFS)]
        y_added = sem("y_added")
        out_saved = sem("out_saved")
        block = ctx.enter_context(nc.Block())

        steps = [("G", 0)]
        for f in range(1, FC):
            steps += [("G", f), ("D", f - 1)]
        steps += [("D", FC - 1)]

        def back(f):
            return 2 if f >= 2 else (1 if f == 0 else 3)

        def slot(i, k):
            return i * PER_BLOCK + (k - PER_BLOCK), i * (PER_BLOCK // 2) + (k // 2 - PER_BLOCK // 2)

        def real(s):
            return not isinstance(s, int) or 0 <= s < SLOTS

        def all_blocks(eng, body):
            for i in (0, 1):
                body(i)
            with eng.Fori(2, SLOT_BLOCKS) as i:
                body(i)
            for i in (SLOT_BLOCKS, BLOCKS - 1):
                body(i)

        def places(i):
            for g in range(3 * PER_BLOCK):
                yield g // 3, g % 3, (steps[g] if g < len(steps) else None)

        def flat(a):
            return a.rearrange("p a d -> p (a d)")

        def row_of(t):
            return flat(x1[:, bass.ds(t, 1), :])

        @block.sync
        def _(sp):
            for f in range(FC):
                if f >= 4:
                    sp.wait_ge(w_low_ready, f - 3)
                sp.dma_start(s_raw[f % 4], io["w_shared"][f].rearrange("p a d -> p (a d)")).then_inc(w_in[f % 4], 16)

            def load(s, q, which):
                raw_w, source, landed = (gu_raw, "w_gate_up", gu_in) if which == 0 else (dn_raw, "w_down", dn_in)
                e = sp.value_load(owner[0:1, bass.ds(s, 1)], min_val=0, max_val=E - 1)
                sp.dma_start(raw_w[q], io[source][bass.ds(e, 1)].rearrange("a (c p) f -> p (a c) f", p=P))\
                  .then_inc(landed[q], 16)

            def save(s, q):
                sp.wait_ge(y_ready, s + 1)
                sp.sem_inc(paced, 1)
                sp.dma_start(dram["y_rows"][bass.ds(s * P, P), :], y_out[q][:]).then_inc(y_saved[q], 16)

            sp.wait_ge(owner_ready, 1)
            for s in range(2):
                sp.wait_ge(w_low_ready, FC - 1 + s)
                load(s, s, 0)
                load(s, s, 1)
            sp.wait_ge(gu_low, 2)
            load(2, 0, 0)

            def slots(i):
                for k in range(PER_BLOCK):
                    s, _ = slot(i, k)
                    if real(s + 3):
                        sp.wait_ge(gu_low, s * 2 + 4)
                        sp.sem_inc(paced, 1)
                        load(s + 3, (k + 1) % 2, 0)
                    if real(s - 1):
                        save(s - 1, (k + 1) % 2)
                    if real(s + 2):
                        sp.wait_ge(dn_low, s + 1)
                        sp.sem_inc(paced, 1)
                        load(s + 2, k % 2, 1)
            slots(1)
            with sp.Fori(2, SLOT_BLOCKS) as i:
                slots(i)
            slots(SLOT_BLOCKS)
            save(SLOTS - 1, (SLOTS - 1) % 2)
            for t in range(T):
                sp.wait_ge(y_added, 2 * t + 2)
                sp.dma_start(out[t * P:(t + 1) * P, :], x1[:, t, :]).then_inc(out_saved, 16)
            sp.wait_ge(out_saved, 16 * T)

        @block.gpsimd
        def _(pool):
            pool_step.did(pool.iota(flat(past[:, 0:P // E, :]).bitcast(I32),
                                    pattern=[[1, P]], base=0, channel_multiplier=0))
            pool_step.settle(pool, pool.iota(row_i[0][:], pattern=[[P, T]], base=0, channel_multiplier=1))
            pool.tensor_copy(count_e[:], flat(past[:, 0:P // E, :]).bitcast(I32)).then_inc(consts_ready, 1)
            pool.tensor_copy(node_id[:], row_i[0][:]).then_inc(consts_ready, 1)
            pool.memset(ones[:], 1.0).then_inc(consts_ready, 1)
            pool.memset(both_led[:, 0, :], 0.0).then_inc(consts_ready, 1)
            pool_step.did(pool.memset(before[:], 1.0))
            pool_step.settle(pool, pool.memset(upto[:], 1.0))
            pool.affine_select(out=before[:], in_=before[:], compare_op=ALU.is_gt, fill=0.0, base=0,
                               pattern=[[1, P]], channel_multiplier=-1).then_inc(consts_ready, 1)
            pool.affine_select(out=upto[:], in_=upto[:], compare_op=ALU.is_ge, fill=0.0, base=0,
                               pattern=[[1, E], [-1, E]], channel_multiplier=0).then_inc(consts_ready, 1)
            pool.wait_ge(tokens_ready, 1)

            def slots(i, first):
                for q in range(2):
                    s = i * 2 + q
                    if not first:
                        pool.wait_ge(e_turned, s - 1)
                    pool.tensor_copy(pick_now[q][:], tokens[:, bass.ds(s, 1)]).then_inc(pick_set, 1)
                    pool.wait_ge(pick_set, s + 1)
                    pool.sem_inc(pool_paced, 1)
                    pool.indirect_dma_start(out=flat(xg[q][:]), out_offset=None, in_=dram["xn_rows"],
                                            in_offset=bass.IndirectOffsetOnAxis(ap=pick_now[q][:], axis=0))\
                        .then_inc(gathered[q], 16)
            peeled(pool, SLOTS // 2, slots)

            for q in range(2):
                pool.wait_ge(y_saved[q], 16 * (SLOTS // 2))
            for n in range(2 * T):
                t, k = divmod(n, 2)
                if n >= Y_BUFS:
                    pool.wait_ge(y_added, n - Y_BUFS + 1)
                pool.indirect_dma_start(out=y_buf[n % Y_BUFS], out_offset=None, in_=dram["y_rows"],
                                        in_offset=bass.IndirectOffsetOnAxis(ap=row_i[k][:, t:t + 1], axis=0))\
                    .then_inc(y_in[n % Y_BUFS], 16)

        @block.tensor
        def _(pe):
            def three(out_ap, count, lhs, rhs):
                n = 0
                for c in range(count):
                    for a, b in ((0, 0), (0, 1), (1, 0)):
                        mm = pe.matmul(out_ap, lhs(a, c), rhs(b, c), start=(n == 0), stop=(n == 3 * count - 1))
                        n += 1
                return mm

            def step(i, kind, f):
                u = i * FC + f
                q = f % 2
                if kind == "G":
                    if isinstance(i, int) and i == 0:
                        pe.wait_ge(w_low_ready, f + 1)
                    wait_from(pe, act_ready, u + (1 - back(f)))
                    for part in range(2):
                        mm = three(p_gu[q][:, part * BLK:(part + 1) * BLK], KC,
                                   lambda a, c: w_sh[a][:, f, part, c * P:(c + 1) * P],
                                   lambda b, c: x_parts[:, b, c, bass.ds(i * BLK, BLK)])
                    mm.then_inc(gated, 1)
                else:
                    pe.wait_ge(a_low_ready, u + 1)
                    if f == 0:
                        wait_from(pe, added, i * TB)
                    for m in range(TB):
                        for n, (a, b) in enumerate(((0, 0), (0, 1), (1, 0))):
                            mm = pe.matmul(p_dn[m][:], a_parts[q][:, a, m * P:(m + 1) * P], w_sh[b][:, f, 2, :],
                                           start=(f == 0 and n == 0), stop=(f == FC - 1 and n == 2))
                    mm.then_inc(downed, 1)

            def turn(s, pair, q):
                pe.wait_ge(gathered[q], pair * 16 + 16)
                wait_from(pe, xg_t_ready, s)
                for r in range(2):
                    for c in range(KC):
                        tr = pe.transpose(p_xt[:, (r * KC + c) * P:(r * KC + c + 1) * P],
                                          xg[q][:, r, c * P:(c + 1) * P], ident16[:])
                tr.then_inc(e_turned, 1)

            def gate_up(s):
                pe.wait_ge(xg_t_ready, s + 1)
                pe.wait_ge(gu_low, s * 2 + 2)
                wait_from(pe, e_act_ready, s)
                three(p_egu[:], KC, lambda a, c: xg_t[:, a, c, :], lambda b, c: gu16[:, b, c, :])\
                    .then_inc(e_gated, 1)

            def turn_act(s, q):
                pe.wait_ge(e_low_ready, s + 1)
                wait_from(pe, e_act_t_ready, s)
                n = FE // P
                for r in range(2):
                    for c in range(n):
                        tr = pe.transpose(p_at[:, (r * n + c) * P:(r * n + c + 1) * P],
                                          e_parts[q][:, r, c * P:(c + 1) * P], ident16[:])
                tr.then_inc(e_act_turned, 1)

            def expert_down(s):
                pe.wait_ge(e_act_t_ready, s + 1)
                pe.wait_ge(dn_low, s + 1)
                wait_from(pe, y_ready, s)
                three(p_y[:], FE // P, lambda a, c: e_parts_t[:, a, c, :], lambda b, c: dn16[:, b, c, :])\
                    .then_inc(e_downed, 1)

            def ranks():
                pe.wait_ge(consts_ready, 6)
                pe.wait_ge(both_ready, 1)
                pe.matmul(rank, before[:], both, start=True, stop=False)
                for d in range(2, T):
                    pe.matmul(rank[:, d:T, :], ones[:], both[:, 0:T - d, :], start=False, stop=False,
                              skip_group_check=True)
                pe.matmul(rank, ones[:], both_led[:, 0:T, :], start=False, stop=True).then_inc(ranked, 1)
                for t in range(T):
                    mm = pe.matmul(total, ones[:], both[:, t, :], start=(t == 0), stop=(t == T - 1))
                mm.then_inc(ranked, 1)

            def use_marks(f):
                for n in range((f - MARK_FROM) * MARKS, min((f - MARK_FROM + 1) * MARKS, 2 * T)):
                    pe.wait_ge(marked, n + 1)
                    pe.matmul(token_table, at_row[n % MARKS][:], at_slot[n % MARKS][:],
                              start=(n == 0), stop=(n == 2 * T - 1)).then_inc(mark_used, 1)

            def body(i):
                for k, r, now in places(i):
                    s, pair = slot(i, k)
                    if r == 0 and real(s):
                        gate_up(s)
                    if r == 1 and real(s - 1):
                        turn_act(s - 1, (k + 1) % 2)
                    if r == 1 and real(s) and real(s + 1):
                        turn(s + 1, slot(i, k + 1)[1], (k + 1) % 2)
                    if r == 2 and real(s - 1):
                        expert_down(s - 1)
                    if now:
                        step(i, *now)
                        if isinstance(i, int) and i == 0 and now[0] == "D":
                            if now[1] == 0:
                                ranks()
                            if MARK_FROM <= now[1] < MARK_TO:
                                use_marks(now[1])
                if isinstance(i, int) and i == 0:
                    turn(0, 0, 0)
            all_blocks(pe, body)

        @block.scalar
        def _(act):
            def split_shared(f):
                act.wait_ge(w_in[f % 4], 16 * (f // 4 + 1))
                act.activation(flat(w_sh[0][:, f, :, :]), s_raw[f % 4], ACT.Copy, scale=WS).then_inc(w_high_ready, 1)

            def split_gu(s, pair, q, h):
                act.wait_ge(gu_in[q], pair * 16 + 16)
                wait_from(act, e_gated, s)
                cs = slice(h * 2, h * 2 + 2)
                act.activation(gu16[:, 0, cs, :], gu_raw[q][:, cs, :], ACT.Copy, scale=WS).then_inc(gu_high, 1)

            def copy_rows(s):
                act.wait_ge(e_turned, s + 1)
                wait_from(act, e_gated, s)
                act.activation(xg_t[:].rearrange("p r c m -> p (r c m)"), p_xt[:], ACT.Copy).then_inc(xg_t_ready, 1)

            def body(i):
                zero = isinstance(i, int) and i == 0
                if zero:
                    split_shared(0)
                    split_shared(1)
                    act.wait_ge(exps_in, 1)
                    act.activation(ratio[:], ratio[:], ACT.Exp).then_inc(exps_out, 1)
                    act.activation(sgate[:], logits[:, :, E], ACT.Exp, scale=-1.0).then_inc(exps_out, 1)
                for k, r, now in places(i):
                    s, pair = slot(i, k)
                    if r == 0 and real(s):
                        act.wait_ge(e_gated, s + 1)
                        wait_from(act, e_act_ready, s)
                        act.activation(e_silu[:], p_egu[:, 0:FE], ACT.Silu, scale=1.0 / WS).then_inc(e_silu_ready, 1)
                    if r < 2 and real(s) and real(s + 1):
                        split_gu(s + 1, slot(i, k + 1)[1], (k + 1) % 2, r)
                    if r == 1 and real(s - 1):
                        act.wait_ge(e_act_turned, s)
                        wait_from(act, e_downed, s - 1)
                        act.activation(e_parts_t[:].rearrange("p r c m -> p (r c m)"), p_at[:, 0:2 * FE],
                                       ACT.Copy).then_inc(e_act_t_ready, 1)
                    if r == 1 and real(s) and real(s + 1):
                        copy_rows(s + 1)
                    if r == 2 and real(s - 1):
                        act.wait_ge(e_downed, s)
                        wait_from(act, y_saved[(k + 1) % 2], slot(i, k - 1)[1] * 16)
                        act.activation(y_out[(k + 1) % 2][:], p_y[:], ACT.Copy, scale=1.0 / (WS * WS))\
                           .then_inc(y_ready, 1)
                    if r == 2 and real(s):
                        act.wait_ge(dn_in[k % 2], pair * 16 + 16)
                        wait_from(act, e_downed, s)
                        act.activation(dn16[:, 0, :, :], dn_raw[k % 2], ACT.Copy, scale=WS).then_inc(dn_high, 1)
                    if now and now[0] == "G":
                        f = now[1]
                        act.wait_ge(gated, i * FC + (f + 1))
                        act.activation(silu[f % 2][:], p_gu[f % 2][:, 0:BLK], ACT.Silu, scale=1.0 / WS)\
                           .then_inc(silu_ready, 1)
                        if zero and f + 2 < FC:
                            split_shared(f + 2)
                if zero:
                    for h in range(2):
                        split_gu(0, 0, 0, h)
                    copy_rows(0)
            all_blocks(act, body)

        @block.vector
        def _(dve):
            def settle(ins):
                dve_step.settle(dve, ins)

            def wide(a, shape, axis):
                return a.unsqueeze(axis).broadcast_to(shape)

            grid = [P, T, E]

            def choose():
                dve.wait_ge(consts_ready, 6)
                e_row = wide(count_e[:, 0:E], grid, 1)
                settle(dve.tensor_copy(raw[:], logits[:, :, 0:E]))
                for k in range(2):
                    settle(dve.tensor_reduce(top[k][:], raw[:], AX.X, ALU.max))
                    settle(dve.tensor_tensor(key[:], raw[:], wide(top[k][:], grid, 2), ALU.is_equal))
                    settle(dve.scalar_tensor_tensor(hit[k][:], e_row, -float(P), key[:], ALU.add, ALU.mult))
                    settle(dve.tensor_reduce(low_key[:], hit[k][:], AX.X, ALU.min))
                    settle(dve.tensor_tensor(hit[k][:], hit[k][:], wide(low_key[:], grid, 2), ALU.is_equal))
                    if k == 0:
                        settle(dve.scalar_tensor_tensor(raw[:], hit[0][:], -1.0e30, raw[:], ALU.mult, ALU.add))
                dve.tensor_tensor(both, hit[0][:], hit[1][:], ALU.add).then_inc(both_ready, 1)
                dve.tensor_tensor(ratio[:], top[1][:], top[0][:], ALU.subtract).then_inc(exps_in, 1)

            def shares():
                dve.wait_ge(exps_out, 2)
                settle(dve.tensor_scalar(share[1][:], ratio[:], 1.0, None, ALU.add))
                settle(dve.reciprocal(share[0][:], share[1][:]))
                settle(dve.tensor_tensor(share[1][:], ratio[:], share[0][:], ALU.mult))
                settle(dve.tensor_scalar(sgate[:], sgate[:], 1.0, None, ALU.add))
                settle(dve.reciprocal(sgate[:], sgate[:]))
                settle(dve.tensor_scalar(sgate[:], sgate[:], 1.0 / (WS * WS), None, ALU.mult))

            def lay_out_slots():
                dve.wait_ge(ranked, 2)
                settle(dve.tensor_copy(held[:], total))
                square = [P, E, E]
                settle(dve.tensor_scalar(base[:], count_e[:, 0:E], float(P), None, ALU.mult))
                settle(dve.tensor_tensor(cube[:], wide(held[:], square, 2), wide(base[:], square, 1), ALU.is_gt))
                settle(dve.tensor_reduce(tiles[:], cube[:], AX.X, ALU.add))
                settle(dve.tensor_tensor(cube[:], upto[:], wide(tiles[:], square, 1), ALU.mult))
                settle(dve.tensor_reduce(ends[:], cube[:], AX.X, ALU.add))
                settle(dve.tensor_tensor(base[:], ends[:], tiles[:], ALU.subtract))
                settle(dve.tensor_scalar(base[:], base[:], float(P), None, ALU.mult))
                settle(dve.tensor_tensor(place[:], rank, wide(base[:], grid, 1), ALU.add))
                slot_grid = [P, SLOTS, E]
                settle(dve.tensor_tensor(past[:], wide(count_e[:, 0:SLOTS], slot_grid, 2),
                                         wide(ends[:], slot_grid, 1), ALU.is_ge))
                settle(dve.tensor_reduce(owner_f[:], past[:], AX.X, ALU.add))
                dve.tensor_scalar(owner[:], owner_f[:], float(E - 1), None, ALU.min).then_inc(owner_ready, 1)

            def rows():
                for k in range(2):
                    settle(dve.tensor_tensor(hit[k][:], hit[k][:], place[:], ALU.mult))
                    settle(dve.tensor_reduce(row_f[k][:], hit[k][:], AX.X, ALU.add))
                    settle(dve.tensor_copy(row_i[k][:], row_f[k][:]))
                    settle(dve.tensor_scalar(in_tile[k][:], row_i[k][:], P - 1, None, ALU.bitwise_and))
                    settle(dve.tensor_copy(in_tile_f[k][:], in_tile[k][:]))
                    settle(dve.tensor_tensor(slot_f[k][:], row_f[k][:], in_tile_f[k][:], ALU.subtract))
                    settle(dve.tensor_scalar(slot_f[k][:], slot_f[k][:], 1.0 / P, None, ALU.mult))

            def mark(f):
                for n in range((f - MARK_FROM) * MARKS, min((f - MARK_FROM + 1) * MARKS, 2 * T)):
                    t, k = divmod(n, 2)
                    wait_from(dve, mark_used, n - MARKS + 1)
                    dve.tensor_scalar(at_row[n % MARKS][:], count_e[:], in_tile_f[k][:, t:t + 1], None, ALU.is_equal)
                    dve.tensor_scalar(at_slot[n % MARKS][:], count_e[:, 0:SLOTS], slot_f[k][:, t:t + 1],
                                      node_id[:, t:t + 1], ALU.is_equal, ALU.mult).then_inc(marked, 1)

            def split_shared(f):
                dve.wait_ge(w_high_ready, f + 1)
                dve.scalar_tensor_tensor(flat(w_sh[1][:, f, :, :]), s_raw[f % 4], WS, flat(w_sh[0][:, f, :, :]),
                                         ALU.mult, ALU.subtract).then_inc(w_low_ready, 1)

            def split_gu(s, q, h):
                dve.wait_ge(gu_high, s * 2 + (h + 1))
                cs = slice(h * 2, h * 2 + 2)
                dve.scalar_tensor_tensor(flat(gu16[:, 1, cs, :]), flat(gu_raw[q][:, cs, :]), WS,
                                         flat(gu16[:, 0, cs, :]), ALU.mult, ALU.subtract).then_inc(gu_low, 1)

            def add_results(t):
                for k in range(2):
                    n = 2 * t + k
                    dve.wait_ge(y_in[n % Y_BUFS], 16 * (n // Y_BUFS + 1))
                    if k == 0:
                        dve.wait_ge(added, (t // TB + 1) * TB)
                    else:
                        dve.wait_ge(y_added, n)
                    dve.scalar_tensor_tensor(x1[:, t, :], y_buf[n % Y_BUFS], share[k][:, t:t + 1], x1[:, t, :],
                                             ALU.mult, ALU.add).then_inc(y_added, 1)

            def hidden_layer(i, f):
                u = i * FC + f
                q = f % 2
                up = p_gu[q][:, BLK:2 * BLK]
                dve.wait_ge(silu_ready, u + 1)
                wait_from(dve, a_low_ready, u)
                wait_from(dve, downed, u + (1 - back(f)))
                dve.tensor_tensor(a_parts[q][:, 0, :], silu[q][:], up, ALU.mult).then_inc(a_high_ready, 1)
                dve.tensor_tensor(act32[:], silu[q][:], up, ALU.mult).then_inc(act_ready, 1)
                dve.wait_ge(a_high_ready, u + 1)
                dve.wait_ge(act_ready, u + 1)
                dve.tensor_tensor(a_parts[q][:, 1, :], act32[:], a_parts[q][:, 0, :], ALU.subtract)\
                   .then_inc(a_low_ready, 1)

            def expert_hidden(s, q):
                up = p_egu[:, FE:2 * FE]
                dve.wait_ge(e_silu_ready, s + 1)
                wait_from(dve, e_low_ready, s)
                wait_from(dve, e_act_turned, s - 1)
                dve.tensor_tensor(e_parts[q][:, 0, :], e_silu[:], up, ALU.mult).then_inc(e_high_ready, 1)
                dve.tensor_tensor(e_act[:], e_silu[:], up, ALU.mult).then_inc(e_act_ready, 1)
                dve.wait_ge(e_high_ready, s + 1)
                dve.wait_ge(e_act_ready, s + 1)
                dve.tensor_tensor(e_parts[q][:, 1, :], e_act[:], e_parts[q][:, 0, :], ALU.subtract)\
                   .then_inc(e_low_ready, 1)

            def body(i):
                zero = isinstance(i, int) and i == 0
                final = isinstance(i, int) and i == BLOCKS - 1
                if zero:
                    choose()
                    split_shared(0)
                    split_shared(1)
                for k, r, now in places(i):
                    s, pair = slot(i, k)
                    if r == 0 and real(s):
                        expert_hidden(s, k % 2)
                    if r < 2 and real(s) and real(s + 1):
                        split_gu(s + 1, (k + 1) % 2, r)
                    if r == 2 and real(s):
                        dve.wait_ge(dn_high, s + 1)
                        dve.scalar_tensor_tensor(flat(dn16[:, 1, :, :]), flat(dn_raw[k % 2]), WS,
                                                 flat(dn16[:, 0, :, :]), ALU.mult, ALU.subtract).then_inc(dn_low, 1)
                    if now and now[0] == "G":
                        f = now[1]
                        hidden_layer(i, f)
                        if zero and f + 2 < FC:
                            split_shared(f + 2)
                        if zero and f == 1:
                            shares()
                        if zero and f == 2:
                            lay_out_slots()
                        if zero and f == MARK_FROM:
                            rows()
                        if zero and MARK_FROM <= f < MARK_TO:
                            mark(f)
                        if zero and f == MARK_TO:
                            dve.wait_ge(mark_used, 2 * T)
                            dve.tensor_copy(tokens[:], token_table).then_inc(tokens_ready, 1)
                        if final and f >= SUM_FROM:
                            add_results(f - SUM_FROM)
                if zero:
                    for h in range(2):
                        split_gu(0, 0, h)
                dve.wait_ge(downed, i * FC + FC)
                for m in range(TB):
                    dve.scalar_tensor_tensor(row_of(i * TB + m), p_dn[m][:], sgate[:, bass.ds(i * TB + m, 1)],
                                             row_of(i * TB + m), ALU.mult, ALU.add).then_inc(added, 1)
                if final:
                    for t in range(FC - SUM_FROM, T):
                        add_results(t)
            all_blocks(dve, body)


def program(nc, io, out):
    dram = {
        "a_rows": nc.dram_tensor("a_rows", [H, N], F32, kind="Internal").ap(),
        "xn_rows": nc.dram_tensor("xn_rows", [N, 2 * D], F16, kind="Internal").ap(),
        "y_rows": nc.dram_tensor("y_rows", [SLOTS * P, D], F32, kind="Internal").ap(),
    }
    with ExitStack() as ctx:
        sb, ps, sem = make_tools(nc, ctx)
        ident = sb("ident", [P, P], F32)
        ident16 = sb("ident16", [P, P], F16)
        with ExitStack() as upper:
            usb, _, _ = make_tools(nc, upper)
            keep = {"ident16": ident16, "hidden": usb("hidden", [P, T, H * (DH + 1)], F32)}
            with ExitStack() as inner:
                isb, _, _ = make_tools(nc, inner)
                keep["mask"] = isb("mask", [P, T, N], F16)
                keep["seq"] = isb("seq", [P, T * D], F32)
                for n in ("e_pos", "e_neg", "f_pos", "f_neg", "neg_b", "step_b"):
                    keep[n] = isb(n, [P, H * T], F32)
                attention_operands(nc, io, dram, keep, ident)
                attention_heads(nc, io, dram, keep)
            keep["x1"] = keep["hidden"][:].rearrange("p t c -> p (t c)")[:, 0:T * D].rearrange("p (t d) -> p t d", t=T)
            keep["x_parts"] = usb("x_parts", [P, 2, KC, N], F16)
            keep["logits"] = usb("logits", [P, T, E + 1], F32)
            output_projection(nc, io, dram, keep, ident)
            feed_forward(nc, io, dram, keep, ident, out)


def kernel(**inputs):
    import numpy as np
    import concourse.bacc as bacc
    from concourse import mybir as mb
    from concourse.bass_utils import run_bass_kernel_spmd

    def plain(name):
        return np.asarray(inputs[name])

    a1, a2 = plain("L0_gnn_a1"), plain("L0_gnn_a2")
    sides = [plain(f"L0_ffn_shared_w_{n}").reshape(FC, P, KC, P).transpose(0, 3, 2, 1).reshape(FC, P, D)
             for n in ("gate", "up")]
    w_shared = np.stack(sides + [plain("L0_ffn_shared_w_down").T.reshape(FC, P, D)], axis=2)
    laid_out = {
        "x": plain("x"),
        "adj_t": plain("adj").T,
        "w_seq": plain("L0_gnn_W_seq"),
        "w_seq_t": plain("L0_gnn_W_seq").T,
        "w_out": plain("L0_gnn_W_out"),
        "b_out": plain("L0_gnn_b_out")[None, :],
        "w_route": np.concatenate([plain("L0_ffn_gate_w"), plain("L0_ffn_shared_gate_w")], axis=0).T,
        "w_shared": w_shared,
        "w_gate_up": plain("L0_ffn_w_gate_up"),
        "w_down": plain("L0_ffn_w_down"),
        "a_rep": np.stack([np.tile(a1, P // DH), np.tile(a2, P // DH)], axis=1),
    }
    nc = bacc.Bacc("TRN2", target_bir_lowering=False, num_devices=1)
    arrays, io = {}, {}
    for name, a in laid_out.items():
        a = np.ascontiguousarray(a)
        arrays[f"in_{name}"] = a
        io[name] = nc.dram_tensor(f"in_{name}", a.shape, mb.dt.from_np(a.dtype), kind="ExternalInput").ap()
    out = nc.dram_tensor("out_0", (N, D), mb.dt.float32, kind="ExternalOutput").ap()
    program(nc, io, out)
    r = run_bass_kernel_spmd(nc, [arrays], core_ids=[0])
    return r.results[0]["out_0"]
```

```python
from contextlib import ExitStack

import concourse.bass as bass
from concourse import mybir

P = 128
N, D = 2048, 512
H, DH = 16, 32
T = N // P
KC = D // P
GW = 2 * (DH + 1)
G_COLS = 3 * GW
PER_BANK = 3
BANKS = -(-T // PER_BANK)
DEGREE_AT = T // 2
GROUPS = [(0, 4), (4, 8), (8, 16)]
RING = 4
OVER = 3
HARD = [[1, 5, 9, 13], [1, 5, 9, 13]]
COPY_AT, HIGH_AT, TURN_AT = 1, 5, 8
FOLD_AT, OPERAND_AT, LOW_AT, COMBINE_AT = 1, 2, 7, 10
ALPHA = 0.2
STEP = 1.0e30
GSCALE = 256.0
EPS = 1.0e-5
WS = 256.0
E = 16
FE = 256
FS = 1408
FC = FS // P
SLOTS = 2 * N // P + E
BLK = 256
BLOCKS = N // BLK
TB = BLK // P
PER_BLOCK = 8
FEW = SLOTS - PER_BLOCK
SLOT_BLOCKS = SLOTS // PER_BLOCK
MARKS = 8
SHARES_AT = 8
MARK_FROM = 5
MARK_TO = MARK_FROM - (-2 * T // MARKS)
SUM_TILES = {
    SLOTS: {(BLOCKS - 1, f): t for f, t in ((4, [0]), (5, [1]), (6, [2, 3]), (7, [4, 5]), (8, [6, 7]),
                                            (9, [8, 9]), (10, [10, 11]))},
    FEW: {(BLOCKS - 2 + (f + 4) // FC, (f + 4) % FC): [f] for f in range(14)},
}
Y_BUFS = 12

F32 = mybir.dt.float32
F16 = mybir.dt.float16
BF16 = mybir.dt.bfloat16
I32 = mybir.dt.int32
ALU = mybir.AluOpType
ACT = mybir.ActivationFunctionType
AX = mybir.AxisListType
RMAX = bass.bass_isa.ReduceOp.max


class Steps:

    def __init__(self, sem):
        self.sem, self.at = sem, 0

    def did(self, ins):
        ins.then_inc(self.sem, 1)
        self.at = self.at + 1
        return self.at

    def settle(self, eng, ins):
        self.did(ins)
        eng.wait_ge(self.sem, self.at)


def peeled(eng, count, body):
    body(0, True)
    with eng.Fori(1, count) as i:
        body(i, False)


def peeled_both(eng, count, body):
    body(0, True, False)
    with eng.Fori(1, count - 1) as i:
        body(i, False, False)
    body(count - 1, False, True)


def rolled(eng, first, last, count, body):
    for i in range(first):
        body(i)
    with eng.Fori(first, last) as i:
        body(i)
    for i in range(last, count):
        body(i)


def tile_there(t):
    return not isinstance(t, int) or 0 <= t < T


def wait_from(eng, sem, value):
    if not (isinstance(value, int) and value <= 0):
        eng.wait_ge(sem, value)


def make_tools(nc, ctx):
    def sb(name, shape, dt):
        return ctx.enter_context(nc.sbuf_tensor(name, shape, dt))

    def ps(name, shape, dt):
        return ctx.enter_context(nc.psum_tensor(name, shape, dt))

    def sem(name):
        return ctx.enter_context(nc.semaphore(name))

    return sb, ps, sem


def attention_operands(nc, io, dram, keep, ident):
    with ExitStack() as ctx:
        sb, ps, sem = make_tools(nc, ctx)
        x_all = keep["hidden"][:].rearrange("p t c -> p (t c)")[:, 0:T * D].rearrange("p (t d) -> p t d", t=T)
        w_seq = sb("w_seq", [P, KC, D], F32)
        w_seq_t = sb("w_seq_t", [P, KC, D], F32)
        a_rep = sb("a_rep", [P, 2], F32)
        a_diag = sb("a_diag", [P, KC, 2 * H], F32)
        v_sb = sb("v_sb", [P, KC, 2 * H], F32)
        stats = sb("stats", [P, T, 6], F32)
        mv = sb("mv", [P, T, 2], F32)
        rstd = sb("rstd", [P, T], F32)
        std = sb("std", [P, T], F32)
        var = sb("var", [P, T], F32)
        w_parts = [sb(f"w_seq_part{r}", [P, KC, D], F16) for r in range(2)]
        v_parts = [sb(f"v_part{r}", [P, KC, 2 * H], F16) for r in range(2)]
        xn_stage = [sb(f"xn_stage{q}", [P, D], F32) for q in range(2)]
        xn_parts = [sb(f"xn_parts{q}", [P, 2, D], F16) for q in range(2)]
        xn_t = [sb(f"xn_t{q}", [P, 2, KC, P], F16) for q in range(2)]
        s_t = w_seq_t[:].rearrange("p c k -> p (c k)")[0:H, 0:N]
        ones = sb("ones", [P, P], F16)
        empty = sb("empty", [P, N], F16)
        b_max = sb("b_max", [P, H], F32)
        b_top = sb("b_top", [P, H], F32)
        z = sb("z", [P, H, T], F32)
        m = sb("m", [P, H, T], F32)
        ea = sb("ea", [P, H, T], F32)
        eb = sb("eb", [P, H, T], F32)
        a_all = sb("a_all", [P, H, T], F32)
        b_all = sb("b_all", [P, H, T], F32)

        p_xt = [ps(f"p_xt{q}", [P, 2 * D], F16) for q in range(2)]
        p_seq = [ps(f"p_seq{q}", [P, 512], F32) for q in range(2)]
        p_s = [ps(f"p_s{q}", [P, 512], F32) for q in range(2)]
        p_w = [ps(f"p_w{q}", [P, 512], F32) for q in range(2)]

        v_banks = p_s + p_w

        x_in = [sem(f"x_in{r}") for r in range(4)]
        ident_ready = sem("ident_ready")
        w_in = sem("w_in")
        wt_in = sem("wt_in")
        a_in = sem("a_in")
        adj_in = sem("adj_in")
        diag_ready = sem("diag_ready")
        ones_ready = sem("ones_ready")
        v_made = sem("v_made")
        v_ready = sem("v_ready")
        stats_ready, mv_ready, rstd_ready = sem("stats_ready"), sem("mv_ready"), sem("rstd_ready")
        var_ready = sem("var_ready")
        std_ready = sem("std_ready")
        w_high, w_low = sem("w_seq_high"), sem("w_seq_low")
        v_high, v_low = sem("v_high"), sem("v_low")
        normed = sem("normed")
        xn_high, xn_low = sem("xn_high"), sem("xn_low")
        turned = sem("turned")
        xn_t_ready = sem("xn_t_ready")
        projected = sem("projected")
        seq_saved = sem("seq_saved")
        scores_saved = sem("scores_saved")
        rows_turned, rows_saved = sem("rows_turned"), sem("rows_saved")
        max_local = sem("max_local")
        max_all = sem("max_all")
        counted = sem("counted")
        dve_step = Steps(sem("dve_step"))
        pool_step = Steps(sem("pool_step"))
        act_step = Steps(sem("act_step"))
        factors_in = sem("factors_in")
        rows_out = sem("rows_out")
        degree_read = sem("degree_read")
        mask_filled = sem("mask_filled")
        block = ctx.enter_context(nc.Block())

        @block.sync
        def _(sp):
            sp.dma_start(w_seq_t[:], io["w_seq_t"].rearrange("(c p) k -> p c k", p=P)).then_inc(wt_in, 16)
            sp.dma_start(a_rep[:], io["a_rep"]).then_inc(a_in, 16)
            xv = io["x"].rearrange("(t p) d -> p t d", p=P)
            for r in range(4):
                part = slice(r * (T // 4), (r + 1) * (T // 4))
                sp.dma_start(x_all[:, part, :], xv[:, part, :]).then_inc(x_in[r], 16)
                if r == 0:
                    sp.dma_start(w_seq[:], io["w_seq"].rearrange("(c p) k -> p c k", p=P)).then_inc(w_in, 16)
            sp.wait_ge(rows_saved, T // 2)
            sp.dma_start(dram["a_rows"], s_t).then_inc(rows_out, 16)
            sp.wait_ge(rows_out, 16)
            for q in range(2):
                sp.dma_start(keep["a_row"][q][:], dram["a_rows"][q:q + 1, :].broadcast_to([P, N]))\
                  .then_inc(keep["rows_in"][q], 16)
        @block.gpsimd
        def _(pool):
            pool_step.settle(pool, pool.memset(ident[:], 0.0))
            pool_step.settle(pool, pool.affine_select(out=ident[:], in_=ident[:], compare_op=ALU.not_equal,
                                                      fill=1.0, base=0, pattern=[[-1, P]], channel_multiplier=1))
            pool.tensor_copy(keep["ident16"][:], ident[:]).then_inc(ident_ready, 1)
            pool.memset(ones[:], 1.0).then_inc(ones_ready, 1)
            pool_step.settle(pool, pool.memset(a_diag[:], 1.0))
            pool.wait_ge(a_in, 16)
            for w in range(2):
                half = a_diag[:, :, w * H:(w + 1) * H]
                pool_step.settle(pool, pool.tensor_scalar(half, half, a_rep[:, w:w + 1], None, ALU.mult))
                pool_step.settle(pool, pool.affine_select(
                    out=half, in_=half, compare_op=ALU.is_ge, fill=0.0, base=0,
                    pattern=[[P, KC], [-DH, H]], channel_multiplier=1))
                last = pool.affine_select(
                    out=half, in_=half, compare_op=ALU.is_ge, fill=0.0, base=DH - 1,
                    pattern=[[-P, KC], [DH, H]], channel_multiplier=-1)
                last.then_inc(diag_ready, 1)
            pool.wait_ge(x_in[2], 16)
            for j in range(T):
                pool.dma_start(keep["mask"][:, j, :], io["adj_t"][j * P:(j + 1) * P, :]).then_inc(adj_in, 16)
            pool.wait_ge(max_local, 1)
            pool.partition_all_reduce(b_top[:], b_max[:], P, RMAX).then_inc(max_all, 1)

        @block.tensor
        def _(pe):
            pe.wait_ge(wt_in, 16)
            pe.wait_ge(diag_ready, 2)
            for k in range(KC):
                for c in range(KC):
                    mm = pe.matmul(v_banks[k][:, 0:2 * H], w_seq_t[:, c, k * P:(k + 1) * P], a_diag[:, c, :],
                                   start=(c == 0), stop=(c == KC - 1))
                mm.then_inc(v_made, 1)
            pe.wait_ge(v_ready, KC)
            pe.wait_ge(w_low, 1)
            pe.wait_ge(v_low, 1)
            pe.wait_ge(ident_ready, 1)

            def turn(t, q):
                pe.wait_ge(xn_low, t + 1)
                wait_from(pe, xn_t_ready, t - 1)
                for r in range(2):
                    for c in range(KC):
                        tr = pe.transpose(p_xt[q][:, (r * KC + c) * P:(r * KC + c + 1) * P],
                                          xn_parts[q][:, r, c * P:(c + 1) * P], keep["ident16"][:])
                tr.then_inc(turned, 1)

            def product(out_ap, lhs, rhs):
                n = 0
                for c in range(KC):
                    for a, b in ((0, 0), (0, 1), (1, 0)):
                        mm = pe.matmul(out_ap, lhs(a, c), rhs(b, c), start=(n == 0), stop=(n == 3 * KC - 1))
                        n += 1
                return mm

            def degree(b):
                if b == 0:
                    pe.wait_ge(ones_ready, 1)
                    pe.wait_ge(adj_in, 16 * T)
                if b >= 2:
                    pe.wait_ge(degree_read, b - 1)
                for j in range(T):
                    mm = pe.matmul(p_w[b % 2][:], ones[:], keep["mask"][:, j, b * 512:(b + 1) * 512],
                                   start=(j == 0), stop=(j == T - 1))
                mm.then_inc(counted, 1)

            def turn_scores(pair):
                pe.wait_ge(scores_saved, max(DEGREE_AT + pair, 2 * pair + 2))
                for q in range(2):
                    tr = pe.transpose(p_s[(pair + 1) % 2][0:H, (q + 1) * P:(q + 2) * P], a_all[:, :, 2 * pair + q], ident[:])
                tr.then_inc(rows_turned, 1)

            turn(0, 0)

            def tile_pair(i):
                for q in range(2):
                    t = i * 2 + q
                    if tile_there(t + 1):
                        turn(t + 1, 1 - q)
                    pe.wait_ge(xn_t_ready, t + 1)
                    wait_from(pe, seq_saved, t - 1)
                    wait_from(pe, scores_saved, t - 1)
                    xs = lambda r, c: xn_t[q][:, r, c, :]
                    product(p_seq[q][:], xs, lambda r, c: w_parts[r][:, c, :])
                    if isinstance(t, int) and t > DEGREE_AT:
                        pe.wait_ge(rows_saved, t - DEGREE_AT)
                    product(p_s[q][:, 0:2 * H], xs, lambda r, c: v_parts[r][:, c, :]).then_inc(projected, 1)
                    if isinstance(t, int) and 0 <= t - DEGREE_AT < T // 2 - 1:
                        turn_scores(t - DEGREE_AT)
                    if isinstance(t, int) and 0 <= t - DEGREE_AT < N // 512:
                        degree(t - DEGREE_AT)

            rolled(pe, 1, DEGREE_AT // 2, T // 2, tile_pair)
            turn_scores(T // 2 - 1)

        @block.scalar
        def _(act):
            def split_weights():
                act.wait_ge(w_in, 16)
                act.activation(w_parts[0][:], w_seq[:], ACT.Copy, scale=WS).then_inc(w_high, 1)
                for k in range(KC):
                    act.wait_ge(v_made, k + 1)
                    act.activation(v_sb[:, k, :], v_banks[k][:, 0:2 * H], ACT.Copy).then_inc(v_ready, 1)
                act.wait_ge(v_ready, KC)
                act.activation(v_parts[0][:], v_sb[:], ACT.Copy, scale=WS).then_inc(v_high, 1)

            def root(group):
                lo, hi = GROUPS[group]
                act.wait_ge(var_ready, group + 1)
                act.activation(std[:, lo:hi], var[:, lo:hi], ACT.Sqrt).then_inc(std_ready, 1)

            def high(t, q):
                act.wait_ge(normed, t + 1)
                wait_from(act, turned, t - 1)
                act.activation(xn_parts[q][:, 0, :], xn_stage[q][:], ACT.Copy).then_inc(xn_high, 1)

            def copy_turned(t, q):
                act.wait_ge(turned, t + 1)
                wait_from(act, projected, t - 1)
                act.activation(xn_t[q][:].rearrange("p r c m -> p (r c m)"), p_xt[q][:],
                               ACT.Copy).then_inc(xn_t_ready, 1)

            def save(t, q):
                act.wait_ge(projected, t + 1)
                act.activation(keep["seq"][:, bass.ds(t * D, D)], p_seq[q][:], ACT.Copy, scale=1.0 / WS)\
                   .then_inc(seq_saved, 1)

            root(0)
            high(0, 0)
            split_weights()
            high(1, 1)
            copy_turned(0, 0)
            high(2, 0)

            def tile_pair(i):
                for q in range(2):
                    t = i * 2 + q
                    if tile_there(t + 1):
                        copy_turned(t + 1, 1 - q)
                    if tile_there(t + 3):
                        high(t + 3, 1 - q)
                    if tile_there(t - 1):
                        save(t - 1, 1 - q)
                    if isinstance(t, int) and t + 1 < len(GROUPS):
                        root(t + 1)

            rolled(act, 1, T // 2 - 2, T // 2, tile_pair)
            save(T - 1, 1)
            act.wait_ge(factors_in, 1)
            act_step.did(act.activation(keep["e_pos"][:], ea[:], ACT.Exp))
            act_step.did(act.activation(keep["e_neg"][:], eb[:], ACT.Exp))
            act_step.did(act.activation(keep["f_pos"][:], z[:], ACT.Exp))
            act_step.did(act.activation(keep["f_neg"][:], m[:], ACT.Exp))
            act.wait_ge(act_step.sem, act_step.at)

        @block.vector
        def _(dve):
            def moments(group):
                lo, hi = GROUPS[group]
                for t in range(lo, hi):
                    last = dve.bn_stats(stats[:, t, :], x_all[:, t, :])
                last.then_inc(stats_ready, 1)
                dve.wait_ge(stats_ready, group + 1)
                for t in range(lo, hi):
                    last = dve.bn_aggr(mv[:, t, :], stats[:, t, :])
                last.then_inc(mv_ready, 1)
                dve.wait_ge(mv_ready, group + 1)
                dve.tensor_scalar(var[:, lo:hi], mv[:, lo:hi, 1], EPS, None, ALU.add).then_inc(var_ready, 1)

            def x_tile(t):
                return x_all[:, bass.ds(t, 1), :].rearrange("p a d -> p (a d)")

            def invert(group):
                lo, hi = GROUPS[group]
                dve.wait_ge(std_ready, group + 1)
                dve.reciprocal(rstd[:, lo:hi], std[:, lo:hi]).then_inc(rstd_ready, 1)
                dve.wait_ge(rstd_ready, group + 1)

            def norm(t, q):
                wait_from(dve, xn_low, t - 1)
                dve.tensor_scalar(xn_stage[q][:], x_tile(t),
                                  mv[:, bass.ds(t, 1), 0], rstd[:, bass.ds(t, 1)],
                                  ALU.subtract, ALU.mult).then_inc(normed, 1)

            def low(t, q):
                dve.wait_ge(xn_high, t + 1)
                dve.tensor_tensor(xn_parts[q][:, 1, :], xn_stage[q][:], xn_parts[q][:, 0, :], ALU.subtract)\
                   .then_inc(xn_low, 1)

            def save_scores(t, q):
                dve.wait_ge(projected, t + 1)
                dve.tensor_scalar(a_all[:, :, bass.ds(t, 1)].rearrange("p h a -> p (h a)"), p_s[q][:, 0:H],
                                  1.0 / WS, None, ALU.mult)
                dve.tensor_scalar(b_all[:, :, bass.ds(t, 1)].rearrange("p h a -> p (h a)"), p_s[q][:, H:2 * H],
                                  1.0 / WS, None, ALU.mult).then_inc(scores_saved, 1)

            def save_rows(pair):
                dve.wait_ge(rows_turned, pair + 1)
                dve.tensor_copy(s_t[:, 2 * pair * P:(2 * pair + 2) * P], p_s[(pair + 1) % 2][0:H, P:3 * P])\
                   .then_inc(rows_saved, 1)

            def fill_empty(b):
                cols = slice(b * 512, (b + 1) * 512)
                dve.wait_ge(counted, b + 1)
                dve.tensor_scalar(empty[:, cols], p_w[b % 2][:], 0.0, None, ALU.is_equal).then_inc(degree_read, 1)
                dve.wait_ge(degree_read, b + 1)
                dve.tensor_tensor(keep["mask"][:, :, cols], keep["mask"][:, :, cols],
                                  empty[:, cols].unsqueeze(1).broadcast_to([P, T, 512]), ALU.max)\
                   .then_inc(mask_filled, 1)

            dve.wait_ge(x_in[0], 16)
            moments(0)
            invert(0)
            norm(0, 0)
            norm(1, 1)
            low(0, 0)
            dve.wait_ge(w_high, 1)
            dve.scalar_tensor_tensor(w_parts[1][:], w_seq[:], WS, w_parts[0][:], ALU.mult, ALU.subtract)\
               .then_inc(w_low, 1)
            dve.wait_ge(v_high, 1)
            dve.scalar_tensor_tensor(v_parts[1][:], v_sb[:], WS, v_parts[0][:], ALU.mult, ALU.subtract)\
               .then_inc(v_low, 1)
            norm(2, 0)
            low(1, 1)

            def tile_pair(i):
                for q in range(2):
                    t = i * 2 + q
                    if tile_there(t + 3):
                        norm(t + 3, 1 - q)
                    if tile_there(t + 2):
                        low(t + 2, q)
                    if tile_there(t - 1):
                        save_scores(t - 1, 1 - q)
                    if isinstance(t, int) and t + 1 < len(GROUPS):
                        for r in range(GROUPS[t + 1][1] // (T // 4)):
                            dve.wait_ge(x_in[r], 16)
                        moments(t + 1)
                        invert(t + 1)
                    if isinstance(t, int) and 0 <= t - DEGREE_AT - 1 < T // 2 - 1:
                        save_rows(t - DEGREE_AT - 1)
                    if isinstance(t, int) and 0 <= t - DEGREE_AT - 1 < N // 512:
                        fill_empty(t - DEGREE_AT - 1)

            rolled(dve, 1, DEGREE_AT // 2, T // 2, tile_pair)
            save_scores(T - 1, 1)
            for pair in range(T - 1 - DEGREE_AT, T // 2):
                save_rows(pair)
            dve.wait_ge(scores_saved, T)
            dve.tensor_reduce(b_max[:], b_all[:], AX.X, ALU.max).then_inc(max_local, 1)
            dve.tensor_scalar(keep["neg_b"][:], b_all[:], -1.0, None, ALU.mult)
            dve_step.did(dve.tensor_scalar(keep["step_b"][:], b_all[:], STEP, None, ALU.mult))
            dve.wait_ge(max_all, 1)
            top = b_top[:].unsqueeze(2).broadcast_to([P, H, T])
            dve_step.settle(dve, dve.tensor_tensor(z[:], a_all[:], top, ALU.add))
            dve_step.settle(dve, dve.tensor_tensor(ea[:], b_all[:], top, ALU.subtract))
            dve_step.settle(dve, dve.tensor_scalar(eb[:], ea[:], ALPHA, None, ALU.mult))
            dve_step.settle(dve, dve.scalar_tensor_tensor(m[:], z[:], ALPHA, z[:], ALU.mult, ALU.max))
            dve_step.settle(dve, dve.scalar_tensor_tensor(b_all[:], z[:], ALPHA, m[:], ALU.mult, ALU.subtract))
            dve_step.settle(dve, dve.tensor_tensor(z[:], z[:], m[:], ALU.subtract))
            dve.tensor_copy(m[:], b_all[:]).then_inc(factors_in, 1)
            dve.wait_ge(mask_filled, N // 512)


def attention_heads(nc, io, dram, keep):
    with ExitStack() as ctx:
        sb, ps, sem = make_tools(nc, ctx)
        SOFT = [[j for j in range(T) if j not in hard] for hard in HARD]
        a_row, rows_in = keep["a_row"], keep["rows_in"]
        pick = [sb(f"pick{r}", [P, N], F16) for r in range(RING)]
        over = [sb(f"over{r}", [P, N], BF16) for r in range(OVER)]
        g32 = sb("g32", [P, T, GW], F32)
        g = [sb(f"g{q}", [P, T, G_COLS], F16) for q in range(2)]
        sums = sb("sums", [P, T, GW], F32)
        acc = ps("acc", [P, BANKS, 512], F32)

        weighted = sem("weighted")
        high_ready = sem("high_ready")
        low_ready = sem("low_ready")
        g_ready = sem("g_ready")
        over_ready = sem("over_ready")
        over_used = sem("over_used")
        pick_used = sem("pick_used")
        head_summed = sem("head_summed")
        low_copied = sem("low_copied")
        paced = sem("paced2")
        bank_read = sem("bank_read")
        combined = sem("combined")
        hard_used = sem("hard_used")
        folded = sem("folded")
        block = ctx.enter_context(nc.Block())
        SP, HP = sum(map(len, SOFT)), sum(map(len, HARD))

        def soft_before(i, q):
            return i * SP + q * len(SOFT[0])

        def hard_before(i, q):
            return i * HP + q * len(HARD[0])

        mask, seq = keep["mask"], keep["seq"]

        def full_banks(s):
            return acc[:, 0:BANKS - 1, 0:PER_BANK * 2 * GW].rearrange("p b (r s c) -> p b r s c", s=2, c=GW)[:, :, :, s, :]

        def by_bank(a):
            return a[:, 0:T - 1, :].rearrange("p (b r) c -> p b r c", r=PER_BANK)

        @block.sync
        def _(sp):
            with sp.Fori(1, H // 2) as i:
                for q in range(2):
                    h = i * 2 + q
                    sp.wait_ge(over_ready, soft_before(i - 1, q) + len(SOFT[q]))
                    sp.sem_inc(paced, 1)
                    sp.wait_ge(hard_used, hard_before(i - 1, q) + len(HARD[q]))
                    sp.sem_inc(paced, 1)
                    sp.dma_start(a_row[q][:], dram["a_rows"][bass.ds(h, 1), :].broadcast_to([P, N]))\
                      .then_inc(rows_in[q], 16)

        @block.scalar
        def _(act):
            def high_part(h, q):
                act.wait_ge(weighted, (h + 1) * 4)
                act.activation(g[q][:, :, 0:GW], g32[:], ACT.Copy).then_inc(high_ready, 1)

            def turned_part(h, q):
                act.wait_ge(low_ready, h + 1)
                act.activation(g[q][:, :, 2 * GW:3 * GW].rearrange("p t (s c) -> p t s c", s=2),
                               g[q][:, :, 0:2 * GW].rearrange("p t (s c) -> p t s c", s=2)[:, :, :, DH + 1:GW],
                               ACT.Copy, scale=-1.0).then_inc(g_ready, 1)

            def copy_low(h):
                act.wait_ge(head_summed, h + 1)
                wait_from(act, combined, h)
                act.activation(by_bank(sums), full_banks(1), ACT.Copy).then_inc(low_copied, 1)
                act.activation(sums[:, T - 1, :], acc[:, BANKS - 1, GW:2 * GW], ACT.Copy).then_inc(low_copied, 1)

            high_part(0, 0)

            def heads(i, first, last):
                for q in range(2):
                    h = i * 2 + q
                    act.wait_ge(rows_in[q], (i + 1) * 16)
                    for n, j in enumerate(SOFT[q]):
                        o = soft_before(0, q) + n
                        if not (first and o < OVER):
                            act.wait_ge(over_used, soft_before(i, q) + (n - OVER + 1))
                        act.activation(over[o % OVER][:], a_row[q][:], ACT.Relu, scale=STEP,
                                       bias=keep["step_b"][:, bass.ds(h * T + j, 1)]).then_inc(over_ready, 1)
                        if n == 0 and first and q == 0:
                            turned_part(0, 0)
                        if n == COPY_AT and not (first and q == 0):
                            copy_low(h - 1)
                        if n == HIGH_AT and not (last and q == 1):
                            high_part(h + 1, 1 - q)
                        if n == TURN_AT and not (last and q == 1):
                            turned_part(h + 1, 1 - q)

            peeled_both(act, H // 2, heads)
            copy_low(H - 1)

        @block.vector
        def _(dve):
            def operand(h, first):
                if not first:
                    dve.wait_ge(low_ready, h)
                for s, e in enumerate(("e_pos", "e_neg")):
                    w = keep[e][:, bass.ds(h * T, T)]
                    lo = s * (DH + 1)
                    dve.scalar_tensor_tensor(
                        g32[:, :, lo:lo + DH], seq[:].rearrange("p (t d) -> p t d", t=T)[:, :, bass.ds(h * DH, DH)],
                        GSCALE, w.unsqueeze(2).broadcast_to([P, T, DH]), ALU.mult, ALU.mult).then_inc(weighted, 1)
                    dve.tensor_scalar(g32[:, :, lo + DH], w, GSCALE, None, ALU.mult).then_inc(weighted, 1)

            def low_part(h, q):
                dve.wait_ge(high_ready, h + 1)
                dve.tensor_tensor(g[q][:, :, GW:2 * GW], g32[:], g[q][:, :, 0:GW], ALU.subtract).then_inc(low_ready, 1)

            def fold(h):
                dve.wait_ge(low_copied, (h + 1) * 2)
                dve.tensor_tensor(by_bank(sums), by_bank(sums), full_banks(0), ALU.add).then_inc(bank_read, 1)
                dve.tensor_tensor(sums[:, T - 1, :], sums[:, T - 1, :], acc[:, BANKS - 1, 0:GW],
                                  ALU.add).then_inc(bank_read, 1)

            def combine(h):
                dve.wait_ge(bank_read, (h + 1) * 2)
                for s, f in enumerate(("f_pos", "f_neg")):
                    part = sums[:, :, s * (DH + 1):(s + 1) * (DH + 1)]
                    w = keep[f][:, bass.ds(h * T, T)]
                    dve.tensor_tensor(part, part, w.unsqueeze(2).broadcast_to([P, T, DH + 1]),
                                      ALU.mult).then_inc(folded, 1)
                dve.wait_ge(folded, h * 2 + 2)
                dve.tensor_tensor(keep["hidden"][:, :, bass.ds(h * (DH + 1), DH + 1)],
                                  sums[:, :, 0:DH + 1], sums[:, :, DH + 1:GW], ALU.subtract).then_inc(combined, 1)

            operand(0, True)
            low_part(0, 0)

            def heads(i, first, last):
                for q in range(2):
                    h = i * 2 + q
                    dve.wait_ge(rows_in[q], (i + 1) * 16)
                    n = 0
                    for j in range(T):
                        slot = (q * T + j) % RING
                        if not (first and q * T + j < RING):
                            dve.wait_ge(pick_used, h * T + j - RING + 1)
                        if j in SOFT[q]:
                            dve.wait_ge(over_ready, soft_before(i, q) + (n + 1))
                            op = dve.tensor_tensor(pick[slot][:], over[(soft_before(0, q) + n) % OVER][:],
                                                   mask[:, j, :], ALU.min)
                            op.then_inc(over_used, 1)
                            n += 1
                        else:
                            op = dve.scalar_tensor_tensor(pick[slot][:], a_row[q][:],
                                                          keep["neg_b"][:, bass.ds(h * T + j, 1)], mask[:, j, :],
                                                          ALU.is_gt, ALU.mult)
                            op.then_inc(hard_used, 1)
                        if j == FOLD_AT and not (first and q == 0):
                            fold(h - 1)
                        if j == OPERAND_AT and not (last and q == 1):
                            operand(h + 1, False)
                        if j == LOW_AT and not (last and q == 1):
                            low_part(h + 1, 1 - q)
                        if j == COMBINE_AT and not (first and q == 0):
                            combine(h - 1)
            peeled_both(dve, H // 2, heads)
            fold(H - 1)
            combine(H - 1)

        @block.tensor
        def _(pe):
            def heads(i, first):
                for q in range(2):
                    h = i * 2 + q
                    pe.wait_ge(g_ready, h + 1)
                    for j in range(T):
                        slot = (q * T + j) % RING
                        if j in SOFT[q]:
                            pe.wait_ge(over_used, soft_before(i, q) + (SOFT[q].index(j) + 1))
                        else:
                            pe.wait_ge(hard_used, hard_before(i, q) + (HARD[q].index(j) + 1))
                        for t in range(T):
                            b, r = divmod(t, PER_BANK)
                            if j == 0 and t in (0, T - 1) and not (first and q == 0):
                                pe.wait_ge(bank_read, (h - 1) * 2 + (2 if t else 1))
                            out = acc[:, b, r * 2 * GW:(r + 1) * 2 * GW]
                            mm = pe.matmul(out, pick[slot][:, t * P:(t + 1) * P], g[q][:, j, 0:2 * GW],
                                           start=(j == 0 and r == 0), stop=False, skip_group_check=True)
                            if t == T - 1:
                                mm.then_inc(pick_used, 1)
                            mm = pe.matmul(out.rearrange("p (s c) -> p s c", s=2)[:, :, DH + 1:GW],
                                           mask[:, j, t * P:(t + 1) * P],
                                           g[q][:, j, 2 * GW:3 * GW].rearrange("p (s c) -> p s c", s=2),
                                           start=False, stop=(j == T - 1), skip_group_check=True)
                    mm.then_inc(head_summed, 1)
            peeled(pe, H // 2, heads)


def output_projection(nc, io, dram, keep, ident):
    with ExitStack() as ctx:
        sb, ps, sem = make_tools(nc, ctx)
        hidden, x1, x_parts = keep["hidden"], keep["x1"], keep["x_parts"]
        rden = sb("rden", [P, T, H], F32)
        halves = [slice(0, KC // 2), slice(KC // 2, KC)]
        w_out = [sb(f"w_out{half}", [P, KC // 2, D], F32) for half in range(2)]
        w_route = sb("w_route", [P, KC, E + 1], F32)
        wo = [sb(f"wo{r}", [P, KC, D], F16) for r in range(2)]
        wr = [sb(f"wr{r}", [P, KC, E + 1], F16) for r in range(2)]
        b_out = sb("b_out", [P, D], F32)
        heads = [sb(f"heads{q}", [P, D], F32) for q in range(2)]
        parts = [sb(f"parts{q}", [P, 2, D], F16) for q in range(2)]
        parts_t = [sb(f"parts_t{q}", [P, 2, KC, P], F16) for q in range(2)]
        x_in_tile = [sb(f"x_in_tile{q}", [P, D], F32) for q in range(2)]
        y = [sb(f"y{q}", [P, D], F32) for q in range(2)]
        below = [sb(f"below{q}", [P, D], F32) for q in range(2)]
        row_parts = parts + [a[:].rearrange("p r c m -> p r (c m)") for a in parts_t]
        stats = sb("stats2", [P, T, 6], F32)
        mv = sb("mv2", [P, T, 2], F32)
        var = sb("var2", [P, T], F32)
        std = sb("std2", [P, T], F32)
        rstd = sb("rstd2", [P, T], F32)
        p_t = [ps(f"p_t{q}", [P, 2 * D], F16) for q in range(2)]
        p_y = [ps(f"p_y{q}", [P, 512], F32) for q in range(2)]
        p_l = [ps(f"p_l{q}", [P, 512], F32) for q in range(2)]

        w_in = [sem(f"w_out_in{half}") for half in range(2)]
        b_in, r_in = sem("b_out_in"), sem("w_route_in")
        x_in = [sem(f"x_in_tile{q}") for q in range(2)]
        paced = sem("paced3")
        wo_high, wo_low = sem("wo_high"), sem("wo_low")
        rden_ready = sem("rden_ready")
        scaled, high_ready, low_ready = sem("head_scaled"), sem("head_high"), sem("head_low")
        head_turned, parts_t_ready = sem("head_turned"), sem("parts_t_ready")
        projected, biased = sem("out_projected"), sem("biased")
        negated, below_ready, above_added = sem("negated"), sem("below_ready"), sem("above_added")
        x1_ready, stats_ready = sem("x1_ready"), sem("stats_ready")
        var_ready, std_ready, rstd_ready = sem("var2_ready"), sem("std2_ready"), sem("rstd2_ready")
        normed, x_high, x_low = sem("normed2"), sem("x_high_made"), sem("x_low_made")
        rows_saved = [sem(f"xn_saved{q}") for q in range(4)]
        turned, x_parts_ready = sem("turned2"), sem("x_parts_ready")
        routed, logits_saved = sem("routed"), sem("logits_saved")
        block = ctx.enter_context(nc.Block())

        def flat(a):
            return a.rearrange("p a d -> p (a d)")

        def tile(a, t):
            return flat(a[:, bass.ds(t, 1), :])

        @block.sync
        def _(sp):
            for half in range(2):
                sp.dma_start(w_out[half][:], io["w_out"].rearrange("(c p) k -> p c k", p=P)[:, halves[half], :])\
                  .then_inc(w_in[half], 16)
            sp.dma_start(b_out[:], io["b_out"].broadcast_to([P, D])).then_inc(b_in, 16)
            for q in range(2):
                sp.dma_start(x_in_tile[q][:], io["x"][q * P:(q + 1) * P, :]).then_inc(x_in[q], 16)
            sp.dma_start(w_route[:], io["w_route"].rearrange("(c p) e -> p c e", p=P)).then_inc(r_in, 16)
            with sp.Fori(1, T // 2) as i:
                for q in range(2):
                    t = i * 2 + q
                    sp.wait_ge(above_added, t - 1)
                    sp.sem_inc(paced, 1)
                    sp.dma_start(x_in_tile[q][:], io["x"][bass.ds(t * P, P), :]).then_inc(x_in[q], 16)

            def rows(i, first):
                for q in range(4):
                    t = i * 4 + q
                    sp.wait_ge(x_low, t + 1)
                    sp.sem_inc(paced, 1)
                    sp.dma_start(dram["xn_rows"][bass.ds(t * P, P), :], flat(row_parts[q][:]))\
                      .then_inc(rows_saved[q], 16)
            for f in range(4):
                sp.dma_start(keep["s_raw"][f], io["w_shared"][f].rearrange("p a d -> p (a d)"))\
                  .then_inc(keep["w_in"][f], 16)
            peeled(sp, T // 4, rows)
            for q in range(4):
                sp.wait_ge(rows_saved[q], 16 * (T // 4))

        @block.tensor
        def _(pe):
            def turn(t, q, source, low, copied, done):
                pe.wait_ge(low, t + 1)
                wait_from(pe, copied, t - 1)
                for r in range(2):
                    for c in range(KC):
                        tr = pe.transpose(p_t[q][:, (r * KC + c) * P:(r * KC + c + 1) * P],
                                          source[:, r, c * P:(c + 1) * P], keep["ident16"][:])
                tr.then_inc(done, 1)

            turn(0, 0, parts[0], low_ready, parts_t_ready, head_turned)
            pe.wait_ge(wo_low, 1)

            def project(i):
                for q in range(2):
                    t = i * 2 + q
                    if tile_there(t + 1):
                        turn(t + 1, 1 - q, parts[1 - q], low_ready, parts_t_ready, head_turned)
                    pe.wait_ge(parts_t_ready, t + 1)
                    wait_from(pe, biased, t - 1)
                    n = 0
                    for c in range(KC):
                        if isinstance(t, int) and t == 0 and c == KC // 2:
                            pe.wait_ge(wo_low, 2)
                        for a, b in ((0, 0), (0, 1), (1, 0)):
                            mm = pe.matmul(p_y[q][:], parts_t[q][:, a, c, :], wo[b][:, c, :],
                                           start=(n == 0), stop=(n == 3 * KC - 1))
                            n += 1
                    mm.then_inc(projected, 1)
            rolled(pe, 1, T // 2 - 2, T // 2, project)

            pe.wait_ge(wo_low, 3)
            turn(0, 0, row_parts[0], x_low, x_parts_ready, turned)

            def route(i):
                for r in range(4):
                    t, q = i * 4 + r, r % 2
                    if tile_there(t + 1):
                        turn(t + 1, 1 - q, row_parts[(r + 1) % 4], x_low, x_parts_ready, turned)
                    pe.wait_ge(x_parts_ready, t + 1)
                    wait_from(pe, logits_saved, t - 1)
                    n = 0
                    for c in range(KC):
                        for a, b in ((0, 0), (0, 1), (1, 0)):
                            mm = pe.matmul(p_l[q][:, 0:E + 1], x_parts[:, a, c, bass.ds(t * P, P)], wr[b][:, c, :],
                                           start=(n == 0), stop=(n == 3 * KC - 1))
                            n += 1
                    mm.then_inc(routed, 1)
            rolled(pe, 1, T // 4 - 1, T // 4, route)

        @block.scalar
        def _(act):
            def high(t, q):
                act.wait_ge(scaled, t + 1)
                wait_from(act, head_turned, t - 1)
                act.activation(parts[q][:, 0, :], heads[q][:], ACT.Copy).then_inc(high_ready, 1)

            high(0, 0)
            high(1, 1)
            for half in range(2):
                act.wait_ge(w_in[half], 16)
                act.activation(wo[0][:, halves[half], :], w_out[half][:], ACT.Copy, scale=WS).then_inc(wo_high, 1)
            act.wait_ge(r_in, 16)
            act.activation(wr[0][:], w_route[:], ACT.Copy, scale=WS).then_inc(wo_high, 1)

            def copy_turned(t, q):
                act.wait_ge(head_turned, t + 1)
                wait_from(act, projected, t - 1)
                act.activation(parts_t[q][:].rearrange("p r c m -> p (r c m)"), p_t[q][:], ACT.Copy)\
                   .then_inc(parts_t_ready, 1)

            copy_turned(0, 0)
            high(2, 0)

            def elu_below(t, q):
                act.wait_ge(biased, t + 1)
                wait_from(act, x1_ready, t - 1)
                act.activation(below[q][:], y[q][:], ACT.Relu, scale=-1.0).then_inc(negated, 1)
                act.wait_ge(negated, t + 1)
                act.activation(below[q][:], below[q][:], ACT.Exp, scale=-1.0).then_inc(below_ready, 1)

            def project(i):
                for q in range(2):
                    t = i * 2 + q
                    if tile_there(t + 1):
                        copy_turned(t + 1, 1 - q)
                    if tile_there(t + 3):
                        high(t + 3, 1 - q)
                    if tile_there(t - 1):
                        elu_below(t - 1, 1 - q)
            rolled(act, 1, T // 2 - 2, T // 2, project)
            elu_below(T - 1, 1)
            act.wait_ge(var_ready, 1)
            act.activation(std[:], var[:], ACT.Sqrt).then_inc(std_ready, 1)

            def spread(t, q):
                act.wait_ge(turned, t + 1)
                act.activation(x_parts[:, :, :, bass.ds(t * P, P)].rearrange("p r c m -> p (r c) m"),
                               p_t[q][:].rearrange("p (g m) -> p g m", m=P), ACT.Copy).then_inc(x_parts_ready, 1)

            def high_row(t, r, quad):
                act.wait_ge(normed, t + 1)
                wait_from(act, rows_saved[r], quad * 16)
                wait_from(act, turned, t - 3)
                act.activation(row_parts[r][:, 0, :], heads[r % 2][:], ACT.Copy).then_inc(x_high, 1)

            high_row(0, 0, 0)
            high_row(1, 1, 0)
            spread(0, 0)
            high_row(2, 2, 0)

            def route(i):
                for r in range(4):
                    t = i * 4 + r
                    if tile_there(t + 1):
                        spread(t + 1, (r + 1) % 2)
                    if tile_there(t + 3):
                        high_row(t + 3, (r + 3) % 4, i + (r + 3) // 4)
            rolled(act, 1, T // 4 - 1, T // 4, route)
            for f in range(2):
                act.wait_ge(keep["w_in"][f], 16)
                act.activation(flat(keep["w_sh"][0][:, f, :, :]), keep["s_raw"][f], ACT.Copy, scale=WS)\
                   .then_inc(keep["w_high_ready"], 1)

        @block.vector
        def _(dve):
            dens = hidden[:].rearrange("p t (h c) -> p t h c", h=H)[:, :, :, DH]
            dve.reciprocal(rden[:], dens).then_inc(rden_ready, 1)
            dve.wait_ge(rden_ready, 1)

            def low(t, q, to, made_high, made):
                dve.wait_ge(made_high, t + 1)
                dve.tensor_tensor(to[:, 1, :], heads[q][:], to[:, 0, :], ALU.subtract).then_inc(made, 1)

            def scale(t, q):
                wait_from(dve, low_ready, t - 1)
                dve.tensor_tensor(
                    heads[q][:].rearrange("p (h d) -> p h d", h=H),
                    hidden[:, bass.ds(t, 1), :].rearrange("p a (h c) -> p (a h) c", h=H)[:, :, 0:DH],
                    tile(rden, t).unsqueeze(2).broadcast_to([P, H, DH]), ALU.mult).then_inc(scaled, 1)

            scale(0, 0)
            scale(1, 1)
            low(0, 0, parts[0], high_ready, low_ready)
            for n, (hi, lo, raw) in enumerate((
                    (wo[0][:, halves[0], :], wo[1][:, halves[0], :], w_out[0][:]),
                    (wo[0][:, halves[1], :], wo[1][:, halves[1], :], w_out[1][:]),
                    (wr[0][:], wr[1][:], w_route[:]))):
                dve.wait_ge(wo_high, n + 1)
                dve.scalar_tensor_tensor(lo, raw, WS, hi, ALU.mult, ALU.subtract).then_inc(wo_low, 1)
            scale(2, 0)
            low(1, 1, parts[1], high_ready, low_ready)
            dve.wait_ge(b_in, 16)

            def finish(t, q):
                row = tile(x1, t)
                dve.wait_ge(below_ready, t + 1)
                dve.wait_ge(above_added, t + 1)
                dve.scalar_tensor_tensor(row, below[q][:], -1.0, row, ALU.add, ALU.add).then_inc(x1_ready, 1)
                dve.wait_ge(x1_ready, t + 1)
                dve.bn_stats(tile(stats, t), row).then_inc(stats_ready, 1)

            def add_bias(t, q):
                dve.wait_ge(projected, t + 1)
                wait_from(dve, above_added, t - 1)
                wait_from(dve, negated, t - 1)
                dve.scalar_tensor_tensor(y[q][:], p_y[q][:], 1.0 / WS, b_out[:], ALU.mult, ALU.add)\
                   .then_inc(biased, 1)

            def add_above(t, q, pair):
                dve.wait_ge(biased, t + 1)
                dve.wait_ge(x_in[q], pair * 16 + 16)
                dve.scalar_tensor_tensor(tile(x1, t), y[q][:], 0.0, x_in_tile[q][:], ALU.max, ALU.add)\
                   .then_inc(above_added, 1)

            def project(i):
                for q in range(2):
                    t = i * 2 + q
                    if tile_there(t + 2):
                        low(t + 2, q, parts[q], high_ready, low_ready)
                    if tile_there(t - 1):
                        add_bias(t - 1, 1 - q)
                    if tile_there(t + 3):
                        scale(t + 3, 1 - q)
                    if tile_there(t - 1):
                        add_above(t - 1, 1 - q, i - 1 + q)
                    if tile_there(t - 2):
                        finish(t - 2, q)
            rolled(dve, 1, T // 2 - 2, T // 2, project)
            add_bias(T - 1, 1)
            add_above(T - 1, 1, T // 2 - 1)
            finish(T - 2, 0)
            finish(T - 1, 1)
            dve.wait_ge(stats_ready, T)
            for t in range(T):
                last = dve.bn_aggr(mv[:, t, :], stats[:, t, :])
            last.then_inc(stats_ready, 1)
            dve.wait_ge(stats_ready, T + 1)
            dve.tensor_scalar(var[:], mv[:, :, 1], EPS, None, ALU.add).then_inc(var_ready, 1)
            dve.wait_ge(std_ready, 1)
            dve.reciprocal(rstd[:], std[:]).then_inc(rstd_ready, 1)
            dve.wait_ge(rstd_ready, 1)

            def norm(t, q):
                wait_from(dve, x_low, t - 1)
                dve.tensor_scalar(heads[q][:], tile(x1, t), mv[:, bass.ds(t, 1), 0], rstd[:, bass.ds(t, 1)],
                                  ALU.subtract, ALU.mult).then_inc(normed, 1)

            def save_logits(t, q):
                dve.wait_ge(routed, t + 1)
                dve.tensor_scalar(tile(keep["logits"], t), p_l[q][:, 0:E + 1], 1.0 / WS, None, ALU.mult)\
                   .then_inc(logits_saved, 1)

            norm(0, 0)
            norm(1, 1)
            low(0, 0, row_parts[0], x_high, x_low)
            norm(2, 0)
            low(1, 1, row_parts[1], x_high, x_low)

            def route(i):
                for r in range(4):
                    t, q = i * 4 + r, r % 2
                    if tile_there(t + 3):
                        norm(t + 3, 1 - q)
                    if tile_there(t + 2):
                        low(t + 2, q, row_parts[(r + 2) % 4], x_high, x_low)
                    if tile_there(t - 1):
                        save_logits(t - 1, 1 - q)
            rolled(dve, 1, T // 4 - 1, T // 4, route)
            save_logits(T - 1, 1)
            for f in range(2):
                dve.wait_ge(keep["w_high_ready"], f + 1)
                dve.scalar_tensor_tensor(flat(keep["w_sh"][1][:, f, :, :]), keep["s_raw"][f], WS,
                                         flat(keep["w_sh"][0][:, f, :, :]), ALU.mult, ALU.subtract)\
                   .then_inc(keep["w_low_ready"], 1)


def feed_forward(nc, io, dram, keep, ident, out):
    with ExitStack() as ctx:
        sb, ps, sem = make_tools(nc, ctx)

        def flat(a):
            return a.rearrange("p a d -> p (a d)")

        x1, x_parts, logits = keep["x1"], keep["x_parts"], keep["logits"]
        ident16 = keep["ident16"]

        count_e = sb("count_e", [P, P], F32)
        before = sb("before", [P, P], F16)
        ones = sb("ones2", [P, P], F16)
        upto = sb("upto", [P, E, E], F32)
        raw = sb("raw", [P, T, E], F32)
        key = sb("key", [P, T, E], F32)
        hit = [sb(f"hit{k}", [P, T, E], F32) for k in range(2)]
        top = [sb(f"top{k}", [P, T], F32) for k in range(2)]
        low_key = sb("low_key", [P, T], F32)
        both_led = sb("both_led", [P, T + 1, E], F16)
        both = both_led[:, 1:T + 1, :]
        ratio = sb("ratio", [P, T], F32)
        share = [sb(f"share{k}", [P, T], F32) for k in range(2)]
        sgate = sb("sgate", [P, T], F32)
        held = sb("held", [P, E], F32)
        cube, place = raw, key
        tiles = sb("tiles", [P, E], F32)
        ends = sb("ends", [P, E], F32)
        base = sb("base", [P, E], F32)
        owner_f = sb("owner_f", [P, SLOTS], F32)
        owner = sb("owner", [P, SLOTS], I32)
        many = sb("many", [P, 1], I32)
        row_f = [sb(f"row_f{k}", [P, T], F32) for k in range(2)]
        row_i = [sb(f"row_i{k}", [P, T], I32) for k in range(2)]
        in_tile = [sb(f"in_tile{k}", [P, T], I32) for k in range(2)]
        in_tile_f = [sb(f"in_tile_f{k}", [P, T], F32) for k in range(2)]
        slot_f = [sb(f"slot_f{k}", [P, T], F32) for k in range(2)]
        count16 = sb("count16", [P, P], F16)
        node16 = sb("node16", [P, T], F16)
        in_tile16 = [sb(f"in_tile16{k}", [P, T], F16) for k in range(2)]
        slot16 = [sb(f"slot16{k}", [P, T], F16) for k in range(2)]
        tokens = sb("tokens", [P, SLOTS], I32)

        w_raw, s_raw = keep["w_raw"], keep["s_raw"]
        gu_raw = [w[:, 0:KC * D].rearrange("p (c f) -> p c f", c=KC) for w in w_raw]
        dn_raw = [w[:, KC * D:6 * D].rearrange("p (c f) -> p c f", c=FE // P) for w in w_raw]
        y_buf = [w_raw[b // 6][:, (b % 6) * D:(b % 6 + 1) * D] for b in range(Y_BUFS)]

        w_sh = keep["w_sh"]
        silu = [sb(f"silu{q}", [P, BLK], F32) for q in range(2)]
        act32 = sb("act32", [P, BLK], F32)
        a_parts = [sb(f"a_parts{q}", [P, 2, BLK], F16) for q in range(2)]

        gu16 = sb("gu16", [P, 2, KC, 2 * FE], F16)
        dn16 = sb("dn16", [P, 2, FE // P, D], F16)
        pick_now = [sb(f"pick_now{q}", [P, 1], I32) for q in range(2)]
        xg = [sb(f"xg{q}", [P, 2, D], F16) for q in range(2)]
        xg_t = sb("xg_t", [P, 2, KC, P], F16)
        e_silu = sb("e_silu", [P, FE], F32)
        e_act = sb("e_act", [P, FE], F32)
        e_parts = [sb(f"e_parts{q}", [P, 2, FE], F16) for q in range(2)]
        e_parts_t = sb("e_parts_t", [P, 2, FE // P, P], F16)
        y_out = [sb(f"y_out{q}", [P, D], F32) for q in range(2)]
        past = sb("past", [P, SLOTS, E], F32)
        zeros = flat(past[:])[:, 0:D]
        at_row = [xg[q][:].rearrange("p r (m c) -> p r m c", c=P) for q in range(2)]
        at_slot = [flat(e_parts[q][:])[:, 0:MARKS * SLOTS].rearrange("p (r m s) -> p r m s", r=2, s=SLOTS)
                   for q in range(2)]

        p_gu = [ps(f"p_gate_up{q}", [P, 512], F32) for q in range(2)]
        p_dn = [ps(f"p_down{m}", [P, 512], F32) for m in range(TB)]
        p_xt = ps("p_x_turned", [P, 1024], F16)
        p_egu = ps("p_expert_gate_up", [P, 512], F32)
        p_at = ps("p_act_turned", [P, 1024], F16)
        p_y = ps("p_expert_down", [P, 512], F32)
        rank = p_egu[:, 0:T * E].rearrange("p (t e) -> p t e", t=T)
        total = p_egu[:, T * E:T * E + E]
        token_table = p_y[:, 0:SLOTS]

        consts_ready = sem("consts_ready")
        dve_step = Steps(sem("route_step"))
        pool_step = Steps(sem("pool_const_step"))
        exps_in, exps_out = sem("exps_in"), sem("exps_out")
        both_ready, ranked = sem("both_ready"), sem("ranked")
        marked, mark_used = sem("marked"), sem("mark_used")
        slots_counted = sem("slots_counted")
        zeros_ready, unused_saved = sem("zeros_ready"), sem("unused_saved")
        owner_ready, tokens_ready = sem("owner_ready"), sem("tokens_ready")
        w_in = keep["w_in"]
        w_high_ready, w_low_ready = keep["w_high_ready"], keep["w_low_ready"]
        gated, silu_ready, act_ready = sem("gated"), sem("silu_ready"), sem("act_ready")
        a_high_ready, a_low_ready = sem("a_high_ready"), sem("a_low_ready")
        downed, added = sem("downed"), sem("added")
        gu_in = [sem(f"gu_in{q}") for q in range(2)]
        dn_in = [sem(f"dn_in{q}") for q in range(2)]
        gu_high, gu_low, dn_high, dn_low = sem("gu_high"), sem("gu_low"), sem("dn_high"), sem("dn_low")
        pick_set, gathered = sem("pick_set"), [sem(f"gathered{q}") for q in range(2)]
        e_turned, xg_t_ready = sem("e_turned"), sem("xg_t_ready")
        e_gated, e_silu_ready, e_act_ready = sem("e_gated"), sem("e_silu_ready"), sem("e_act_ready")
        e_high_ready, e_low_ready = sem("e_high_ready"), sem("e_low_ready")
        e_act_turned, e_act_t_ready = sem("e_act_turned"), sem("e_act_t_ready")
        e_downed, y_ready, y_saved = sem("e_downed"), sem("y_ready"), [sem(f"y_saved{q}") for q in range(2)]
        paced, pool_paced = sem("paced"), sem("pool_paced")
        y_in = [sem(f"y_in{b}") for b in range(Y_BUFS // 2)]
        y_added = sem("y_added")
        out_saved = sem("out_saved")
        block = ctx.enter_context(nc.Block())

        steps = [("G", 0)]
        for f in range(1, FC):
            steps += [("G", f), ("D", f - 1)]
        steps += [("D", FC - 1)]

        def back(f):
            return 2 if f >= 2 else (1 if f == 0 else 3)

        def slot(i, k):
            return i * PER_BLOCK + (k - PER_BLOCK), i * (PER_BLOCK // 2) + (k // 2 - PER_BLOCK // 2)

        def real(s, used=SLOTS):
            return not isinstance(s, int) or 0 <= s < used

        def by_need(eng, body):
            eng.wait_ge(slots_counted, 1)
            more = eng.value_load(many[0:1, 0:1], min_val=0, max_val=1)
            with eng.If(more > 0):
                body(SLOTS)
            with eng.Else():
                body(FEW)

        def all_blocks(eng, body):
            for i in (0, 1):
                body(i)
            with eng.Fori(2, SLOT_BLOCKS) as i:
                body(i)

            def last_blocks(used):
                for i in (SLOT_BLOCKS, BLOCKS - 1):
                    body(i, used)
            by_need(eng, last_blocks)

        def places(i):
            for g in range(3 * PER_BLOCK):
                yield g // 3, g % 3, (steps[g] if g < len(steps) else None)

        def row_of(t):
            return flat(x1[:, bass.ds(t, 1), :])

        @block.sync
        def _(sp):
            for f in range(4, FC):
                sp.wait_ge(w_low_ready, f - 3)
                sp.dma_start(s_raw[f % 4], io["w_shared"][f].rearrange("p a d -> p (a d)")).then_inc(w_in[f % 4], 16)

            def load(s, q, which):
                raw_w, source, landed = (gu_raw, "w_gate_up", gu_in) if which == 0 else (dn_raw, "w_down", dn_in)
                e = sp.value_load(owner[0:1, bass.ds(s, 1)], min_val=0, max_val=E - 1)
                sp.dma_start(raw_w[q], io[source][bass.ds(e, 1)].rearrange("a (c p) f -> p (a c) f", p=P))\
                  .then_inc(landed[q], 16)

            def save(s, q):
                sp.wait_ge(y_ready, s + 1)
                sp.sem_inc(paced, 1)
                sp.dma_start(dram["y_rows"][bass.ds(s * P, P), :], y_out[q][:]).then_inc(y_saved[q], 16)

            sp.wait_ge(owner_ready, 1)
            for s in range(2):
                sp.wait_ge(w_low_ready, FC - 1 + s)
                load(s, s, 0)
                load(s, s, 1)
            sp.wait_ge(gu_low, 2)
            load(2, 0, 0)

            def slots(i, used=SLOTS):
                for k in range(PER_BLOCK):
                    s, _ = slot(i, k)
                    if real(s + 3, used):
                        sp.wait_ge(gu_low, s * 2 + 4)
                        sp.sem_inc(paced, 1)
                        load(s + 3, (k + 1) % 2, 0)
                    if real(s - 1, used):
                        save(s - 1, (k + 1) % 2)
                    if real(s + 2, used):
                        sp.wait_ge(dn_low, s + 1)
                        sp.sem_inc(paced, 1)
                        load(s + 2, k % 2, 1)
            slots(1)
            with sp.Fori(2, SLOT_BLOCKS) as i:
                slots(i)
            def last_slots(used):
                if used == FEW:
                    sp.wait_ge(zeros_ready, 1)
                    sp.dma_start(dram["y_rows"][FEW * P:SLOTS * P, :].rearrange("(s p) d -> p s d", p=P),
                                 zeros.unsqueeze(1).broadcast_to([P, SLOTS - FEW, D])).then_inc(unused_saved, 16)
                slots(SLOT_BLOCKS, used)
                if used == SLOTS:
                    save(SLOTS - 1, (SLOTS - 1) % 2)
            by_need(sp, last_slots)
            for t in range(T):
                sp.wait_ge(y_added, 2 * t + 2)
                sp.dma_start(out[t * P:(t + 1) * P, :], x1[:, t, :]).then_inc(out_saved, 16)
            sp.wait_ge(out_saved, 16 * T)

        @block.gpsimd
        def _(pool):
            pool_step.did(pool.iota(flat(past[:, 0:P // E, :]).bitcast(I32),
                                    pattern=[[1, P]], base=0, channel_multiplier=0))
            pool_step.settle(pool, pool.iota(row_i[0][:], pattern=[[P, T]], base=0, channel_multiplier=1))
            pool.tensor_copy(count_e[:], flat(past[:, 0:P // E, :]).bitcast(I32)).then_inc(consts_ready, 1)
            pool.tensor_copy(count16[:], flat(past[:, 0:P // E, :]).bitcast(I32)).then_inc(consts_ready, 1)
            pool.tensor_copy(node16[:], row_i[0][:]).then_inc(consts_ready, 1)
            pool.memset(ones[:], 1.0).then_inc(consts_ready, 1)
            pool.memset(both_led[:, 0, :], 0.0).then_inc(consts_ready, 1)
            pool_step.did(pool.memset(before[:], 1.0))
            pool_step.settle(pool, pool.memset(upto[:], 1.0))
            pool.affine_select(out=before[:], in_=before[:], compare_op=ALU.is_gt, fill=0.0, base=0,
                               pattern=[[1, P]], channel_multiplier=-1).then_inc(consts_ready, 1)
            pool.affine_select(out=upto[:], in_=upto[:], compare_op=ALU.is_ge, fill=0.0, base=0,
                               pattern=[[1, E], [-1, E]], channel_multiplier=0).then_inc(consts_ready, 1)
            pool.wait_ge(tokens_ready, 1)
            pool.memset(zeros, 0.0).then_inc(zeros_ready, 1)

            def slots(i, first):
                for q in range(2):
                    s = i * 2 + q
                    if not first:
                        pool.wait_ge(e_turned, s - 1)
                    pool.tensor_copy(pick_now[q][:], tokens[:, bass.ds(s, 1)]).then_inc(pick_set, 1)
                    pool.wait_ge(pick_set, s + 1)
                    pool.sem_inc(pool_paced, 1)
                    pool.indirect_dma_start(out=flat(xg[q][:]), out_offset=None, in_=dram["xn_rows"],
                                            in_offset=bass.IndirectOffsetOnAxis(ap=pick_now[q][:], axis=0))\
                        .then_inc(gathered[q], 16)
            peeled(pool, FEW // 2 + 1, slots)

            def last_slots(used):
                if used == SLOTS:
                    with pool.Fori(FEW // 2 + 1, SLOTS // 2) as i:
                        slots(i, False)
                else:
                    pool.wait_ge(unused_saved, 16)
                    pool.wait_ge(gu_low, 2 * (FEW + 1))
                    for q in range(2):
                        pool.wait_ge(gu_in[q], 16 * ((FEW + 3 + 1 - q) // 2))
                        pool.wait_ge(dn_in[q], 16 * (FEW // 2 + 1))
                        pool.wait_ge(gathered[q], 16 * (FEW // 2 + 1))
                for q in range(2):
                    pool.wait_ge(y_saved[q], 16 * (used // 2))
            by_need(pool, last_slots)

            for n in range(2 * T):
                t, k = divmod(n, 2)
                if n >= Y_BUFS:
                    pool.wait_ge(y_added, n - Y_BUFS + 1)
                pool.indirect_dma_start(out=y_buf[n % Y_BUFS], out_offset=None, in_=dram["y_rows"],
                                        in_offset=bass.IndirectOffsetOnAxis(ap=row_i[k][:, t:t + 1], axis=0))\
                    .then_inc(y_in[t % (Y_BUFS // 2)], 16)

        @block.tensor
        def _(pe):
            def three(out_ap, count, lhs, rhs):
                n = 0
                for c in range(count):
                    for a, b in ((0, 0), (0, 1), (1, 0)):
                        mm = pe.matmul(out_ap, lhs(a, c), rhs(b, c), start=(n == 0), stop=(n == 3 * count - 1))
                        n += 1
                return mm

            def step(i, kind, f):
                u = i * FC + f
                q = f % 2
                if kind == "G":
                    if isinstance(i, int) and i == 0:
                        pe.wait_ge(w_low_ready, f + 1)
                    wait_from(pe, act_ready, u + (1 - back(f)))
                    for part in range(2):
                        mm = three(p_gu[q][:, part * BLK:(part + 1) * BLK], KC,
                                   lambda a, c: w_sh[a][:, f, part, c * P:(c + 1) * P],
                                   lambda b, c: x_parts[:, b, c, bass.ds(i * BLK, BLK)])
                    mm.then_inc(gated, 1)
                else:
                    pe.wait_ge(a_low_ready, u + 1)
                    if f == 0:
                        wait_from(pe, added, i * TB)
                    for m in range(TB):
                        for n, (a, b) in enumerate(((0, 0), (0, 1), (1, 0))):
                            mm = pe.matmul(p_dn[m][:], a_parts[q][:, a, m * P:(m + 1) * P], w_sh[b][:, f, 2, :],
                                           start=(f == 0 and n == 0), stop=(f == FC - 1 and n == 2))
                    mm.then_inc(downed, 1)

            def turn(s, pair, q):
                pe.wait_ge(gathered[q], pair * 16 + 16)
                wait_from(pe, xg_t_ready, s)
                for r in range(2):
                    for c in range(KC):
                        tr = pe.transpose(p_xt[:, (r * KC + c) * P:(r * KC + c + 1) * P],
                                          xg[q][:, r, c * P:(c + 1) * P], ident16[:])
                tr.then_inc(e_turned, 1)

            def gate_up(s):
                pe.wait_ge(xg_t_ready, s + 1)
                pe.wait_ge(gu_low, s * 2 + 2)
                wait_from(pe, e_act_ready, s)
                three(p_egu[:], KC, lambda a, c: xg_t[:, a, c, :], lambda b, c: gu16[:, b, c, :])\
                    .then_inc(e_gated, 1)

            def turn_act(s, q):
                pe.wait_ge(e_low_ready, s + 1)
                wait_from(pe, e_act_t_ready, s)
                n = FE // P
                for r in range(2):
                    for c in range(n):
                        tr = pe.transpose(p_at[:, (r * n + c) * P:(r * n + c + 1) * P],
                                          e_parts[q][:, r, c * P:(c + 1) * P], ident16[:])
                tr.then_inc(e_act_turned, 1)

            def expert_down(s):
                pe.wait_ge(e_act_t_ready, s + 1)
                pe.wait_ge(dn_low, s + 1)
                wait_from(pe, y_ready, s)
                three(p_y[:], FE // P, lambda a, c: e_parts_t[:, a, c, :], lambda b, c: dn16[:, b, c, :])\
                    .then_inc(e_downed, 1)

            def ranks():
                pe.wait_ge(consts_ready, 7)
                pe.wait_ge(both_ready, 1)
                pe.matmul(rank, before[:], both, start=True, stop=False)
                for d in range(2, T):
                    pe.matmul(rank[:, d:T, :], ones[:], both[:, 0:T - d, :], start=False, stop=False,
                              skip_group_check=True)
                pe.matmul(rank, ones[:], both_led[:, 0:T, :], start=False, stop=True).then_inc(ranked, 1)
                for t in range(T):
                    mm = pe.matmul(total, ones[:], both[:, t, :], start=(t == 0), stop=(t == T - 1))
                mm.then_inc(ranked, 1)

            def use_marks(f):
                batch = f - MARK_FROM
                pe.wait_ge(marked, 2 * (batch + 1))
                for n in range(MARKS):
                    mm = pe.matmul(token_table, at_row[batch % 2][:, n % 2, n // 2, :],
                                   at_slot[batch % 2][:, n % 2, n // 2, :],
                                   start=(batch == 0 and n == 0), stop=(f == MARK_TO - 1 and n == MARKS - 1))
                mm.then_inc(mark_used, 1)

            def body(i, used=SLOTS):
                for k, r, now in places(i):
                    s, pair = slot(i, k)
                    if r == 0 and real(s, used):
                        gate_up(s)
                    if r == 1 and real(s - 1, used):
                        turn_act(s - 1, (k + 1) % 2)
                    if r == 1 and real(s, used) and real(s + 1, used):
                        turn(s + 1, slot(i, k + 1)[1], (k + 1) % 2)
                    if r == 2 and real(s - 1, used):
                        expert_down(s - 1)
                    if now:
                        step(i, *now)
                        if isinstance(i, int) and i == 0 and now[0] == "D":
                            if now[1] == 0:
                                ranks()
                            if MARK_FROM <= now[1] < MARK_TO:
                                use_marks(now[1])
                if isinstance(i, int) and i == 0:
                    turn(0, 0, 0)
            all_blocks(pe, body)

        @block.scalar
        def _(act):
            def split_shared(f):
                act.wait_ge(w_in[f % 4], 16 * (f // 4 + 1))
                act.activation(flat(w_sh[0][:, f, :, :]), s_raw[f % 4], ACT.Copy, scale=WS).then_inc(w_high_ready, 1)

            def split_gu(s, pair, q, h):
                act.wait_ge(gu_in[q], pair * 16 + 16)
                wait_from(act, e_gated, s)
                cs = slice(h * 2, h * 2 + 2)
                act.activation(gu16[:, 0, cs, :], gu_raw[q][:, cs, :], ACT.Copy, scale=WS).then_inc(gu_high, 1)

            def copy_rows(s):
                act.wait_ge(e_turned, s + 1)
                wait_from(act, e_gated, s)
                act.activation(xg_t[:].rearrange("p r c m -> p (r c m)"), p_xt[:], ACT.Copy).then_inc(xg_t_ready, 1)

            def body(i, used=SLOTS):
                zero = isinstance(i, int) and i == 0
                for k, r, now in places(i):
                    s, pair = slot(i, k)
                    if r == 0 and real(s, used):
                        act.wait_ge(e_gated, s + 1)
                        wait_from(act, e_act_ready, s)
                        act.activation(e_silu[:], p_egu[:, 0:FE], ACT.Silu, scale=1.0 / WS).then_inc(e_silu_ready, 1)
                    if r < 2 and real(s, used) and real(s + 1, used):
                        split_gu(s + 1, slot(i, k + 1)[1], (k + 1) % 2, r)
                    if r == 1 and real(s - 1, used):
                        act.wait_ge(e_act_turned, s)
                        wait_from(act, e_downed, s - 1)
                        act.activation(e_parts_t[:].rearrange("p r c m -> p (r c m)"), p_at[:, 0:2 * FE],
                                       ACT.Copy).then_inc(e_act_t_ready, 1)
                    if r == 1 and real(s, used) and real(s + 1, used):
                        copy_rows(s + 1)
                    if r == 2 and real(s - 1, used):
                        act.wait_ge(e_downed, s)
                        wait_from(act, y_saved[(k + 1) % 2], slot(i, k - 1)[1] * 16)
                        act.activation(y_out[(k + 1) % 2][:], p_y[:], ACT.Copy, scale=1.0 / (WS * WS))\
                           .then_inc(y_ready, 1)
                    if r == 2 and real(s, used):
                        act.wait_ge(dn_in[k % 2], pair * 16 + 16)
                        wait_from(act, e_downed, s)
                        act.activation(dn16[:, 0, :, :], dn_raw[k % 2], ACT.Copy, scale=WS).then_inc(dn_high, 1)
                    if now and now[0] == "G":
                        f = now[1]
                        act.wait_ge(gated, i * FC + (f + 1))
                        act.activation(silu[f % 2][:], p_gu[f % 2][:, 0:BLK], ACT.Silu, scale=1.0 / WS)\
                           .then_inc(silu_ready, 1)
                        if zero and f + 2 < FC:
                            split_shared(f + 2)
                        if zero and f == 1:
                            act.wait_ge(exps_in, 1)
                            act.activation(ratio[:], ratio[:], ACT.Exp).then_inc(exps_out, 1)
                            act.activation(sgate[:], logits[:, :, E], ACT.Exp, scale=-1.0).then_inc(exps_out, 1)
                if zero:
                    for h in range(2):
                        split_gu(0, 0, 0, h)
                    copy_rows(0)
            all_blocks(act, body)

        @block.vector
        def _(dve):
            def settle(ins):
                dve_step.settle(dve, ins)

            def wide(a, shape, axis):
                return a.unsqueeze(axis).broadcast_to(shape)

            grid = [P, T, E]

            def choose():
                dve.wait_ge(consts_ready, 1)
                e_row = wide(count_e[:, 0:E], grid, 1)
                settle(dve.tensor_copy(raw[:], logits[:, :, 0:E]))
                for k in range(2):
                    settle(dve.tensor_reduce(top[k][:], raw[:], AX.X, ALU.max))
                    settle(dve.tensor_tensor(key[:], raw[:], wide(top[k][:], grid, 2), ALU.is_equal))
                    settle(dve.scalar_tensor_tensor(hit[k][:], e_row, -float(P), key[:], ALU.add, ALU.mult))
                    settle(dve.tensor_reduce(low_key[:], hit[k][:], AX.X, ALU.min))
                    settle(dve.tensor_tensor(hit[k][:], hit[k][:], wide(low_key[:], grid, 2), ALU.is_equal))
                    if k == 0:
                        settle(dve.scalar_tensor_tensor(raw[:], hit[0][:], -1.0e30, raw[:], ALU.mult, ALU.add))
                dve.tensor_tensor(both, hit[0][:], hit[1][:], ALU.add).then_inc(both_ready, 1)
                dve.tensor_tensor(ratio[:], top[1][:], top[0][:], ALU.subtract).then_inc(exps_in, 1)

            def shares():
                dve.wait_ge(exps_out, 2)
                settle(dve.tensor_scalar(share[1][:], ratio[:], 1.0, None, ALU.add))
                settle(dve.reciprocal(share[0][:], share[1][:]))
                settle(dve.tensor_tensor(share[1][:], ratio[:], share[0][:], ALU.mult))
                settle(dve.tensor_scalar(sgate[:], sgate[:], 1.0, None, ALU.add))
                settle(dve.reciprocal(sgate[:], sgate[:]))
                settle(dve.tensor_scalar(sgate[:], sgate[:], 1.0 / (WS * WS), None, ALU.mult))

            def count_tiles():
                dve.wait_ge(consts_ready, 7)
                dve.wait_ge(ranked, 2)
                settle(dve.tensor_copy(held[:], total))
                square = [P, E, E]
                settle(dve.tensor_scalar(base[:], count_e[:, 0:E], float(P), None, ALU.mult))
                settle(dve.tensor_tensor(cube[:], wide(held[:], square, 2), wide(base[:], square, 1), ALU.is_gt))
                settle(dve.tensor_reduce(tiles[:], cube[:], AX.X, ALU.add))
                settle(dve.tensor_tensor(cube[:], upto[:], wide(tiles[:], square, 1), ALU.mult))
                settle(dve.tensor_reduce(ends[:], cube[:], AX.X, ALU.add))

            def lay_out_slots():
                settle(dve.tensor_tensor(base[:], ends[:], tiles[:], ALU.subtract))
                settle(dve.tensor_scalar(base[:], base[:], float(P), None, ALU.mult))
                settle(dve.tensor_tensor(place[:], rank, wide(base[:], grid, 1), ALU.add))
                slot_grid = [P, SLOTS, E]
                settle(dve.tensor_tensor(past[:], wide(count_e[:, 0:SLOTS], slot_grid, 2),
                                         wide(ends[:], slot_grid, 1), ALU.is_ge))
                settle(dve.tensor_reduce(owner_f[:], past[:], AX.X, ALU.add))
                dve.tensor_scalar(owner[:], owner_f[:], float(E - 1), None, ALU.min).then_inc(owner_ready, 1)
                dve.tensor_scalar(many[:], ends[:, E - 1:E], float(FEW), None, ALU.is_gt).then_inc(slots_counted, 1)

            def rows(k):
                settle(dve.tensor_tensor(hit[k][:], hit[k][:], place[:], ALU.mult))
                settle(dve.tensor_reduce(row_f[k][:], hit[k][:], AX.X, ALU.add))
                settle(dve.tensor_copy(row_i[k][:], row_f[k][:]))
                settle(dve.tensor_scalar(in_tile[k][:], row_i[k][:], P - 1, None, ALU.bitwise_and))
                dve.tensor_copy(in_tile16[k][:], in_tile[k][:])
                settle(dve.tensor_copy(in_tile_f[k][:], in_tile[k][:]))
                settle(dve.tensor_tensor(slot_f[k][:], row_f[k][:], in_tile_f[k][:], ALU.subtract))
                settle(dve.tensor_scalar(slot16[k][:], slot_f[k][:], 1.0 / P, None, ALU.mult))

            def mark(f):
                batch = f - MARK_FROM
                tiles_now = slice(batch * MARKS // 2, (batch + 1) * MARKS // 2)
                wait_from(dve, mark_used, batch - 1)
                for k in range(2):
                    row, slot_mark = at_row[batch % 2][:, k], at_slot[batch % 2][:, k]
                    row_grid, slot_grid = [P, MARKS // 2, P], [P, MARKS // 2, SLOTS]
                    dve.tensor_tensor(row, wide(count16[:], row_grid, 1), wide(in_tile16[k][:, tiles_now], row_grid, 2),
                                      ALU.is_equal)
                    settle(dve.tensor_tensor(slot_mark, wide(count16[:, 0:SLOTS], slot_grid, 1),
                                             wide(slot16[k][:, tiles_now], slot_grid, 2), ALU.is_equal))
                    dve.tensor_tensor(slot_mark, slot_mark, wide(node16[:, tiles_now], slot_grid, 2),
                                      ALU.mult).then_inc(marked, 1)

            def split_shared(f):
                dve.wait_ge(w_high_ready, f + 1)
                dve.scalar_tensor_tensor(flat(w_sh[1][:, f, :, :]), s_raw[f % 4], WS, flat(w_sh[0][:, f, :, :]),
                                         ALU.mult, ALU.subtract).then_inc(w_low_ready, 1)

            def split_gu(s, q, h):
                dve.wait_ge(gu_high, s * 2 + (h + 1))
                cs = slice(h * 2, h * 2 + 2)
                dve.scalar_tensor_tensor(flat(gu16[:, 1, cs, :]), flat(gu_raw[q][:, cs, :]), WS,
                                         flat(gu16[:, 0, cs, :]), ALU.mult, ALU.subtract).then_inc(gu_low, 1)

            def add_results(t):
                dve.wait_ge(y_in[t % (Y_BUFS // 2)], 32 * (2 * t // Y_BUFS + 1))
                for k in range(2):
                    n = 2 * t + k
                    if k == 0:
                        dve.wait_ge(added, (t // TB + 1) * TB)
                    else:
                        dve.wait_ge(y_added, n)
                    dve.scalar_tensor_tensor(x1[:, t, :], y_buf[n % Y_BUFS], share[k][:, t:t + 1], x1[:, t, :],
                                             ALU.mult, ALU.add).then_inc(y_added, 1)

            def hidden_layer(i, f):
                u = i * FC + f
                q = f % 2
                up = p_gu[q][:, BLK:2 * BLK]
                dve.wait_ge(silu_ready, u + 1)
                wait_from(dve, a_low_ready, u)
                wait_from(dve, downed, u + (1 - back(f)))
                dve.tensor_tensor(a_parts[q][:, 0, :], silu[q][:], up, ALU.mult).then_inc(a_high_ready, 1)
                dve.tensor_tensor(act32[:], silu[q][:], up, ALU.mult).then_inc(act_ready, 1)
                dve.wait_ge(a_high_ready, u + 1)
                dve.wait_ge(act_ready, u + 1)
                dve.tensor_tensor(a_parts[q][:, 1, :], act32[:], a_parts[q][:, 0, :], ALU.subtract)\
                   .then_inc(a_low_ready, 1)

            def expert_hidden(s, q):
                up = p_egu[:, FE:2 * FE]
                dve.wait_ge(e_silu_ready, s + 1)
                wait_from(dve, e_low_ready, s)
                wait_from(dve, e_act_turned, s - 1)
                dve.tensor_tensor(e_parts[q][:, 0, :], e_silu[:], up, ALU.mult).then_inc(e_high_ready, 1)
                dve.tensor_tensor(e_act[:], e_silu[:], up, ALU.mult).then_inc(e_act_ready, 1)
                dve.wait_ge(e_high_ready, s + 1)
                dve.wait_ge(e_act_ready, s + 1)
                dve.tensor_tensor(e_parts[q][:, 1, :], e_act[:], e_parts[q][:, 0, :], ALU.subtract)\
                   .then_inc(e_low_ready, 1)

            def body(i, used=SLOTS):
                zero = isinstance(i, int) and i == 0
                final = isinstance(i, int) and i == BLOCKS - 1
                if zero:
                    choose()
                for k, r, now in places(i):
                    s, pair = slot(i, k)
                    if r == 0 and real(s, used):
                        expert_hidden(s, k % 2)
                    if r < 2 and real(s, used) and real(s + 1, used):
                        split_gu(s + 1, (k + 1) % 2, r)
                    if r == 2 and real(s, used):
                        dve.wait_ge(dn_high, s + 1)
                        dve.scalar_tensor_tensor(flat(dn16[:, 1, :, :]), flat(dn_raw[k % 2]), WS,
                                                 flat(dn16[:, 0, :, :]), ALU.mult, ALU.subtract).then_inc(dn_low, 1)
                    if now and now[0] == "G":
                        f = now[1]
                        hidden_layer(i, f)
                        if zero and f + 2 < FC:
                            split_shared(f + 2)
                        if zero and f == 2:
                            count_tiles()
                        if zero and f == SHARES_AT:
                            shares()
                        if zero and f == 3:
                            lay_out_slots()
                        if zero and f in (4, 5):
                            rows(f - 4)
                        if zero and MARK_FROM <= f < MARK_TO:
                            mark(f)
                        if zero and f == MARK_TO:
                            dve.wait_ge(mark_used, MARK_TO - MARK_FROM)
                            dve.tensor_copy(tokens[:], token_table).then_inc(tokens_ready, 1)
                        for t in SUM_TILES[used].get((i, f), ()) if isinstance(i, int) else ():
                            add_results(t)
                if zero:
                    for h in range(2):
                        split_gu(0, 0, h)
                dve.wait_ge(downed, i * FC + FC)
                for m in range(TB):
                    dve.scalar_tensor_tensor(row_of(i * TB + m), p_dn[m][:], sgate[:, bass.ds(i * TB + m, 1)],
                                             row_of(i * TB + m), ALU.mult, ALU.add).then_inc(added, 1)
                if final:
                    for t in range(1 + max(t for now in SUM_TILES[used].values() for t in now), T):
                        add_results(t)
            all_blocks(dve, body)


def program(nc, io, out):
    dram = {
        "a_rows": nc.dram_tensor("a_rows", [H, N], F32, kind="Internal").ap(),
        "xn_rows": nc.dram_tensor("xn_rows", [N, 2 * D], F16, kind="Internal").ap(),
        "y_rows": nc.dram_tensor("y_rows", [SLOTS * P, D], F32, kind="Internal").ap(),
    }
    with ExitStack() as ctx:
        sb, ps, sem = make_tools(nc, ctx)
        ident = sb("ident", [P, P], F32)
        ident16 = sb("ident16", [P, P], F16)
        with ExitStack() as upper:
            usb, _, _ = make_tools(nc, upper)
            keep = {"ident16": ident16, "hidden": usb("hidden", [P, T, H * (DH + 1)], F32)}
            with ExitStack() as inner:
                isb, _, _ = make_tools(nc, inner)
                keep["mask"] = isb("mask", [P, T, N], F16)
                keep["seq"] = isb("seq", [P, T * D], F32)
                for n in ("e_pos", "e_neg", "f_pos", "f_neg", "neg_b", "step_b"):
                    keep[n] = isb(n, [P, H * T], F32)
                keep["a_row"] = [isb(f"a_row{q}", [P, N], F32) for q in range(2)]
                keep["rows_in"] = [sem(f"rows_in{q}") for q in range(2)]
                attention_operands(nc, io, dram, keep, ident)
                attention_heads(nc, io, dram, keep)
            keep["x1"] = keep["hidden"][:].rearrange("p t c -> p (t c)")[:, 0:T * D].rearrange("p (t d) -> p t d", t=T)
            keep["x_parts"] = usb("x_parts", [P, 2, KC, N], F16)
            keep["logits"] = usb("logits", [P, T, E + 1], F32)
            w_raw = [usb(f"w_raw{q}", [P, 6 * D], F32) for q in range(2)]
            keep["w_raw"] = w_raw
            keep["s_raw"] = [w_raw[r // 2][:, (r % 2) * 3 * D:(r % 2 + 1) * 3 * D] for r in range(4)]
            keep["w_in"] = [sem(f"w_shared_in{r}") for r in range(4)]
            keep["w_sh"] = [usb(f"w_shared_part{r}", [P, FC, 3, D], F16) for r in range(2)]
            keep["w_high_ready"], keep["w_low_ready"] = sem("w_high_ready"), sem("w_low_ready")
            output_projection(nc, io, dram, keep, ident)
            feed_forward(nc, io, dram, keep, ident, out)


def kernel(**inputs):
    import numpy as np
    import concourse.bacc as bacc
    from concourse import mybir as mb
    from concourse.bass_utils import run_bass_kernel_spmd

    def plain(name):
        return np.asarray(inputs[name])

    a1, a2 = plain("L0_gnn_a1"), plain("L0_gnn_a2")
    sides = [plain(f"L0_ffn_shared_w_{n}").reshape(FC, P, KC, P).transpose(0, 3, 2, 1).reshape(FC, P, D)
             for n in ("gate", "up")]
    w_shared = np.stack(sides + [plain("L0_ffn_shared_w_down").T.reshape(FC, P, D)], axis=2)
    laid_out = {
        "x": plain("x"),
        "adj_t": plain("adj").T,
        "w_seq": plain("L0_gnn_W_seq"),
        "w_seq_t": plain("L0_gnn_W_seq").T,
        "w_out": plain("L0_gnn_W_out"),
        "b_out": plain("L0_gnn_b_out")[None, :],
        "w_route": np.concatenate([plain("L0_ffn_gate_w"), plain("L0_ffn_shared_gate_w")], axis=0).T,
        "w_shared": w_shared,
        "w_gate_up": plain("L0_ffn_w_gate_up"),
        "w_down": plain("L0_ffn_w_down"),
        "a_rep": np.stack([np.tile(a1, P // DH), np.tile(a2, P // DH)], axis=1),
    }
    nc = bacc.Bacc("TRN2", target_bir_lowering=False, num_devices=1)
    arrays, io = {}, {}
    for name, a in laid_out.items():
        a = np.ascontiguousarray(a)
        arrays[f"in_{name}"] = a
        io[name] = nc.dram_tensor(f"in_{name}", a.shape, mb.dt.from_np(a.dtype), kind="ExternalInput").ap()
    out = nc.dram_tensor("out_0", (N, D), mb.dt.float32, kind="ExternalOutput").ap()
    program(nc, io, out)
    r = run_bass_kernel_spmd(nc, [arrays], core_ids=[0])
    return r.results[0]["out_0"]
```
